# Optimizing a Trainium2 kernel written in Bass

```python
import numpy as np
import jax
import jax.numpy as jnp

def _softmax(x, axis=-1):
    return jax.nn.softmax(x, axis=axis)

def _gelu(x):
    return jax.nn.gelu(x, approximate=True)

def _silu(x):
    return jax.nn.silu(x)

def _sigmoid(x):
    return jax.nn.sigmoid(x)

def _layernorm(x, axis=-1, eps=1e-05):
    m = jnp.mean(x, axis=axis, keepdims=True)
    v = jnp.var(x, axis=axis, keepdims=True)
    return (x - m) / jnp.sqrt(v + eps)

def _scatter_add(tgt, idx, src, axis=0):
    return tgt.at[idx].add(src)

def _segment_sum(src, seg, n):
    return jax.ops.segment_sum(src, seg, n)
kernel_name = 'mk_gnn_resnorm_d4_gnn_r64_38391f'

def setup_inputs(seed: int=0):
    np.random.seed(seed)
    _w = jnp.asarray

    def _rec_inputs():
        import jax
        import jax.numpy as jnp
        _gk = jax.random.key(seed)
        x = -0.000202 + 1 * jax.random.normal(jax.random.fold_in(_gk, 1), (50000, 128), jnp.float32)
        src = jax.random.randint(jax.random.fold_in(_gk, 2), (12500,), 0, 50000, jnp.int32)
        dst = jnp.minimum((50000 * jax.random.uniform(jax.random.fold_in(_gk, 3), (12500,)) ** 2.0).astype(jnp.int32), 49999)
        _o = jnp.argsort(dst, stable=True)
        src = src[_o]
        dst = dst[_o]
        edge_attr_42 = 0.000171677 + 1.0001 * jax.random.normal(jax.random.fold_in(_gk, 12), (12500, 42), jnp.float32)
        edge_weight = jax.random.uniform(jax.random.fold_in(_gk, 14), (12500,), jnp.float32, 0.0, 0.999998)
        node_vec = jax.random.uniform(jax.random.fold_in(_gk, 15), (50000,), jnp.float32, 0.0, 0.999994)
        return (x, src, dst, edge_attr_42, edge_weight, node_vec)
    x, src, dst, edge_attr_42, edge_weight, node_vec = _rec_inputs()

    def _L0_gnn_setup():
        import jax, jax.numpy as jnp
        import numpy as np
        N = 50000
        E = 12500
        IN = 128
        OUT = 128
        H = 8
        D = OUT // H

        def _xavier(key, shape, fan_in, fan_out):
            bound = np.sqrt(6.0 / (fan_in + fan_out)).astype(np.float32)
            return jax.random.uniform(key, shape, jnp.float32, -bound, bound)
        key = jax.random.key(seed)
        ks = jax.random.split(key, 12)
        feat = jax.random.normal(ks[0], (N, IN), jnp.float32)
        src = jax.random.randint(ks[1], (E,), 0, N, jnp.int32)
        dst = jax.random.randint(ks[2], (E,), 0, N, jnp.int32)
        Wq = _xavier(ks[3], (H, IN, D), IN, D)
        Wk = _xavier(ks[4], (H, IN, D), IN, D)
        Wv = _xavier(ks[5], (H, IN, D), IN, D)
        b = 1.0 / np.sqrt(IN).astype(np.float32)
        bq = jax.random.uniform(ks[6], (H, D), jnp.float32, -b, b)
        bk = jax.random.uniform(ks[7], (H, D), jnp.float32, -b, b)
        bv = jax.random.uniform(ks[8], (H, D), jnp.float32, -b, b)
        Ws = _xavier(ks[9], (IN, OUT), IN, OUT)
        bs = jax.random.uniform(ks[10], (OUT,), jnp.float32, -b, b)
        return {'feat': feat, 'src': src, 'dst': dst, 'Wq': Wq, 'bq': bq, 'Wk': Wk, 'bk': bk, 'Wv': Wv, 'bv': bv, 'Ws': Ws, 'bs': bs}
    _L0_gnn_all = _L0_gnn_setup()
    _L0_gnn_in = {k: v for k, v in _L0_gnn_all.items() if k in ('Wq', 'bq', 'Wk', 'bk', 'Wv', 'bv', 'Ws', 'bs')}
    del _L0_gnn_all

    def _L1_gnn_setup():
        import jax, jax.numpy as jnp
        import numpy as np

        def _gcn_layer(x, W, b, src, dst, norm, n_nodes):
            h = x @ W
            msgs = h[src] * norm[:, None]
            agg = jax.ops.segment_sum(msgs, dst, num_segments=n_nodes)
            return agg + b
        key = jax.random.key(seed)
        k1, k2, k3, k4 = jax.random.split(key, 4)
        N, E, F_IN, HID, OUT = (50000, 12500, 128, 256, 128)
        x = jax.random.normal(k1, (N, F_IN), dtype=jnp.float32)
        edge_index = jax.random.randint(k2, (2, E), 0, N, dtype=jnp.int64)
        W1 = jax.random.normal(k3, (F_IN, HID), dtype=jnp.float32) / np.sqrt(F_IN)
        b1 = jnp.zeros((HID,), dtype=jnp.float32)
        W2 = jax.random.normal(k4, (HID, OUT), dtype=jnp.float32) / np.sqrt(HID)
        b2 = jnp.zeros((OUT,), dtype=jnp.float32)
        return {'x': x, 'edge_index': edge_index, 'W1': W1, 'b1': b1, 'W2': W2, 'b2': b2}
    _L1_gnn_all = _L1_gnn_setup()
    _L1_gnn_in = {k: v for k, v in _L1_gnn_all.items() if k in ('W1', 'b1', 'W2', 'b2')}
    del _L1_gnn_all

    def _L2_gnn_setup():
        import jax, jax.numpy as jnp
        import numpy as np
        N = 50000
        E = 25000
        IN_F = 128
        OUT_F = 32
        H = 4
        ALPHA = 0.2

        def _gat_head(x, src, dst, Wh, asrc, adst):
            h = x @ Wh
            s_src = h @ asrc
            s_dst = h @ adst
            e = jax.nn.leaky_relu(s_src[src] + s_dst[dst], negative_slope=ALPHA)
            m = jax.ops.segment_max(e, dst, num_segments=N)
            ex = jnp.exp(e - m[dst])
            denom = jax.ops.segment_sum(ex, dst, num_segments=N)
            attn = ex / denom[dst]
            out = jax.ops.segment_sum(attn[:, None] * h[src], dst, num_segments=N)
            return jax.nn.elu(out)
        key = jax.random.key(seed)
        ks = jax.random.split(key, 5)
        x = jax.random.normal(ks[0], (N, IN_F), dtype=jnp.float32)
        edge_index = jax.random.randint(ks[1], (2, E), 0, N, dtype=jnp.int64)
        W = jax.random.normal(ks[2], (H, IN_F, OUT_F), dtype=jnp.float32) * 0.05
        a_src = jax.random.normal(ks[3], (H, OUT_F), dtype=jnp.float32) * 0.05
        a_dst = jax.random.normal(ks[4], (H, OUT_F), dtype=jnp.float32) * 0.05
        return {'x': x, 'edge_index': edge_index, 'W': W, 'a_src': a_src, 'a_dst': a_dst}
    _L2_gnn_all = _L2_gnn_setup()
    _L2_gnn_in = {k: v for k, v in _L2_gnn_all.items() if k in ('W', 'a_src', 'a_dst')}
    del _L2_gnn_all

    def _L3_gnn_setup():
        import jax, jax.numpy as jnp
        import numpy as np
        NODE_EMB_DIM = 16
        NUM_REL = 10

        def _rgcn_layer(x, src, dst, edge_type, w_rel, root, bias):
            N = x.shape[0]
            seg = dst * NUM_REL + edge_type
            xs = x[src]
            sums = jax.ops.segment_sum(xs, seg, num_segments=N * NUM_REL)
            cnt = jax.ops.segment_sum(jnp.ones(seg.shape, x.dtype), seg, num_segments=N * NUM_REL)
            mean = (sums / jnp.maximum(cnt, 1.0)[:, None]).reshape(N, NUM_REL, -1)
            return jnp.einsum('nrd,rdo->no', mean, w_rel) + x @ root + bias
        key = jax.random.key(seed)
        ks = jax.random.split(key, 10)
        N, E, C = (50000, 12500, 128)
        s = 1.0 / np.sqrt(C).astype(np.float32)
        x = jax.random.normal(ks[0], (N, C), jnp.float32)
        last_update = jax.random.uniform(ks[1], (N,), jnp.float32)
        t = jax.random.uniform(ks[2], (E,), jnp.float32)
        msg = jax.random.normal(ks[3], (E, 2 * NODE_EMB_DIM + NUM_REL), jnp.float32)
        w_rel1 = jax.random.normal(ks[4], (NUM_REL, C, C), jnp.float32) * s
        root1 = jax.random.normal(ks[5], (C, C), jnp.float32) * s
        b1 = jnp.zeros((C,), jnp.float32)
        w_rel2 = jax.random.normal(ks[6], (NUM_REL, C, C), jnp.float32) * s
        root2 = jax.random.normal(ks[7], (C, C), jnp.float32) * s
        b2 = jnp.zeros((C,), jnp.float32)
        edge_index = jax.random.randint(ks[8], (2, E), 0, N, dtype=jnp.int32)
        return dict(x=x, last_update=last_update, t=t, msg=msg, w_rel1=w_rel1, root1=root1, b1=b1, w_rel2=w_rel2, root2=root2, b2=b2, edge_index=edge_index)
    _L3_gnn_all = _L3_gnn_setup()
    _L3_gnn_in = {k: v for k, v in _L3_gnn_all.items() if k in ('w_rel1', 'root1', 'b1', 'w_rel2', 'root2', 'b2')}
    del _L3_gnn_all
    return {'x': x, 'src': src, 'dst': dst, 'edge_attr_42': edge_attr_42, 'edge_weight': edge_weight, 'node_vec': node_vec, 'L0_gnn_Wq': _L0_gnn_in['Wq'], 'L0_gnn_bq': _L0_gnn_in['bq'], 'L0_gnn_Wk': _L0_gnn_in['Wk'], 'L0_gnn_bk': _L0_gnn_in['bk'], 'L0_gnn_Wv': _L0_gnn_in['Wv'], 'L0_gnn_bv': _L0_gnn_in['bv'], 'L0_gnn_Ws': _L0_gnn_in['Ws'], 'L0_gnn_bs': _L0_gnn_in['bs'], 'L1_gnn_W1': _L1_gnn_in['W1'], 'L1_gnn_b1': _L1_gnn_in['b1'], 'L1_gnn_W2': _L1_gnn_in['W2'], 'L1_gnn_b2': _L1_gnn_in['b2'], 'L2_gnn_W': _L2_gnn_in['W'], 'L2_gnn_a_src': _L2_gnn_in['a_src'], 'L2_gnn_a_dst': _L2_gnn_in['a_dst'], 'L3_gnn_w_rel1': _L3_gnn_in['w_rel1'], 'L3_gnn_root1': _L3_gnn_in['root1'], 'L3_gnn_b1': _L3_gnn_in['b1'], 'L3_gnn_w_rel2': _L3_gnn_in['w_rel2'], 'L3_gnn_root2': _L3_gnn_in['root2'], 'L3_gnn_b2': _L3_gnn_in['b2']}

def reference(x, src, dst, edge_attr_42, edge_weight, node_vec, L0_gnn_Wq, L0_gnn_bq, L0_gnn_Wk, L0_gnn_bk, L0_gnn_Wv, L0_gnn_bv, L0_gnn_Ws, L0_gnn_bs, L1_gnn_W1, L1_gnn_b1, L1_gnn_W2, L1_gnn_b2, L2_gnn_W, L2_gnn_a_src, L2_gnn_a_dst, L3_gnn_w_rel1, L3_gnn_root1, L3_gnn_b1, L3_gnn_w_rel2, L3_gnn_root2, L3_gnn_b2):
    import jax
    import jax.numpy as jnp

    def _L0_gnn_ref(feat, src, dst, Wq, bq, Wk, bk, Wv, bv, Ws, bs):
        import jax, jax.numpy as jnp
        import numpy as np
        N = 50000
        E = 12500
        IN = 128
        OUT = 128
        H = 8
        D = OUT // H

        def _xavier(key, shape, fan_in, fan_out):
            bound = np.sqrt(6.0 / (fan_in + fan_out)).astype(np.float32)
            return jax.random.uniform(key, shape, jnp.float32, -bound, bound)
        q = jnp.einsum('ni,hid->nhd', feat, Wq) + bq
        k = jnp.einsum('ni,hid->nhd', feat, Wk) + bk
        v = jnp.einsum('ni,hid->nhd', feat, Wv) + bv
        scores = jnp.einsum('ehd,ehd->eh', k[src], q[dst]) / np.sqrt(D).astype(np.float32)
        m = jax.ops.segment_max(scores, dst, num_segments=N)
        m = jax.lax.stop_gradient(jnp.where(jnp.isfinite(m), m, 0.0))
        ex = jnp.exp(scores - m[dst])
        den = jax.ops.segment_sum(ex, dst, num_segments=N)
        attn = ex / den[dst]
        msg = v[src] * attn[:, :, None]
        h = jax.ops.segment_sum(msg, dst, num_segments=N)
        rst = h.reshape(N, H * D)
        rst = rst + feat @ Ws + bs
        return rst

    def _L1_gnn_ref(x, edge_index, W1, b1, W2, b2):
        import jax, jax.numpy as jnp
        import numpy as np

        def _gcn_layer(x, W, b, src, dst, norm, n_nodes):
            h = x @ W
            msgs = h[src] * norm[:, None]
            agg = jax.ops.segment_sum(msgs, dst, num_segments=n_nodes)
            return agg + b
        N = x.shape[0]
        self_loops = jnp.arange(N, dtype=edge_index.dtype)
        src = jnp.concatenate([edge_index[0], self_loops])
        dst = jnp.concatenate([edge_index[1], self_loops])
        deg = jax.ops.segment_sum(jnp.ones_like(dst, dtype=x.dtype), dst, num_segments=N)
        dinv = jnp.where(deg > 0, jax.lax.rsqrt(deg), 0.0)
        norm = dinv[src] * dinv[dst]
        h = _gcn_layer(x, W1, b1, src, dst, norm, N)
        h = jax.nn.relu(h)
        out = _gcn_layer(h, W2, b2, src, dst, norm, N)
        return out

    def _L2_gnn_ref(x, edge_index, W, a_src, a_dst):
        import jax, jax.numpy as jnp
        import numpy as np
        N = 50000
        E = 25000
        IN_F = 128
        OUT_F = 32
        H = 4
        ALPHA = 0.2

        def _gat_head(x, src, dst, Wh, asrc, adst):
            h = x @ Wh
            s_src = h @ asrc
            s_dst = h @ adst
            e = jax.nn.leaky_relu(s_src[src] + s_dst[dst], negative_slope=ALPHA)
            m = jax.ops.segment_max(e, dst, num_segments=N)
            ex = jnp.exp(e - m[dst])
            denom = jax.ops.segment_sum(ex, dst, num_segments=N)
            attn = ex / denom[dst]
            out = jax.ops.segment_sum(attn[:, None] * h[src], dst, num_segments=N)
            return jax.nn.elu(out)
        src, dst = (edge_index[0], edge_index[1])
        heads = jax.vmap(lambda w, asr, ads: _gat_head(x, src, dst, w, asr, ads))(W, a_src, a_dst)
        return jnp.transpose(heads, (1, 0, 2)).reshape(N, H * OUT_F)

    def _L3_gnn_ref(x, last_update, t, msg, w_rel1, root1, b1, w_rel2, root2, b2, edge_index):
        import jax, jax.numpy as jnp
        import numpy as np
        NODE_EMB_DIM = 16
        NUM_REL = 10

        def _rgcn_layer(x, src, dst, edge_type, w_rel, root, bias):
            N = x.shape[0]
            seg = dst * NUM_REL + edge_type
            xs = x[src]
            sums = jax.ops.segment_sum(xs, seg, num_segments=N * NUM_REL)
            cnt = jax.ops.segment_sum(jnp.ones(seg.shape, x.dtype), seg, num_segments=N * NUM_REL)
            mean = (sums / jnp.maximum(cnt, 1.0)[:, None]).reshape(N, NUM_REL, -1)
            return jnp.einsum('nrd,rdo->no', mean, w_rel) + x @ root + bias
        src, dst = (edge_index[0], edge_index[1])
        edge_type = jnp.argmax(msg[:, NODE_EMB_DIM:-NODE_EMB_DIM], axis=1).astype(jnp.int32)
        h = jax.nn.relu(_rgcn_layer(x, src, dst, edge_type, w_rel1, root1, b1))
        return _rgcn_layer(h, src, dst, edge_type, w_rel2, root2, b2)
    edge_index = jnp.stack([src, dst])
    x = _layernorm(x + _L0_gnn_ref(x, src, dst, L0_gnn_Wq, L0_gnn_bq, L0_gnn_Wk, L0_gnn_bk, L0_gnn_Wv, L0_gnn_bv, L0_gnn_Ws, L0_gnn_bs), axis=-1)
    x = _layernorm(x + _L1_gnn_ref(x, edge_index, L1_gnn_W1, L1_gnn_b1, L1_gnn_W2, L1_gnn_b2), axis=-1)
    x = _layernorm(x + _L2_gnn_ref(x, edge_index, L2_gnn_W, L2_gnn_a_src, L2_gnn_a_dst), axis=-1)
    x = _layernorm(x + _L3_gnn_ref(x, node_vec, edge_weight, edge_attr_42, L3_gnn_w_rel1, L3_gnn_root1, L3_gnn_b1, L3_gnn_w_rel2, L3_gnn_root2, L3_gnn_b2, edge_index), axis=-1)
    return x

_drawn_inputs = setup_inputs


def setup_inputs(seed=0):
    import zlib

    import numpy as np

    out = dict(_drawn_inputs(seed))
    spreads = {'L1_gnn_b1': (0.0, 0.1),
     'L1_gnn_b2': (0.0, 0.1),
     'L3_gnn_b1': (0.0, 0.1),
     'L3_gnn_b2': (0.0, 0.1)}
    factors = {'L0_gnn_bq': 40.44,
     'L0_gnn_bk': 64.0,
     'L0_gnn_bv': 7.65,
     'L2_gnn_a_src': 25.028,
     'L2_gnn_a_dst': 64.0}
    for name, (base, spread) in spreads.items():
        noise = np.random.default_rng([zlib.crc32(name.encode()), seed]).standard_normal(out[name].shape)
        drawn = base * np.exp(spread * noise) if base else spread * noise
        out[name] = jnp.asarray(drawn.astype(out[name].dtype))
    for name, factor in factors.items():
        out[name] = (out[name] * factor).astype(out[name].dtype)
    return out
```

```python
from contextlib import ExitStack

import numpy as np

import concourse.bass as bass
from concourse import mybir
from concourse.alu_op_type import AluOpType as ALU

fp32 = mybir.dt.float32
i32 = mybir.dt.int32
ACT = mybir.ActivationFunctionType
AX = mybir.AxisListType

N = 50000
E = 12500
F = 128
GROUPS = (N + 511) // 512
LAST_BASE = N - 512
EPS = 1e-5
HEADS = 8
GAT_HEADS = 4
ALPHA = 0.2
RELATIONS = 10
EMB = 16
BLOCKS, BLOCK = 10, 10
T = BLOCKS * BLOCK
SLOTS = T * F
UNROLL = 4
PASSES = T // UNROLL
PAD_KEY = 1 << 16
BEYOND = 1 << 20
FAR = 1e30


class Memory:

    def __init__(self, nc, stack, prefix=""):
        self.nc, self.stack, self.prefix = nc, stack, prefix

    def sb(self, name, shape, dt=fp32):
        return self.stack.enter_context(self.nc.sbuf_tensor(self.prefix + name, shape, dt))

    def pb(self, name, shape, dt=fp32):
        return self.stack.enter_context(self.nc.psum_tensor(self.prefix + name, shape, dt))

    def sem(self, name):
        return self.stack.enter_context(self.nc.semaphore(self.prefix + name))


def clear(nc, sems):
    numbers = sorted(s.num for s in sems)
    with nc.Block() as block:

        @block.gpsimd
        def _(pool):
            at_ = 0
            while at_ < len(numbers):
                end = at_
                while end + 1 < len(numbers) and numbers[end + 1] == numbers[end] + 1:
                    end += 1
                pool.sem_clear(range(numbers[at_], numbers[end] + 1))
                at_ = end + 1


class Phase(Memory):

    opened = 0

    def __init__(self, nc):
        Phase.opened += 1
        super().__init__(nc, ExitStack(), f"phase{Phase.opened}_")
        self.sems = []

    def sem(self, name):
        s = super().sem(name)
        self.sems.append(s)
        return s

    def named(self, names):
        return {n: self.sem(n) for n in names.split()}

    def __enter__(self):
        self.stack.__enter__()
        return self

    def __exit__(self, *e):
        if e[0] is None and self.sems:
            clear(self.nc, self.sems)
        return self.stack.__exit__(*e)


class PoolMoves:

    def __init__(self, mem, name):
        self.sems = [mem.sem(f"{name}{u}") for u in range(UNROLL)]
        self.passes = 0

    def after(self, j):
        return 16 * (self.passes + j) if isinstance(j, int) else (j + self.passes) * 16


def wait(eng, s, count):
    if not isinstance(count, int) or count > 0:
        eng.wait_ge(s, count)


def row_vector(v):
    return v.rearrange("(a n) -> a n", a=1).partition_broadcast(F)


def take_waits(eng, taken):
    eng.sem_inc(taken)


def prepare_weights(nc, mem, m, io, W):
    sb = mem.sb
    for name, shape in (("ident", [F, F]), ("eps", [F, 1]), ("Wsc", [F, F]), ("W1", [F, 2 * F]), ("W2c", [F, 2, F]),
                        ("root1", [F, F]), ("root2c", [F, F]), ("b_W1", [F, 2]), ("b_root1", [F, 1]),
                        ("bsc", [F, F]), ("b2c", [F, F]), ("b4c", [F, F]), ("ones", [1, F]), ("b_root1_row", [1, F]),
                        ("Wq", [F, F]), ("Wkv", [F, 2, F]), ("bqk", [F, 2, F]), ("bv", [F, F]), ("Wgat", [F, GAT_HEADS, F // GAT_HEADS]),
                        ("w_src", [F, GAT_HEADS]), ("w_dst", [F, GAT_HEADS])):
        W[name] = sb(name, shape)
    mean, a_src, a_dst, prod = m.sb("mean", [F, 1]), m.sb("a_src", [F, F]), m.sb("a_dst", [F, F]), m.sb("a_prod", [F, F])
    loaded, ident_done, step_done = m.sem("loaded"), m.sem("ident_done"), m.sem("step_done")
    by_head = lambda w: w.rearrange("h p d -> p h d")
    heads = lambda m: m.rearrange("p (h d) -> p h d", h=HEADS)
    loads = [
        (heads(W["Wq"][:, :]), by_head(io["L0_gnn_Wq"])), (heads(W["Wkv"][:, 0, :]), by_head(io["L0_gnn_Wk"])),
        (heads(W["Wkv"][:, 1, :]), by_head(io["L0_gnn_Wv"])), (W["Wgat"][:, :, :], by_head(io["L2_gnn_W"])),
        (W["bqk"][:, 0, :], row_vector(io["L0_gnn_bq"].rearrange("h d -> (h d)"))),
        (W["bqk"][:, 1, :], row_vector(io["L0_gnn_bk"].rearrange("h d -> (h d)"))),
        (W["bv"][:, :], row_vector(io["L0_gnn_bv"].rearrange("h d -> (h d)"))),
        (a_src[:, :], row_vector(io["L2_gnn_a_src"].rearrange("h d -> (h d)"))),
        (a_dst[:, :], row_vector(io["L2_gnn_a_dst"].rearrange("h d -> (h d)"))),
        (W["b_root1_row"][:, :], io["L3_gnn_b1"].rearrange("(a n) -> a n", a=1)),
        (W["Wsc"][:, :], io["L0_gnn_Ws"]), (W["W1"][:, :], io["L1_gnn_W1"]),
        (W["W2c"][:, :, :], io["L1_gnn_W2"].rearrange("(k p) f -> p k f", k=2)),
        (W["root1"][:, :], io["L3_gnn_root1"]), (W["root2c"][:, :], io["L3_gnn_root2"]),
        (W["b_W1"][:, :], io["L1_gnn_b1"].rearrange("(k p) -> p k", k=2)),
        (W["b_root1"][:, :], io["L3_gnn_b1"].rearrange("(p a) -> p a", a=1)),
        (W["bsc"][:, :], row_vector(io["L0_gnn_bs"])), (W["b2c"][:, :], row_vector(io["L1_gnn_b2"])),
        (W["b4c"][:, :], row_vector(io["L3_gnn_b2"])),
    ]
    with nc.Block() as block:

        @block.sync
        def _(sp):
            for dst, src in loads:
                sp.dma_start(dst, src, allow_slow_non_contiguous=True).then_inc(loaded, 16)

        @block.gpsimd
        def _(pool):
            pool.memset(W["ident"][:, :], 0.0).then_inc(ident_done, 1)
            pool.memset(W["eps"][:, :], EPS)
            pool.memset(W["ones"][:, :], 1.0).then_inc(ident_done, 1)
            pool.wait_ge(ident_done, 2)
            pool.affine_select(out=W["ident"][:, :], in_=W["ident"][:, :], compare_op=ALU.not_equal, fill=1.0,
                               base=0, pattern=[[-1, F]], channel_multiplier=1).then_inc(ident_done, 1)

        @block.vector
        def _(dve):
            done = 0

            def chained(ins):
                nonlocal done
                done += 1
                ins.then_inc(step_done, 1)
                dve.wait_ge(step_done, done)

            dve.wait_ge(loaded, 16 * len(loads))
            dve.wait_ge(ident_done, 3)
            chained(nc.vector.tensor_tensor(W["Wsc"][:, :], W["Wsc"][:, :], W["ident"][:, :], ALU.add))
            for m in (W["Wsc"][:, :], W["W2c"][:, 0, :], W["W2c"][:, 1, :], W["root2c"][:, :],
                      W["bsc"][:, :], W["b2c"][:, :], W["b4c"][:, :]):
                chained(nc.vector.tensor_reduce(mean[:, :], m, AX.X, ALU.add))
                chained(nc.vector.tensor_scalar(mean[:, :], mean[:, :], -1.0 / F, None, ALU.mult))
                chained(nc.vector.tensor_scalar(m, m, mean[:, 0:1], None, ALU.add))
            for a, w in ((a_src, W["w_src"]), (a_dst, W["w_dst"])):
                p = prod[:, :].rearrange("p (h d) -> p h d", h=GAT_HEADS)
                chained(nc.vector.tensor_tensor(p, W["Wgat"][:, :, :], a[:, :].rearrange("p (h d) -> p h d", h=GAT_HEADS), ALU.mult))
                chained(nc.vector.tensor_reduce(w[:, :], p, AX.X, ALU.add))
def dense_phase(nc, mem, io, W):
    sb, pb, sem = mem.sb, mem.pb, mem.sem
    ident, eps = W["ident"], W["eps"]

    two = lambda name: [sb(f"{name}{u}", [F, 4, F], fp32) for u in range(2)]
    one = lambda name: sb(name, [F, 4, F], fp32)
    x, x1, h2, x2, x3, h, o = (two(n) for n in ("x", "x1", "h2", "x2", "x3", "h", "o"))
    xT, y1, x1T, gT0, gT1, x1b, y2, x3T, x3b, hT, y4, sq1, sq2, sq4 = (
        one(n) for n in ("xT", "y1", "x1T", "gT0", "gT1", "x1b", "y2", "x3T", "x3b", "hT", "y4", "sq1", "sq2", "sq4"))
    gT = [gT0, gT1]
    stat = {n: sb(f"stat_{n}", [F, 4], fp32) for n in ("ss1", "sd1", "r1", "ss2", "sd2", "r2", "v2", "w2", "q2", "sd3", "r3", "ss4", "sd4", "r4")}

    P = [pb(f"P{b}", [F, 4, F], fp32) for b in range(8)]
    p_xT, p_y1, p_x1T, p_g0, p_g1, p_h2, p_x3T, p_hT = P
    p_h, p_y4 = p_x3T, p_hT

    names = ("p_xT_full xT_full p_y1_full y1_full sq1_full ss1_full sd1_full r1_full x1_full "
             "p_x1T_full x1T_full p_g0_full p_g1_full g0_full g1_full p_h2_full h2_full x1b_full y2_full sq2_full ss2_full "
             "sd2_full r2_full v2_full w2_full q2_full sd3_full r3_full x2_full x3_full "
             "p_x3T_full x3T_full p_hT_full hT_full p_h_full h_full p_y4_full x3b_full y4_full sq4_full ss4_full sd4_full "
             "r4_full o_full").split()
    S = {n: sem("d_" + n) for n in names}
    x_loaded = [sem(f"d_x_loaded{u}") for u in range(2)]
    stored = {n: [sem(f"d_{n}_stored{u}") for u in range(2)] for n in ("x1", "h2", "x2", "x3", "h", "o")}
    PAIRS = GROUPS // 2

    def has(j):
        return not isinstance(j, int) or 0 <= j < PAIRS

    def rows(table, j, u):
        g = 2 * j + u
        base = LAST_BASE if isinstance(g, int) and g == GROUPS - 1 else g * 512
        return table[bass.ds(base, 512), :].rearrange("(p t) f -> p t f", t=4)

    def run(eng, step):
        for j in range(2):
            for u in range(2):
                step(j, u)
        with eng.Fori(2, PAIRS - 2) as j:
            for u in range(2):
                step(j, u)
        for j in range(PAIRS - 2, PAIRS + 2):
            for u in range(2):
                step(j, u)

    over_tiles = lambda w: w[:, :].unsqueeze(1).to_broadcast([F, 4, F])
    over_rows = lambda r: r[:, :].unsqueeze(2).to_broadcast([F, 4, F])

    with nc.Block() as block:

        @block.sync
        def _(sp):
            for u in range(2):
                sp.dma_start(x[u][:, :, :], rows(io["x"], 0, u)).then_inc(x_loaded[u], 16)

            def store(table, buf, name, ready, j, u):
                sp.wait_ge(S[ready], 2 * j + u + 1)
                if isinstance(j, int) and 2 * j + u == GROUPS - 1:
                    sp.wait_ge(stored[name][1 - u], 16 * (j + 1))
                sp.dma_start(rows(table, j, u), buf[u][:, :, :]).then_inc(stored[name][u], 16)

            def step(j, u):
                if has(j - 2):
                    store(io["H"], h, "h", "h_full", j - 2, u)
                if has(j + 1):
                    wait(sp, S["p_xT_full"], 2 * j + u + 1)
                    sp.dma_start(x[u][:, :, :], rows(io["x"], j + 1, u)).then_inc(x_loaded[u], 16)
                if has(j - 2):
                    store(io["out"], o, "o", "o_full", j - 2, u)
                if has(j):
                    store(io["Z1"], x1, "x1", "x1_full", j, u)
                if has(j - 1):
                    store(io["H2"], h2, "h2", "h2_full", j - 1, u)
                    store(io["X2"], x2, "x2", "x2_full", j - 1, u)
                    store(io["X3"], x3, "x3", "x3_full", j - 1, u)
            run(sp, step)
            for n in stored:
                for u in range(2):
                    sp.wait_ge(stored[n][u], 16 * PAIRS)

        @block.tensor
        def _(pe):
            def transposes(out, src, done):
                for t in range(4):
                    last = nc.tensor.transpose(out[:, t, :], src[:, t, :], ident[:, :])
                last.then_inc(done, 1)

            def step(j, u):
                a, b, c = 2 * j + u, 2 * j + u - 2, 2 * j + u - 4
                if has(j - 2):
                    pe.wait_ge(S["x3_full"], c + 1)
                    wait(pe, S["h_full"], c)
                    transposes(p_x3T, x3[u], S["p_x3T_full"])
                if has(j - 1):
                    pe.wait_ge(S["x1_full"], b + 1)
                    wait(pe, S["x1T_full"], b)
                    transposes(p_x1T, x1[u], S["p_x1T_full"])
                if has(j):
                    pe.wait_ge(x_loaded[u], 16 * (j + 1))
                    wait(pe, S["xT_full"], a)
                    transposes(p_xT, x[u], S["p_xT_full"])
                if has(j - 2):
                    pe.wait_ge(S["x3T_full"], c + 1)
                    wait(pe, S["y4_full"], c)
                    nc.tensor.matmul(p_hT[:, :, :], W["root1"][:, :], x3T[:, :, :], start=True, stop=True).then_inc(S["p_hT_full"], 1)
                if has(j - 1):
                    pe.wait_ge(S["x1T_full"], b + 1)
                    for k in range(2):
                        wait(pe, S[f"g{k}_full"], b)
                        nc.tensor.matmul((p_g0, p_g1)[k][:, :, :], W["W1"][:, k * F:(k + 1) * F], x1T[:, :, :],
                                         start=True, stop=True).then_inc(S[f"p_g{k}_full"], 1)
                if has(j):
                    pe.wait_ge(S["xT_full"], a + 1)
                    wait(pe, S["y1_full"], a)
                    for t in range(4):
                        last = nc.tensor.matmul(p_y1[:, t, :], xT[:, t, :], W["Wsc"][:, :], start=True, stop=True)
                    last.then_inc(S["p_y1_full"], 1)
                if has(j - 2):
                    pe.wait_ge(S["hT_full"], c + 1)
                    transposes(p_h, hT, S["p_h_full"])
                    for t in range(4):
                        last = nc.tensor.matmul(p_y4[:, t, :], hT[:, t, :], W["root2c"][:, :], start=True, stop=True)
                    last.then_inc(S["p_y4_full"], 1)
                if has(j - 1):
                    pe.wait_ge(S["g0_full"], b + 1)
                    pe.wait_ge(S["g1_full"], b + 1)
                    wait(pe, S["h2_full"], b)
                    for t in range(4):
                        for k in range(2):
                            last = nc.tensor.matmul(p_h2[:, t, :], gT[k][:, t, :], W["W2c"][:, k, :], start=(k == 0), stop=(k == 1))
                    last.then_inc(S["p_h2_full"], 1)
            run(pe, step)

        @block.scalar
        def _(act):
            def square(dst, src, ready, used, done, n):
                act.wait_ge(S[ready], n + 1)
                wait(act, S[used], n)
                nc.scalar.activation(dst[:, :, :], src[:, :, :], ACT.Square).then_inc(S[done], 1)

            def root(dst, src, ready, used, done, n):
                act.wait_ge(S[ready], n + 1)
                wait(act, S[used], n)
                nc.scalar.activation(stat[dst][:, :], stat[src][:, :], ACT.Sqrt, bias=eps[:, :], scale=1.0 / F).then_inc(S[done], 1)

            def step(j, u):
                a, b, c = 2 * j + u, 2 * j + u - 2, 2 * j + u - 4
                if has(j - 2):
                    act.wait_ge(S["p_x3T_full"], c + 1)
                    wait(act, S["p_hT_full"], c)
                    nc.scalar.copy(x3T[:, :, :], p_x3T[:, :, :]).then_inc(S["x3T_full"], 1)
                if has(j):
                    act.wait_ge(S["p_xT_full"], a + 1)
                    wait(act, S["p_y1_full"], a)
                    nc.scalar.copy(xT[:, :, :], p_xT[:, :, :]).then_inc(S["xT_full"], 1)
                if has(j - 2):
                    act.wait_ge(S["p_hT_full"], c + 1)
                    wait(act, S["p_y4_full"], c)
                    nc.scalar.activation(hT[:, :, :], p_hT[:, :, :], ACT.Relu, bias=W["b_root1"][:, :]).then_inc(S["hT_full"], 1)
                if has(j - 1):
                    for k in range(2):
                        act.wait_ge(S[f"p_g{k}_full"], b + 1)
                        wait(act, S["p_h2_full"], b)
                        nc.scalar.activation(gT[k][:, :, :], (p_g0, p_g1)[k][:, :, :], ACT.Relu, bias=W["b_W1"][:, k:k + 1]).then_inc(S[f"g{k}_full"], 1)
                if has(j):
                    square(sq1, y1, "y1_full", "ss1_full", "sq1_full", a)
                    root("sd1", "ss1", "ss1_full", "r1_full", "sd1_full", a)
                if has(j - 2):
                    square(sq4, y4, "y4_full", "ss4_full", "sq4_full", c)
                    root("sd4", "ss4", "ss4_full", "r4_full", "sd4_full", c)
                if has(j - 1):
                    square(sq2, y2, "y2_full", "ss2_full", "sq2_full", b)
                    root("sd2", "ss2", "ss2_full", "r2_full", "sd2_full", b)
                    act.wait_ge(S["q2_full"], b + 1)
                    wait(act, S["w2_full"], b)
                    nc.scalar.activation(stat["sd3"][:, :], stat["q2"][:, :], ACT.Sqrt, bias=eps[:, :], scale=1.0 / F).then_inc(S["sd3_full"], 1)
            run(act, step)

        @block.vector
        def _(dve):
            def total(dst, src, ready, used, done, n):
                dve.wait_ge(S[ready], n + 1)
                wait(dve, S[used], n)
                nc.vector.tensor_reduce(stat[dst][:, :], src[:, :, :], AX.X, ALU.add).then_inc(S[done], 1)

            def inverse(dst, src, ready, used, done, n):
                dve.wait_ge(S[ready], n + 1)
                wait(dve, S[used], n)
                nc.vector.reciprocal(stat[dst][:, :], stat[src][:, :]).then_inc(S[done], 1)

            def step(j, u):
                a, b, c = 2 * j + u, 2 * j + u - 2, 2 * j + u - 4
                if has(j - 1):
                    dve.wait_ge(S["p_x1T_full"], b + 1)
                    wait(dve, S["p_g1_full"], b)
                    nc.vector.tensor_copy(x1T[:, :, :], p_x1T[:, :, :]).then_inc(S["x1T_full"], 1)
                if has(j):
                    dve.wait_ge(S["p_y1_full"], a + 1)
                    wait(dve, S["x1_full"], a)
                    wait(dve, S["sq1_full"], a)
                    nc.vector.tensor_tensor(y1[:, :, :], p_y1[:, :, :], over_tiles(W["bsc"]), ALU.add).then_inc(S["y1_full"], 1)
                if has(j - 2):
                    dve.wait_ge(S["p_h_full"], c + 1)
                    wait(dve, stored["h"][u], 16 * (j - 2))
                    nc.vector.tensor_copy(h[u][:, :, :], p_h[:, :, :]).then_inc(S["h_full"], 1)
                if has(j):
                    total("ss1", sq1, "sq1_full", "sd1_full", "ss1_full", a)
                if has(j - 2):
                    dve.wait_ge(S["p_y4_full"], c + 1)
                    dve.wait_ge(S["x3b_full"], c + 1)
                    wait(dve, S["sq4_full"], c)
                    wait(dve, S["o_full"], c)
                    nc.vector.tensor_tensor(y4[:, :, :], p_y4[:, :, :], x3b[:, :, :], ALU.add).then_inc(S["y4_full"], 1)
                if has(j - 1):
                    dve.wait_ge(S["p_h2_full"], b + 1)
                    wait(dve, stored["h2"][u], 16 * (j - 1))
                    wait(dve, S["y2_full"], b)
                    nc.vector.tensor_copy(h2[u][:, :, :], p_h2[:, :, :]).then_inc(S["h2_full"], 1)
                if has(j):
                    inverse("r1", "sd1", "sd1_full", "x1_full", "r1_full", a)
                if has(j - 2):
                    total("ss4", sq4, "sq4_full", "sd4_full", "ss4_full", c)
                    inverse("r4", "sd4", "sd4_full", "o_full", "r4_full", c)
                    dve.wait_ge(S["r4_full"], c + 1)
                    wait(dve, stored["o"][u], 16 * (j - 2))
                    nc.vector.tensor_tensor(o[u][:, :, :], y4[:, :, :], over_rows(stat["r4"]), ALU.mult).then_inc(S["o_full"], 1)
                if has(j - 1):
                    total("ss2", sq2, "sq2_full", "sd2_full", "ss2_full", b)
                    inverse("r2", "sd2", "sd2_full", "x2_full", "r2_full", b)
                    dve.wait_ge(S["r2_full"], b + 1)
                    wait(dve, S["w2_full"], b)
                    nc.vector.tensor_tensor(stat["v2"][:, :], stat["ss2"][:, :], stat["r2"][:, :], ALU.mult).then_inc(S["v2_full"], 1)
                    dve.wait_ge(S["v2_full"], b + 1)
                    wait(dve, S["sd3_full"], b)
                    nc.vector.tensor_tensor(stat["q2"][:, :], stat["v2"][:, :], stat["r2"][:, :], ALU.mult).then_inc(S["q2_full"], 1)
                    dve.wait_ge(S["sd3_full"], b + 1)
                    nc.vector.reciprocal(stat["w2"][:, :], stat["sd3"][:, :]).then_inc(S["w2_full"], 1)
                    dve.wait_ge(S["w2_full"], b + 1)
                    wait(dve, S["x3_full"], b)
                    nc.vector.tensor_tensor(stat["r3"][:, :], stat["w2"][:, :], stat["r2"][:, :], ALU.mult).then_inc(S["r3_full"], 1)
                    dve.wait_ge(S["r3_full"], b + 1)
                    wait(dve, S["p_x3T_full"], b - 1)
                    wait(dve, S["x3b_full"], b - 1)
                    wait(dve, stored["x3"][u], 16 * (j - 1))
                    nc.vector.tensor_tensor(x3[u][:, :, :], y2[:, :, :], over_rows(stat["r3"]), ALU.mult).then_inc(S["x3_full"], 1)
            run(dve, step)

        @block.gpsimd
        def _(pool):
            def step(j, u):
                a, b, c = 2 * j + u, 2 * j + u - 2, 2 * j + u - 4
                if has(j - 2):
                    pool.wait_ge(S["x3_full"], c + 1)
                    wait(pool, S["y4_full"], c)
                    nc.gpsimd.tensor_tensor(x3b[:, :, :], x3[u][:, :, :], over_tiles(W["b4c"]), ALU.add).then_inc(S["x3b_full"], 1)
                if has(j - 1):
                    pool.wait_ge(S["x1_full"], b + 1)
                    wait(pool, S["y2_full"], b)
                    nc.gpsimd.tensor_tensor(x1b[:, :, :], x1[u][:, :, :], over_tiles(W["b2c"]), ALU.add).then_inc(S["x1b_full"], 1)
                if has(j):
                    pool.wait_ge(S["r1_full"], a + 1)
                    wait(pool, S["p_x1T_full"], a - 1)
                    wait(pool, S["x1b_full"], a - 1)
                    wait(pool, stored["x1"][u], 16 * j)
                    nc.gpsimd.tensor_tensor(x1[u][:, :, :], y1[:, :, :], over_rows(stat["r1"]), ALU.mult).then_inc(S["x1_full"], 1)
                if has(j - 1):
                    pool.wait_ge(S["h2_full"], b + 1)
                    pool.wait_ge(S["x1b_full"], b + 1)
                    wait(pool, S["x2_full"], b)
                    wait(pool, S["x3_full"], b)
                    wait(pool, S["sq2_full"], b)
                    nc.gpsimd.tensor_tensor(y2[:, :, :], h2[u][:, :, :], x1b[:, :, :], ALU.add).then_inc(S["y2_full"], 1)
                    pool.wait_ge(S["r2_full"], b + 1)
                    pool.wait_ge(S["y2_full"], b + 1)
                    wait(pool, stored["x2"][u], 16 * (j - 1))
                    nc.gpsimd.tensor_tensor(x2[u][:, :, :], y2[:, :, :], over_rows(stat["r2"]), ALU.mult).then_inc(S["x2_full"], 1)
            run(pool, step)




def at(j, u, k):
    jj, uu = j + (u - k) // UNROLL, (u - k) % UNROLL
    if isinstance(jj, int) and not 0 <= jj < PASSES:
        return None
    return jj, uu


def over_all_tiles(eng, step, lag):
    for u in range(UNROLL):
        step(0, u)
    with eng.Fori(1, PASSES) as j:
        for u in range(UNROLL):
            step(j, u)
    for u in range(lag):
        step(PASSES, u)


def tile(ref):
    return UNROLL * ref[0] + ref[1]


def column(m, ref):
    return m[:, bass.ds(tile(ref), 1)]


def plane(m, ref, a, b):
    return m[:, bass.ds(tile(ref), 1), a:b].rearrange("p a c -> p (a c)")


def prepare_edges(nc, io, W, D):
    with Phase(nc) as m:
        dst_rows, next_rows, src_rows = (m.sb(n, [T, F], i32) for n in ("dst_rows", "next_rows", "src_rows"))
        next_f, src_f = m.sb("next_f", [T, F]), m.sb("src_f", [T, F])
        dst_f, end_keys_apart = m.sb("dst_f", [T, F]), m.sb("end_keys_apart", [HEADS, 2, T])
        node = m.sb("node", [125, N // 125], i32)
        attr = m.sb("attr", [F, T, RELATIONS])
        best, order, score = m.sb("best", [F, T]), m.sb("order", [F, RELATIONS]), m.sb("score", [F, T, RELATIONS])
        next_col, same_as_next, off = m.sb("next_col", [F, T]), m.sb("same_as_next", [F, T]), m.sb("off", [F, T])
        p_cols = m.pb("p_cols", [F, 3, F])
        s = m.named("rows_loaded attr_loaded attr_zeroed rows_converted cols_transposed dst_stored drow_loaded node_made node_stored "
                    "masks_made step_done")
        reach = [D["reach"][:, :, n:n + 1].rearrange("k t a -> k (t a)") for n in range(2)]
        with nc.Block() as block:

            @block.sync
            def _(sp):
                for dst, src in ((dst_rows, io["dst"][0:SLOTS]), (next_rows, io["dst"][1:SLOTS + 1]), (src_rows, io["src"])):
                    sp.dma_start(dst[:, :], src.rearrange("(t e) -> t e", e=F)).then_inc(s["rows_loaded"], 16)
                sp.wait_ge(s["attr_zeroed"], 1)
                whole = E // F
                edges = io["edge_attr_42"][:, EMB:EMB + RELATIONS]
                sp.dma_start(attr[:, 0:whole, :], edges[0:whole * F, :].rearrange("(t e) r -> e t r", e=F),
                             allow_slow_non_contiguous=True).then_inc(s["attr_loaded"], 16)
                sp.dma_start(attr[0:E - whole * F, whole, :], edges[whole * F:E, :],
                             allow_slow_non_contiguous=True).then_inc(s["attr_loaded"], 16)
                sp.wait_ge(s["rows_converted"], 1)
                sp.dma_start(io["dst_f"].rearrange("(t e) -> t e", e=F), dst_f[:, :]).then_inc(s["dst_stored"], 16)
                sp.wait_ge(s["dst_stored"], 16)
                sp.dma_start(D["drow"][:, :], row_vector(io["dst_f"])).then_inc(s["drow_loaded"], 16)
                for end, c in enumerate((0, F - 1)):
                    edge_keys = io["dst_f"].rearrange("(t e) -> t e", e=F)[:, c:c + 1].rearrange("t a -> a t")
                    sp.dma_start(end_keys_apart[:, end, :], edge_keys.partition_broadcast(HEADS),
                                 allow_slow_non_contiguous=True).then_inc(s["drow_loaded"], 16)
                sp.wait_ge(s["node_made"], 1)
                sp.dma_start(io["row_of"].rearrange("(p n) a -> p (n a)", p=125), node[:, :]).then_inc(s["node_stored"], 16)
                sp.wait_ge(s["node_stored"], 16)
                sp.wait_ge(s["drow_loaded"], 48)

            @block.gpsimd
            def _(pool):
                pool.memset(attr[:, :, :], 0.0).then_inc(s["attr_zeroed"], 1)
                pool.iota(node[:, :], pattern=[[1, N // 125]], base=0, channel_multiplier=N // 125).then_inc(s["node_made"], 1)
                pool.iota(D["slot_row"][:, :], pattern=[[F, T]], base=N, channel_multiplier=1)
                pool.wait_ge(s["rows_converted"], 1)
                pool.tensor_copy(reach[0], dst_f[:, F - 1:F].to_broadcast([T, T])).then_inc(s["masks_made"], 1)
                pool.tensor_copy(reach[1], dst_f[:, 0:1].to_broadcast([T, T])).then_inc(s["masks_made"], 1)
                pool.wait_ge(s["masks_made"], 2)
                pool.affine_select(out=reach[0], in_=reach[0], compare_op=ALU.is_gt, fill=-1.0, base=0,
                                   pattern=[[1, T]], channel_multiplier=-1)
                pool.affine_select(out=reach[1], in_=reach[1], compare_op=ALU.is_gt, fill=-1.0, base=0,
                                   pattern=[[-1, T]], channel_multiplier=1)

            @block.tensor
            def _(pe):
                pe.wait_ge(s["rows_converted"], 3)
                for n, rows in enumerate((dst_f, next_f, src_f)):
                    last = nc.tensor.transpose(p_cols[:, n, 0:T], rows[:, :], W["ident"][0:T, 0:T])
                last.then_inc(s["cols_transposed"], 1)

            @block.vector
            def _(dve):
                done = 0

                def chained(ins):
                    nonlocal done
                    done += 1
                    ins.then_inc(s["step_done"], 1)
                    dve.wait_ge(s["step_done"], done)

                for r in range(RELATIONS):
                    chained(nc.vector.memset(order[:, r:r + 1], float(RELATIONS - r)))
                dve.wait_ge(s["rows_loaded"], 48)
                for f, i in ((dst_f, dst_rows), (next_f, next_rows), (src_f, src_rows)):
                    nc.vector.tensor_copy(f[:, :], i[:, :]).then_inc(s["rows_converted"], 1)
                dve.wait_ge(s["cols_transposed"], 1)
                nc.vector.tensor_copy(D["src_col"][:, :], p_cols[:, 2, 0:T])
                chained(nc.vector.tensor_copy(D["dst_col"][:, :], p_cols[:, 0, 0:T]))
                chained(nc.vector.tensor_copy(next_col[:, :], p_cols[:, 1, 0:T]))
                chained(nc.vector.tensor_scalar(D["dst_read"][:, :], D["dst_col"][:, :], float(N - 1), None, ALU.min))
                chained(nc.vector.tensor_tensor(same_as_next[:, :], D["dst_col"][:, :], next_col[:, :], ALU.is_equal))
                chained(nc.vector.tensor_scalar(off[:, :], same_as_next[:, :], float(BEYOND), None, ALU.mult))
                chained(nc.vector.tensor_tensor(D["dst_write"][:, :], D["dst_col"][:, :], off[:, :], ALU.add))
                wide = lambda c: c[:, :].unsqueeze(2).to_broadcast([F, T, RELATIONS])
                dve.wait_ge(s["attr_loaded"], 32)
                chained(nc.vector.tensor_reduce(best[:, :], attr[:, :, :], AX.X, ALU.max))
                chained(nc.vector.tensor_tensor(score[:, :, :], attr[:, :, :], wide(best), ALU.is_equal))
                chained(nc.vector.tensor_tensor(score[:, :, :], score[:, :, :],
                                                order[:, :].unsqueeze(1).to_broadcast([F, T, RELATIONS]), ALU.mult))
                chained(nc.vector.tensor_reduce(best[:, :], score[:, :, :], AX.X, ALU.max))
                chained(nc.vector.tensor_tensor(D["relation"][:, :, :], score[:, :, :], wide(best), ALU.is_equal))
                dve.wait_ge(s["drow_loaded"], 48)
                chained(nc.vector.tensor_copy(D["end_keys"][:, :, :], end_keys_apart[:, :, :].rearrange("h s t -> h t s")))


def map_sources(nc, io, D):
    with Phase(nc) as m:
        index = [m.sb(f"index{u}", [F, 1], i32) for u in range(UNROLL)]
        value = [m.sb(f"value{u}", [F, 1], i32) for u in range(UNROLL)]
        moves = D["moves"]
        moved = moves.sems
        index_ready, value_ready, value_kept = m.sem("map_index_ready"), m.sem("map_value_ready"), m.sem("map_value_kept")
        taken = m.sem("waits_taken")
        with nc.Block() as block:

            @block.gpsimd
            def _(pool):
                def scatter(j, u):
                    wait(pool, moved[u], moves.after(j))
                    pool.tensor_copy(index[u][:, :], column(D["dst_write"], (j, u))).then_inc(index_ready, 1)
                    pool.tensor_copy(value[u][:, :], column(D["slot_row"], (j, u))).then_inc(value_ready, 1)
                    pool.wait_ge(index_ready, UNROLL * j + u + 1)
                    pool.wait_ge(value_ready, UNROLL * j + u + 1)
                    take_waits(pool, taken)
                    pool.indirect_dma_start(out=io["row_of"], out_offset=bass.IndirectOffsetOnAxis(ap=index[u][:, 0:1], axis=0),
                                            in_=value[u][:, :], in_offset=None, bounds_check=N - 1,
                                            oob_is_err=False).then_inc(moved[u], 16)
                over_all_tiles(pool, scatter, 0)

                for u in range(UNROLL):
                    pool.wait_ge(moved[u], moves.after(PASSES))

                def keep(ref):
                    j, u = ref
                    pool.wait_ge(moved[u], moves.after(j + PASSES + 1))
                    pool.tensor_copy(column(D["src_row"], ref), value[u][:, :]).then_inc(value_kept, 1)

                def gather(j, u):
                    if (ref := at(j, u, 3)) is not None:
                        keep(ref)
                    if (ref := at(j, u, 0)) is None:
                        return
                    wait(pool, value_kept, UNROLL * j + u - UNROLL + 1)
                    pool.tensor_copy(index[u][:, :], column(D["src_col"], (j, u))).then_inc(index_ready, 1)
                    pool.wait_ge(index_ready, T + UNROLL * j + u + 1)
                    take_waits(pool, taken)
                    pool.indirect_dma_start(out=value[u][:, :], out_offset=None, in_=io["row_of"],
                                            in_offset=bass.IndirectOffsetOnAxis(ap=index[u][:, 0:1], axis=0)).then_inc(moved[u], 16)
                over_all_tiles(pool, gather, 3)
        moves.passes += 2 * PASSES


def gather_rows(pool, taken, table, index_of, index, index_ready, rows, gathered, rows_used, j, u):
    wait(pool, rows_used, UNROLL * j + u - UNROLL + 1)
    wait(pool, gathered.sems[u], gathered.after(j))
    pool.tensor_copy(index[u][:, :], column(index_of, (j, u))).then_inc(index_ready, 1)
    pool.wait_ge(index_ready, UNROLL * j + u + 1)
    take_waits(pool, taken)
    pool.indirect_dma_start(out=rows[u][:, :], out_offset=None, in_=table,
                            in_offset=bass.IndirectOffsetOnAxis(ap=index[u][:, 0:1], axis=0)).then_inc(gathered.sems[u], 16)


def ends_over_tiles(nc, io, D, width, name):
    with Phase(nc) as m:
        ends_stored, ends_loaded = m.sem(f"{name}_ends_stored"), m.sem(f"{name}_ends_loaded")
        with nc.Block() as block:

            @block.sync
            def _(sp):
                for n, e in enumerate((0, F - 1)):
                    sp.dma_start(io["ends"][n:n + 1, :, 0:width], D["R"][e:e + 1, :, 0:width]).then_inc(ends_stored, 16)
                sp.wait_ge(ends_stored, 32)
                for n in range(2):
                    sp.dma_start(D["ends"][:, n, 0:width], io["ends"][n, :, 0:width]).then_inc(ends_loaded, 16)
                sp.wait_ge(ends_loaded, 32)


def attention_messages(nc, io, W, D):
    with Phase(nc) as m:
        index, index_d = ([m.sb(f"{n}{u}", [F, 1], i32) for u in range(UNROLL)] for n in ("index_s", "index_d"))
        xs, xd = ([m.sb(f"{n}{u}", [F, F]) for u in range(UNROLL)] for n in ("xs", "xd"))
        xT = [m.sb(f"xT{u}", [F, 2, F]) for u in range(2)]
        qk = [m.sb(f"qk{u}", [F, 2, F]) for u in range(2)]
        prod = m.sb("prod", [F, F])
        p_xT = [m.pb(f"p_xT{u}", [F, 2, F]) for u in range(2)]
        p_qkvy = [m.pb(f"p_qkvy{u}", [F, 4, F]) for u in range(2)]
        got_s, got_d = D["moves"], D["dst_moves"]
        s = m.named("waits_taken xs_index_ready xd_index_ready xT_transposed xT_full qkvy_full qk_full v_kept y_kept prod_full scores_full")
        with nc.Block() as block:

            @block.gpsimd
            def _(pool):
                def step(j, u):
                    gather_rows(pool, s["waits_taken"], io["x"], D["src_col"], index, s["xs_index_ready"], xs, got_s, s["xT_transposed"], j, u)
                    gather_rows(pool, s["waits_taken"], io["x"], D["dst_read"], index_d, s["xd_index_ready"], xd, got_d, s["xT_transposed"], j, u)
                over_all_tiles(pool, step, 0)

            @block.tensor
            def _(pe):
                def step(j, u):
                    if (ref := at(j, u, 0)) is not None:
                        t = tile(ref)
                        pe.wait_ge(got_s.sems[u], got_s.after(j + 1))
                        pe.wait_ge(got_d.sems[u], got_d.after(j + 1))
                        wait(pe, s["xT_full"], t - 1)
                        nc.tensor.transpose(p_xT[u % 2][:, 0, :], xs[u][:, :], W["ident"][:, :])
                        nc.tensor.transpose(p_xT[u % 2][:, 1, :], xd[u][:, :], W["ident"][:, :]).then_inc(s["xT_transposed"], 1)
                    if (ref := at(j, u, 1)) is not None:
                        t, v = tile(ref), ref[1] % 2
                        pe.wait_ge(s["xT_full"], t + 1)
                        wait(pe, s["qk_full"], t - 1)
                        wait(pe, s["v_kept"], t - 1)
                        wait(pe, s["y_kept"], t - 1)
                        nc.tensor.matmul(p_qkvy[v][:, 1:3, :], xT[v][:, 0, :], W["Wkv"][:, :, :], start=True, stop=True)
                        nc.tensor.matmul(p_qkvy[v][:, 0, :], xT[v][:, 1, :], W["Wq"][:, :], start=True, stop=True)
                        nc.tensor.matmul(p_qkvy[v][:, 3, :], xT[v][:, 1, :], W["Wsc"][:, :], start=True, stop=True).then_inc(s["qkvy_full"], 1)
                over_all_tiles(pe, step, 1)

            @block.scalar
            def _(act):
                def step(j, u):
                    t = UNROLL * j + u
                    act.wait_ge(s["xT_transposed"], t + 1)
                    wait(act, s["qkvy_full"], t - 1)
                    nc.scalar.copy(xT[u % 2][:, :, :], p_xT[u % 2][:, 0:2, :]).then_inc(s["xT_full"], 1)
                over_all_tiles(act, step, 0)

            @block.vector
            def _(dve):
                def step(j, u):
                    t, v = UNROLL * j + u, u % 2
                    dve.wait_ge(s["qkvy_full"], t + 1)
                    wait(dve, s["prod_full"], t - 1)
                    nc.vector.tensor_tensor(qk[v][:, :, :], p_qkvy[v][:, 0:2, :], W["bqk"][:, :, :], ALU.add).then_inc(s["qk_full"], 1)
                    nc.vector.tensor_tensor(plane(D["R"], (j, u), 0, F), p_qkvy[v][:, 2, :], W["bv"][:, :], ALU.add).then_inc(s["v_kept"], 1)
                    nc.vector.tensor_tensor(plane(D["Y"], (j, u), 0, F), p_qkvy[v][:, 3, :], W["bsc"][:, :], ALU.add).then_inc(s["y_kept"], 1)
                    dve.wait_ge(s["qk_full"], t + 1)
                    wait(dve, s["scores_full"], t)
                    nc.vector.tensor_tensor(prod[:, :], qk[v][:, 0, :], qk[v][:, 1, :], ALU.mult).then_inc(s["prod_full"], 1)
                    dve.wait_ge(s["prod_full"], t + 1)
                    nc.vector.tensor_reduce(plane(D["scores"], (j, u), 0, HEADS), prod[:, :].rearrange("p (h d) -> p h d", h=HEADS),
                                            AX.X, ALU.add).then_inc(s["scores_full"], 1)
                over_all_tiles(dve, step, 0)
        got_s.passes += PASSES
        got_d.passes += PASSES


def weights_of_edges(nc, io, W, D, name, scale):
    P = BLOCK * HEADS
    with Phase(nc) as m:
        top, keys = m.sb("top", [P, BLOCKS, F]), m.sb("keys", [P, BLOCKS, F])
        fresh = m.sb("fresh", [P, BLOCKS * F + 1])
        off_first, off_last = fresh[:, 0:BLOCKS * F].rearrange("p (b e) -> p b e", e=F), keys
        keys8 = m.sb("keys8", [F, T, HEADS])
        ends, ends_out = m.sb("max_ends", [P, BLOCKS, 2]), m.sb("max_ends_out", [P, BLOCKS, 2])
        row = m.sb("row", [HEADS, 2 * T])
        row_fresh = m.sb("row_fresh", [HEADS, 2 * T + 1])
        p_sT, p_kT = m.pb("p_sT", [F, 12, F]), m.pb("p_kT", [F, 12, F])
        p_back = [m.pb(f"p_back{n}", [F, 512]) for n in range(2)]
        s = m.named("keys8_full scores_transposed keys_transposed step_done ends_ready ends_stored row_loaded row_ready row_stored "
                    "ends_loaded top_ready top_back shifted weights_ready")
        half = BLOCKS // 2
        with nc.Block() as block:

            @block.tensor
            def _(pe):
                pe.wait_ge(s["keys8_full"], 1)
                for src, out, done in ((D["scores"], p_sT, "scores_transposed"), (keys8, p_kT, "keys_transposed")):
                    for b in range(BLOCKS):
                        part = src[:, b * BLOCK:(b + 1) * BLOCK, :].rearrange("p t h -> p (t h)")
                        last = nc.tensor.transpose(out[0:P, b, :], part, W["ident"][:, :])
                    last.then_inc(s[done], 1)
                pe.wait_ge(s["top_ready"], 1)
                for b in range(BLOCKS):
                    at_ = (b % half) * P
                    last = nc.tensor.transpose(p_back[b // half][:, at_:at_ + P], top[:, b, :], W["ident"][0:P, 0:P])
                last.then_inc(s["top_back"], 1)

            @block.sync
            def _(sp):
                by_block = io["max_ends"].rearrange("(b p s) -> p b s", b=BLOCKS, s=2)
                by_head = io["max_ends"].rearrange("(t h s) -> h t s", h=HEADS, s=2)
                by_head2 = io["max_ends_out"].rearrange("(t h s) -> h t s", h=HEADS, s=2)
                by_block2 = io["max_ends_out"].rearrange("(b p s) -> p b s", b=BLOCKS, s=2)
                sp.wait_ge(s["ends_ready"], 2)
                sp.dma_start(by_block, ends[:, :, :]).then_inc(s["ends_stored"], 16)
                sp.wait_ge(s["ends_stored"], 16)
                sp.dma_start(row[:, :].rearrange("h (t s) -> h t s", s=2), by_head).then_inc(s["row_loaded"], 16)
                sp.wait_ge(s["row_ready"], 1)
                sp.dma_start(by_head2, row[:, :].rearrange("h (t s) -> h t s", s=2)).then_inc(s["row_stored"], 16)
                sp.wait_ge(s["row_stored"], 16)
                sp.dma_start(ends_out[:, :, :], by_block2).then_inc(s["ends_loaded"], 16)

            @block.vector
            def _(dve):
                done = 0

                def chained(ins):
                    nonlocal done
                    done += 1
                    ins.then_inc(s["step_done"], 1)
                    dve.wait_ge(s["step_done"], done)

                nc.vector.tensor_copy(keys8[:, :, :], D["dst_col"][:, :].unsqueeze(2).to_broadcast([F, T, HEADS])).then_inc(s["keys8_full"], 1)
                row_keys = D["end_keys"][:, :, :].rearrange("h t s -> h (t s)")
                chained(nc.vector.memset(row_fresh[:, :], 0.0))
                chained(nc.vector.tensor_tensor(row_fresh[:, 1:2 * T], row_keys[:, 1:2 * T], row_keys[:, 0:2 * T - 1], ALU.is_equal))
                chained(nc.vector.tensor_scalar(row_fresh[:, :], row_fresh[:, :], -1.0, FAR, ALU.add, ALU.mult))
                dve.wait_ge(s["keys_transposed"], 1)
                chained(nc.vector.tensor_copy(keys[:, :, :], p_kT[0:P, 0:BLOCKS, :]))
                flat = lambda t: t[:, :, :].rearrange("p b e -> p (b e)")
                W_ = BLOCKS * F
                chained(nc.vector.memset(fresh[:, :], 0.0))
                chained(nc.vector.tensor_tensor(fresh[:, 1:W_], flat(keys)[:, 1:W_], flat(keys)[:, 0:W_ - 1], ALU.is_equal))
                chained(nc.vector.memset(fresh[:, 0:W_].rearrange("p (b e) -> p b e", e=F)[:, :, 0:1], 0.0))
                chained(nc.vector.tensor_scalar(fresh[:, :], fresh[:, :], -1.0, FAR, ALU.add, ALU.mult))
                dve.wait_ge(s["scores_transposed"], 1)
                chained(nc.vector.tensor_tensor_scan(flat(top), fresh[:, 0:W_], p_sT[0:P, 0:BLOCKS, :].rearrange("p b e -> p (b e)"),
                                                     -FAR, ALU.add, ALU.max))
                chained(nc.vector.tensor_tensor_scan(flat(top)[:, ::-1], fresh[:, 1:W_ + 1][:, ::-1], flat(top)[:, ::-1], -FAR, ALU.add, ALU.max))
                nc.vector.tensor_copy(ends[:, :, 0:1], top[:, :, 0:1]).then_inc(s["ends_ready"], 1)
                nc.vector.tensor_copy(ends[:, :, 1:2], top[:, :, F - 1:F]).then_inc(s["ends_ready"], 1)
                for out, e in ((off_first, 0), (off_last, F - 1)):
                    chained(nc.vector.tensor_tensor(out[:, :, :], keys[:, :, :], keys[:, :, e:e + 1].to_broadcast([P, BLOCKS, F]), ALU.is_equal))
                    chained(nc.vector.tensor_scalar(out[:, :, :], out[:, :, :], -1.0, FAR, ALU.add, ALU.mult))
                dve.wait_ge(s["row_loaded"], 16)
                chained(nc.vector.tensor_tensor_scan(row[:, :], row_fresh[:, 0:2 * T], row[:, :], -FAR, ALU.add, ALU.max))
                nc.vector.tensor_tensor_scan(row[:, ::-1], row_fresh[:, 1:2 * T + 1][:, ::-1], row[:, ::-1], -FAR,
                                             ALU.add, ALU.max).then_inc(s["row_ready"], 1)
                dve.wait_ge(s["ends_loaded"], 16)
                for off, n in ((off_first, 0), (off_last, 1)):
                    chained(nc.vector.tensor_tensor(off[:, :, :], off[:, :, :], ends_out[:, :, n:n + 1].to_broadcast([P, BLOCKS, F]), ALU.add))
                    chained(nc.vector.tensor_tensor(top[:, :, :], top[:, :, :], off[:, :, :], ALU.max))
                nc.vector.tensor_copy(ends[:, :, 0:1], top[:, :, 0:1]).then_inc(s["top_ready"], 1)
                dve.wait_ge(s["top_back"], 1)
                for n in range(2):
                    part = D["scores"][:, n * T // 2:(n + 1) * T // 2, :].rearrange("p t h -> p (t h)")
                    nc.vector.tensor_tensor(part, part, p_back[n][:, 0:half * P], ALU.subtract).then_inc(s["shifted"], 1)

            @block.scalar
            def _(act):
                act.wait_ge(s["shifted"], 2)
                act.activation(D["scores"][:, :, :], D["scores"][:, :, :], ACT.Exp, scale=scale).then_inc(s["weights_ready"], 1)


def sums_in_tiles(nc, io, W, D, name, table=None, heads=0, extra=None):
    width = F + (heads or 0) + (extra.shape[2] if extra is not None else 0)
    with Phase(nc) as m:
        same = [m.sb(f"same{u}", [F, F]) for u in range(2)]
        rows = [m.sb(f"rows{u}", [F, F]) for u in range(UNROLL)]
        index = [m.sb(f"index{u}", [F, 1], i32) for u in range(UNROLL)]
        p_R = [m.pb(f"p_R{u}", [F, 512]) for u in range(2)]
        gathered = D["moves"]
        s = m.named("waits_taken index_ready same_full rows_weighted summed R_full")
        with nc.Block() as block:
            if table is not None:
                @block.gpsimd
                def _(pool):
                    def step(j, u):
                        gather_rows(pool, s["waits_taken"], table, D["src_row"], index, s["index_ready"], rows, gathered, s["summed"], j, u)
                    over_all_tiles(pool, step, 0)

            @block.vector
            def _(dve):
                def step(j, u):
                    t = UNROLL * j + u
                    wait(dve, s["summed"], t - 1)
                    nc.vector.tensor_scalar(same[u % 2][:, :], D["drow"][:, bass.ds(t * F, F)], column(D["dst_col"], (j, u)),
                                            None, ALU.is_equal).then_inc(s["same_full"], 1)
                    if table is None:
                        wait(dve, s["summed"], t - UNROLL + 1)
                        w = plane(D["scores"], (j, u), 0, heads).unsqueeze(2).to_broadcast([F, heads, F // heads])
                        nc.vector.tensor_tensor(rows[u][:, :].rearrange("p (h d) -> p h d", h=heads),
                                                plane(D["R"], (j, u), 0, F).rearrange("p (h d) -> p h d", h=heads),
                                                w, ALU.mult).then_inc(s["rows_weighted"], 1)
                over_all_tiles(dve, step, 0)

            @block.tensor
            def _(pe):
                def step(j, u):
                    t = UNROLL * j + u
                    pe.wait_ge(s["same_full"], t + 1)
                    wait(pe, s["R_full"], t - 1)
                    if table is None:
                        pe.wait_ge(s["rows_weighted"], t + 1)
                    else:
                        pe.wait_ge(gathered.sems[u], gathered.after(j + 1))
                    last = nc.tensor.matmul(p_R[u % 2][:, 0:F], same[u % 2][:, :], rows[u][:, :], start=True, stop=True)
                    if heads:
                        last = nc.tensor.matmul(p_R[u % 2][:, F:F + heads], same[u % 2][:, :], plane(D["scores"], (j, u), 0, heads),
                                                start=True, stop=True)
                    if extra is not None:
                        last = nc.tensor.matmul(p_R[u % 2][:, F + heads:width], same[u % 2][:, :], plane(extra, (j, u), 0, extra.shape[2]),
                                                start=True, stop=True)
                    last.then_inc(s["summed"], 1)
                over_all_tiles(pe, step, 0)

            @block.scalar
            def _(act):
                def step(j, u):
                    t = UNROLL * j + u
                    act.wait_ge(s["summed"], t + 1)
                    nc.scalar.copy(plane(D["R"], (j, u), 0, width), p_R[u % 2][:, 0:width]).then_inc(s["R_full"], 1)
                over_all_tiles(act, step, 0)
        if table is not None:
            gathered.passes += PASSES
    ends_over_tiles(nc, io, D, width, name)


def select_tiles(pool, D, apart, select, s, j, u):
    t = UNROLL * j + u
    keys = D["drow"][0:T, bass.ds(t * F, F)].unsqueeze(1).to_broadcast([T, 2, F])
    wait(pool, s["selected"], t)
    pool.tensor_tensor(apart[:, :, :], keys, plane(D["reach"], (j, u), 0, 2)[0:T, :].unsqueeze(2).to_broadcast([T, 2, F]),
                       ALU.subtract).then_inc(s["apart_full"], 1)
    pool.wait_ge(s["apart_full"], t + 1)
    wait(pool, s["carried"], t - 1)
    take_waits(pool, s["waits_taken"])
    pool.tensor_scalar(select[u % 2][:, :, :], apart[:, :, :], 0.0, None, ALU.is_equal).then_inc(s["selected"], 1)


def carry(nc, pe, D, p_carry, select, s, width, j, u, more=()):
    t, v = UNROLL * j + u, u % 2
    pe.wait_ge(s["selected"], t + 1)
    wait(pe, s["carry_added"], t - 1)
    nc.tensor.matmul(p_carry[v][:, 0:width], select[v][:, 0, :], D["ends"][:, 1, 0:width], start=True, stop=False)
    last = nc.tensor.matmul(p_carry[v][:, 0:width], select[v][:, 1, :], D["ends"][:, 0, 0:width], start=False, stop=not more)
    last.then_inc(s["carried"], 1)
    for n, (lhsT, rhs) in enumerate(more):
        last = nc.tensor.matmul(p_carry[v][:, 0:width], lhsT, rhs, start=False, stop=(n == len(more) - 1))
    return last


def selectors(m):
    return m.sb("apart", [T, 2, F]), [m.sb(f"select{u}", [T, 2, F]) for u in range(2)]


def attention_rows(nc, io, W, D):
    width = F + HEADS + RELATIONS
    with Phase(nc) as m:
        apart, select = selectors(m)
        whole = [m.sb(f"whole{u}", [F, width]) for u in range(2)]
        inverse, mean = m.sb("inverse", [F, HEADS]), m.sb("mean_value", [F, F])
        p_carry = [m.pb(f"p_carry{u}", [F, 512]) for u in range(2)]
        s = m.named("waits_taken apart_full selected carried carry_added inverse_full mean_full y_full stats_full count_kept")
        with nc.Block() as block:

            @block.gpsimd
            def _(pool):
                over_all_tiles(pool, lambda j, u: select_tiles(pool, D, apart, select, s, j, u), 0)

            @block.tensor
            def _(pe):
                over_all_tiles(pe, lambda j, u: carry(nc, pe, D, p_carry, select, s, width, j, u), 0)

            @block.vector
            def _(dve):
                def step(j, u):
                    t, v = UNROLL * j + u, u % 2
                    dve.wait_ge(s["carried"], t + 1)
                    wait(dve, s["count_kept"], t - 1)
                    nc.vector.tensor_tensor(whole[v][:, :], p_carry[v][:, 0:width], plane(D["R"], (j, u), 0, width), ALU.add).then_inc(s["carry_added"], 1)
                    dve.wait_ge(s["carry_added"], t + 1)
                    nc.vector.reciprocal(inverse[:, :], whole[v][:, F:F + HEADS]).then_inc(s["inverse_full"], 1)
                    dve.wait_ge(s["inverse_full"], t + 1)
                    nc.vector.tensor_tensor(mean[:, :].rearrange("p (h d) -> p h d", h=HEADS), whole[v][:, 0:F].rearrange("p (h d) -> p h d", h=HEADS),
                                            inverse[:, :].unsqueeze(2).to_broadcast([F, HEADS, F // HEADS]), ALU.mult).then_inc(s["mean_full"], 1)
                    dve.wait_ge(s["mean_full"], t + 1)
                    y = plane(D["Y"], (j, u), 0, F)
                    nc.vector.tensor_tensor(y, y, mean[:, :], ALU.add).then_inc(s["y_full"], 1)
                    dve.wait_ge(s["y_full"], t + 1)
                    nc.vector.bn_stats(plane(D["stats"], (j, u), 0, 6), y).then_inc(s["stats_full"], 1)
                over_all_tiles(dve, step, 0)

            @block.scalar
            def _(act):
                def step(j, u):
                    act.wait_ge(s["carry_added"], UNROLL * j + u + 1)
                    nc.scalar.copy(plane(D["count"], (j, u), 0, RELATIONS), whole[u % 2][:, F + HEADS:width]).then_inc(s["count_kept"], 1)
                over_all_tiles(act, step, 0)


def degrees(nc, io, W, D):
    with Phase(nc) as m:
        deg, root = m.sb("deg", [F, T]), m.sb("root", [F, T])
        s = m.named("step_done deg_full root_full")
        with nc.Block() as block:

            @block.vector
            def _(dve):
                done = 0

                def chained(ins):
                    nonlocal done
                    done += 1
                    ins.then_inc(s["step_done"], 1)
                    dve.wait_ge(s["step_done"], done)

                count, share = D["count"][:, :, :], D["share"][:, :, :]
                chained(nc.vector.tensor_reduce(deg[:, :], count, AX.X, ALU.add))
                nc.vector.tensor_scalar(deg[:, :], deg[:, :], 1.0, None, ALU.add).then_inc(s["deg_full"], 1)
                chained(nc.vector.tensor_scalar(share, count, 1.0, None, ALU.max))
                chained(nc.vector.reciprocal(share, share))
                chained(nc.vector.tensor_tensor(share, share, D["relation"][:, :, :], ALU.mult))
                dve.wait_ge(s["root_full"], 1)
                chained(nc.vector.reciprocal(D["dinv"][:, :], root[:, :]))

            @block.scalar
            def _(act):
                act.wait_ge(s["deg_full"], 1)
                act.activation(root[:, :], deg[:, :], ACT.Sqrt).then_inc(s["root_full"], 1)


def normalise(nc, io, W, D, name, table=None, scaled=False):
    with Phase(nc) as m:
        mean, var, dev, r = (m.sb(n, [F, T]) for n in ("mean", "var", "dev", "r"))
        rows = [m.sb(f"rows{u}", [F, F]) for u in range(UNROLL)]
        index = [m.sb(f"index{u}", [F, 1], i32) for u in range(UNROLL)]
        written = D["moves"]
        s = m.named("waits_taken step_done var_full dev_full normal_full scaled_full stored index_ready")
        with nc.Block() as block:

            @block.vector
            def _(dve):
                done = 0

                def chained(ins):
                    nonlocal done
                    done += 1
                    ins.then_inc(s["step_done"], 1)
                    dve.wait_ge(s["step_done"], done)

                part = lambda n: D["stats"][:, :, n:n + 1].rearrange("p t a -> p (t a)")
                chained(nc.vector.tensor_tensor(mean[:, :], part(1), part(4), ALU.add))
                chained(nc.vector.tensor_scalar(mean[:, :], mean[:, :], 0.5, None, ALU.mult))
                chained(nc.vector.tensor_tensor(dev[:, :], part(1), part(4), ALU.subtract))
                chained(nc.vector.tensor_tensor(dev[:, :], dev[:, :], dev[:, :], ALU.mult))
                chained(nc.vector.tensor_tensor(var[:, :], part(2), part(5), ALU.add))
                nc.vector.scalar_tensor_tensor(out=var[:, :], in0=dev[:, :], scalar=F / 4.0, in1=var[:, :],
                                               op0=ALU.mult, op1=ALU.add).then_inc(s["var_full"], 1)
                dve.wait_ge(s["dev_full"], 1)
                chained(nc.vector.reciprocal(r[:, :], dev[:, :]))

                def step(j, u):
                    y = plane(D["Y"], (j, u), 0, F)
                    out = y
                    if table is None:
                        wait(dve, written.sems[u], written.after(j))
                        out = rows[u][:, :]
                    nc.vector.tensor_scalar(out, y, column(mean, (j, u)), column(r, (j, u)), ALU.subtract, ALU.mult).then_inc(s["normal_full"], 1)
                over_all_tiles(dve, step, 0)

            @block.scalar
            def _(act):
                act.wait_ge(s["var_full"], 1)
                act.activation(dev[:, :], var[:, :], ACT.Sqrt, bias=W["eps"][:, :], scale=1.0 / F).then_inc(s["dev_full"], 1)

            if table is None or scaled:
                @block.gpsimd
                def _(pool):
                    def step(j, u):
                        t = UNROLL * j + u
                        if scaled:
                            pool.wait_ge(s["normal_full"], t + 1)
                            pool.tensor_tensor(plane(D["R"], (j, u), 0, F), plane(D["Y"], (j, u), 0, F),
                                               column(D["dinv"], (j, u)).to_broadcast([F, F]), ALU.mult).then_inc(s["scaled_full"], 1)
                        if table is None:
                            wait(pool, written.sems[u], written.after(j))
                            pool.tensor_copy(index[u][:, :], column(D["dst_write"], (j, u))).then_inc(s["index_ready"], 1)
                            pool.wait_ge(s["index_ready"], t + 1)
                            pool.wait_ge(s["normal_full"], t + 1)
                            take_waits(pool, s["waits_taken"])
                            pool.indirect_dma_start(out=io["out"], out_offset=bass.IndirectOffsetOnAxis(ap=index[u][:, 0:1], axis=0),
                                                    in_=rows[u][:, :], in_offset=None, bounds_check=N - 1,
                                                    oob_is_err=False).then_inc(written.sems[u], 16)
                    over_all_tiles(pool, step, 0)
                    if table is None:
                        for u in range(UNROLL):
                            pool.wait_ge(written.sems[u], written.after(PASSES))

            if table is not None:
                @block.sync
                def _(sp):
                    store_slots(sp, table, D["R"] if scaled else D["Y"], s["scaled_full" if scaled else "normal_full"], s["stored"])


def store_slots(sp, table, src, ready, stored):
    for b in range(BLOCKS):
        sp.wait_ge(ready, BLOCK * (b + 1))
        a = N + b * BLOCK * F
        sp.dma_start(table[a:a + BLOCK * F, :].rearrange("(t p) f -> p t f", p=F), src[:, b * BLOCK:(b + 1) * BLOCK, 0:F]).then_inc(stored, 16)
    sp.wait_ge(stored, 16 * BLOCKS)


def hidden_rows(nc, io, W, D, layer):
    one = layer == 1
    with Phase(nc) as m:
        apart, select = selectors(m)
        sum_, inner = m.sb("sum_", [F, F]), [m.sb(f"inner{u}", [F, F]) for u in range(2)]
        mid = m.sb("mid", [F, F])
        innerT = [m.sb(f"innerT{u}", [F, F]) for u in range(2)]
        gT = [m.sb(f"gT{u}", [F, 2, F]) for u in range(2)]
        own, yT = ([m.sb(f"{n}{u}", [F, F]) for u in range(2)] for n in ("own", "yT"))
        p_carry = [m.pb(f"p_carry{u}", [F, 512]) for u in range(2)]
        p_T = [m.pb(f"p_T{u}", [F, 512]) for u in range(2)]
        p_g = [m.pb(f"p_g{u}", [F, 4, F]) for u in range(2)]
        p_out = [m.pb(f"p_out{u}", [F, 512]) for u in range(2)]
        s = m.named("waits_taken apart_full selected carried complete carry_added mid_full inner_full inner_transposed innerT_full g_multiplied gT_full "
                    "out_multiplied z_full y_full y_biased stored own_full y_transposed yT_full")
        table = io["H2"] if one else io["H"]
        with nc.Block() as block:

            @block.gpsimd
            def _(pool):
                def step(j, u):
                    select_tiles(pool, D, apart, select, s, j, u)
                    y = plane(D["Y"], (j, u), 0, F)
                    if one:
                        if (ref := at(j, u, 1)) is not None:
                            pool.wait_ge(s["mid_full"], tile(ref) + 1)
                            y = plane(D["Y"], ref, 0, F)
                            pool.tensor_tensor(y, y, W["b2c"][:, :], ALU.add).then_inc(s["y_biased"], 1)
                def last_step(j, u):
                    if (ref := at(j, u, 0)) is not None:
                        step(j, u)
                    elif one and u == 0:
                        ref = at(j, u, 1)
                        pool.wait_ge(s["mid_full"], tile(ref) + 1)
                        y = plane(D["Y"], ref, 0, F)
                        pool.tensor_tensor(y, y, W["b2c"][:, :], ALU.add).then_inc(s["y_biased"], 1)
                over_all_tiles(pool, last_step, 1)

            @block.tensor
            def _(pe):
                def step(j, u):
                    if not one and (ref := at(j, u, 0)) is not None:
                        t = tile(ref)
                        wait(pe, s["innerT_full"], t - 1)
                        wait(pe, s["yT_full"], t - 1)
                        pe.wait_ge(s["own_full"], t + 1)
                        nc.tensor.transpose(p_g[u % 2][:, 0, :], own[u % 2][:, :], W["ident"][:, :]).then_inc(s["y_transposed"], 1)
                    if (ref := at(j, u, 3)) is not None:
                        t, v = tile(ref), ref[1] % 2
                        if one:
                            pe.wait_ge(s["gT_full"], t + 1)
                            wait(pe, s["z_full"], t - 1)
                            for k in range(2):
                                last = nc.tensor.matmul(p_out[v][:, 0:F], gT[v][:, k, :], W["W2c"][:, k, :], start=(k == 0), stop=(k == 1))
                        else:
                            pe.wait_ge(s["innerT_full"], t + 1)
                            wait(pe, s["y_full"], t - 1)
                            nc.tensor.matmul(p_out[v][:, 0:F], innerT[v][:, :], W["root2c"][:, :], start=True, stop=False)
                            last = nc.tensor.matmul(p_out[v][:, 0:F], W["ones"][0:1, :], W["b4c"][0:1, :], start=False, stop=True)
                        last.then_inc(s["out_multiplied"], 1)
                    if one and (ref := at(j, u, 2)) is not None:
                        t, v = tile(ref), ref[1] % 2
                        pe.wait_ge(s["innerT_full"], t + 1)
                        wait(pe, s["gT_full"], t - 1)
                        for k in range(2):
                            last = nc.tensor.matmul(p_g[v][:, k, :], W["W1"][:, k * F:(k + 1) * F], innerT[v][:, :], start=True, stop=True)
                        last.then_inc(s["g_multiplied"], 1)
                    if (ref := at(j, u, 1)) is not None:
                        t, v = tile(ref), ref[1] % 2
                        pe.wait_ge(s["inner_full"], t + 1)
                        wait(pe, s["innerT_full"], t - 1)
                        nc.tensor.transpose(p_T[v][:, 0:F], inner[v][:, :], W["ident"][:, :]).then_inc(s["inner_transposed"], 1)
                    if (ref := at(j, u, 0)) is not None:
                        if one:
                            carry(nc, pe, D, p_carry, select, s, F, j, u)
                        else:
                            pe.wait_ge(s["yT_full"], tile(ref) + 1)
                            carry(nc, pe, D, p_carry, select, s, F, j, u,
                                  ((yT[u % 2][:, :], W["root1"][:, :]), (W["ones"][0:1, :], W["b_root1_row"][0:1, :]))).then_inc(s["complete"], 1)
                over_all_tiles(pe, step, 3)

            @block.scalar
            def _(act):
                def step(j, u):
                    if not one and (ref := at(j, u, 0)) is not None:
                        wait(act, s["y_transposed"], tile(ref) - 1)
                        nc.scalar.copy(own[u % 2][:, :], plane(D["Y"], ref, 0, F)).then_inc(s["own_full"], 1)
                    if one and (ref := at(j, u, 2)) is not None:
                        t, v = tile(ref), ref[1] % 2
                        act.wait_ge(s["g_multiplied"], t + 1)
                        wait(act, s["out_multiplied"], t - 1)
                        for k in range(2):
                            last = nc.scalar.activation(gT[v][:, k, :], p_g[v][:, k, :], ACT.Relu, bias=W["b_W1"][:, k:k + 1])
                            if k == 1:
                                last.then_inc(s["gT_full"], 1)
                    if (ref := at(j, u, 1)) is not None:
                        t, v = tile(ref), ref[1] % 2
                        act.wait_ge(s["inner_transposed"], t + 1)
                        wait(act, s["g_multiplied" if one else "out_multiplied"], t - 1)
                        nc.scalar.copy(innerT[v][:, :], p_T[v][:, 0:F]).then_inc(s["innerT_full"], 1)
                    if not one and (ref := at(j, u, 0)) is not None:
                        act.wait_ge(s["y_transposed"], tile(ref) + 1)
                        wait(act, s["complete"], tile(ref) - 1)
                        nc.scalar.copy(yT[u % 2][:, :], p_g[u % 2][:, 0, :]).then_inc(s["yT_full"], 1)
                over_all_tiles(act, step, 2)

            @block.vector
            def _(dve):
                def step(j, u):
                    if (ref := at(j, u, 3)) is not None:
                        t, v = tile(ref), ref[1] % 2
                        dve.wait_ge(s["out_multiplied"], t + 1)
                        y = plane(D["Y"], ref, 0, F)
                        if one:
                            z = plane(D["R"], ref, 0, F)
                            nc.vector.tensor_scalar(z, p_out[v][:, 0:F], column(D["dinv"], ref), None, ALU.mult).then_inc(s["z_full"], 1)
                            dve.wait_ge(s["z_full"], t + 1)
                            dve.wait_ge(s["y_biased"], t + 1)
                            nc.vector.scalar_tensor_tensor(out=y, in0=z, scalar=column(D["dinv"], ref), in1=y, op0=ALU.mult, op1=ALU.add).then_inc(s["y_full"], 1)
                        else:
                            dve.wait_ge(s["own_full"], t + 1)
                            nc.vector.tensor_tensor(y, p_out[v][:, 0:F], y, ALU.add).then_inc(s["y_full"], 1)
                    if (ref := at(j, u, 0)) is not None:
                        t, v = tile(ref), u % 2
                        dve.wait_ge(s["carried" if one else "complete"], t + 1)
                        wait(dve, s["mid_full" if one else "inner_full"], t)
                        nc.vector.tensor_tensor(sum_[:, :], p_carry[v][:, 0:F], plane(D["R"], ref, 0, F), ALU.add).then_inc(s["carry_added"], 1)
                        dve.wait_ge(s["carry_added"], t + 1)
                        if one:
                            wait(dve, s["inner_full"], t)
                            nc.vector.scalar_tensor_tensor(out=mid[:, :], in0=plane(D["Y"], ref, 0, F), scalar=column(D["dinv"], ref), in1=sum_[:, :],
                                                           op0=ALU.mult, op1=ALU.add).then_inc(s["mid_full"], 1)
                            dve.wait_ge(s["mid_full"], t + 1)
                            wait(dve, s["inner_transposed"], t - 1)
                            nc.vector.tensor_scalar(inner[v][:, :], mid[:, :], column(D["dinv"], ref), None, ALU.mult).then_inc(s["inner_full"], 1)
                        else:
                            wait(dve, s["inner_transposed"], t - 1)
                            wait(dve, s["z_full"], t - 1)
                            nc.vector.tensor_scalar(inner[v][:, :], sum_[:, :], 0.0, None, ALU.max).then_inc(s["inner_full"], 1)
                            dve.wait_ge(s["inner_full"], t + 1)
                            nc.vector.tensor_scalar(plane(D["R"], ref, 0, F), inner[v][:, :], 0.0, None, ALU.max).then_inc(s["z_full"], 1)
                over_all_tiles(dve, step, 3)

            @block.sync
            def _(sp):
                store_slots(sp, table, D["R"], s["z_full"], s["stored"])


def summed_rows(nc, io, W, D, scaled):
    with Phase(nc) as m:
        apart, select = selectors(m)
        sum_ = m.sb("sum_", [F, F])
        p_carry = [m.pb(f"p_carry{u}", [F, 512]) for u in range(2)]
        s = m.named("waits_taken apart_full selected carried carry_added y_full stats_full")
        with nc.Block() as block:

            @block.gpsimd
            def _(pool):
                over_all_tiles(pool, lambda j, u: select_tiles(pool, D, apart, select, s, j, u), 0)

            @block.tensor
            def _(pe):
                over_all_tiles(pe, lambda j, u: carry(nc, pe, D, p_carry, select, s, F, j, u), 0)

            @block.vector
            def _(dve):
                def step(j, u):
                    t = UNROLL * j + u
                    y = plane(D["Y"], (j, u), 0, F)
                    dve.wait_ge(s["carried"], t + 1)
                    wait(dve, s["y_full"], t)
                    nc.vector.tensor_tensor(sum_[:, :], p_carry[u % 2][:, 0:F], plane(D["R"], (j, u), 0, F), ALU.add).then_inc(s["carry_added"], 1)
                    dve.wait_ge(s["carry_added"], t + 1)
                    if scaled:
                        nc.vector.scalar_tensor_tensor(out=y, in0=sum_[:, :], scalar=column(D["dinv"], (j, u)), in1=y,
                                                       op0=ALU.mult, op1=ALU.add).then_inc(s["y_full"], 1)
                    else:
                        nc.vector.tensor_tensor(y, sum_[:, :], y, ALU.add).then_inc(s["y_full"], 1)
                    dve.wait_ge(s["y_full"], t + 1)
                    nc.vector.bn_stats(plane(D["stats"], (j, u), 0, 6), y).then_inc(s["stats_full"], 1)
                over_all_tiles(dve, step, 0)


def gat_messages(nc, io, W, D):
    with Phase(nc) as m:
        index = [m.sb(f"index{u}", [F, 1], i32) for u in range(UNROLL)]
        rows = [m.sb(f"rows{u}", [F, F]) for u in range(UNROLL)]
        own = [m.sb(f"own{u}", [F, F]) for u in range(2)]
        bothT = [m.sb(f"bothT{u}", [F, 2, F]) for u in range(2)]
        raw = m.sb("raw", [F, GAT_HEADS])
        p_T = [m.pb(f"p_T{u}", [F, 4, F]) for u in range(2)]
        p_h = [m.pb(f"p_h{u}", [F, 512]) for u in range(2)]
        gathered = D["moves"]
        s = m.named("waits_taken index_ready own_full transposed bothT_full multiplied h_kept raw_full scores_full step_done")
        H4 = GAT_HEADS
        with nc.Block() as block:

            @block.gpsimd
            def _(pool):
                over_all_tiles(pool, lambda j, u: gather_rows(pool, s["waits_taken"], io["X2"], D["src_row"], index, s["index_ready"], rows, gathered,
                                                              s["transposed"], j, u), 0)

            @block.tensor
            def _(pe):
                def step(j, u):
                    if (ref := at(j, u, 0)) is not None:
                        t = tile(ref)
                        pe.wait_ge(gathered.sems[u], gathered.after(j + 1))
                        wait(pe, s["bothT_full"], t - 1)
                        nc.tensor.transpose(p_T[u % 2][:, 0, :], rows[u][:, :], W["ident"][:, :])
                        pe.wait_ge(s["own_full"], t + 1)
                        nc.tensor.transpose(p_T[u % 2][:, 1, :], own[u % 2][:, :], W["ident"][:, :]).then_inc(s["transposed"], 1)
                    if (ref := at(j, u, 1)) is not None:
                        t, v = tile(ref), ref[1] % 2
                        pe.wait_ge(s["bothT_full"], t + 1)
                        wait(pe, s["h_kept"], t - 1)
                        wait(pe, s["raw_full"], t - 1)
                        nc.tensor.matmul(p_h[v][:, 0:F], bothT[v][:, 0, :], W["Wgat"][:, :, :], start=True, stop=True)
                        nc.tensor.matmul(p_h[v][:, F:F + H4], bothT[v][:, 0, :], W["w_src"][:, :], start=True, stop=False)
                        nc.tensor.matmul(p_h[v][:, F:F + H4], bothT[v][:, 1, :], W["w_dst"][:, :], start=False, stop=True).then_inc(s["multiplied"], 1)
                over_all_tiles(pe, step, 1)

            @block.scalar
            def _(act):
                def step(j, u):
                    if (ref := at(j, u, 0)) is not None:
                        wait(act, s["transposed"], tile(ref) - 1)
                        nc.scalar.copy(own[u % 2][:, :], plane(D["Y"], ref, 0, F)).then_inc(s["own_full"], 1)
                    if (ref := at(j, u, 1)) is not None:
                        act.wait_ge(s["multiplied"], tile(ref) + 1)
                        nc.scalar.copy(plane(D["R"], ref, 0, F), p_h[ref[1] % 2][:, 0:F]).then_inc(s["h_kept"], 1)
                    if (ref := at(j, u, 0)) is not None:
                        t = tile(ref)
                        act.wait_ge(s["transposed"], t + 1)
                        wait(act, s["multiplied"], t - 1)
                        nc.scalar.copy(bothT[u % 2][:, :, :], p_T[u % 2][:, 0:2, :]).then_inc(s["bothT_full"], 1)
                over_all_tiles(act, step, 1)

            @block.vector
            def _(dve):
                def step(j, u):
                    t = UNROLL * j + u
                    dve.wait_ge(s["h_kept"], t + 1)
                    wait(dve, s["scores_full"], t)
                    nc.vector.tensor_copy(raw[:, :], p_h[u % 2][:, F:F + H4]).then_inc(s["raw_full"], 1)
                    dve.wait_ge(s["raw_full"], t + 1)
                    nc.vector.scalar_tensor_tensor(out=plane(D["scores"], (j, u), 0, H4), in0=raw[:, :], scalar=ALPHA, in1=raw[:, :],
                                                   op0=ALU.mult, op1=ALU.max).then_inc(s["scores_full"], 1)
                over_all_tiles(dve, step, 0)
                dve.wait_ge(s["scores_full"], T)
                nc.vector.tensor_copy(D["scores"][:, :, H4:HEADS], D["scores"][:, :, 0:H4]).then_inc(s["step_done"], 1)
                dve.wait_ge(s["step_done"], 1)
        gathered.passes += PASSES


def gat_rows(nc, io, W, D):
    H4 = GAT_HEADS
    width = F + H4
    with Phase(nc) as m:
        apart, select = selectors(m)
        whole = m.sb("whole", [F, width])
        inverse = m.sb("inverse", [F, H4])
        mean, low = ([m.sb(f"{n}{u}", [F, F]) for u in range(2)] for n in ("mean_h", "low"))
        grown = [m.sb(f"grown{u}", [F, F]) for u in range(2)]
        p_carry = [m.pb(f"p_carry{u}", [F, 512]) for u in range(2)]
        s = m.named("waits_taken apart_full selected carried carry_added inverse_full mean_full low_full grown_full high_full y_full stats_full")
        with nc.Block() as block:

            @block.gpsimd
            def _(pool):
                over_all_tiles(pool, lambda j, u: select_tiles(pool, D, apart, select, s, j, u), 0)

            @block.tensor
            def _(pe):
                over_all_tiles(pe, lambda j, u: carry(nc, pe, D, p_carry, select, s, width, j, u), 0)

            @block.scalar
            def _(act):
                def step(j, u):
                    t = UNROLL * j + u
                    act.wait_ge(s["low_full"], t + 1)
                    wait(act, s["y_full"], t - 1)
                    act.activation(grown[u % 2][:, :], low[u % 2][:, :], ACT.Exp).then_inc(s["grown_full"], 1)
                over_all_tiles(act, step, 0)

            @block.vector
            def _(dve):
                def step(j, u):
                    if (ref := at(j, u, 0)) is not None:
                        t, v = tile(ref), u % 2
                        dve.wait_ge(s["carried"], t + 1)
                        wait(dve, s["mean_full"], t)
                        nc.vector.tensor_tensor(whole[:, :], p_carry[v][:, 0:width], plane(D["R"], ref, 0, width), ALU.add).then_inc(s["carry_added"], 1)
                        dve.wait_ge(s["carry_added"], t + 1)
                        nc.vector.reciprocal(inverse[:, :], whole[:, F:width]).then_inc(s["inverse_full"], 1)
                        dve.wait_ge(s["inverse_full"], t + 1)
                        wait(dve, s["high_full"], t - 1)
                        nc.vector.tensor_tensor(mean[v][:, :].rearrange("p (h d) -> p h d", h=H4), whole[:, 0:F].rearrange("p (h d) -> p h d", h=H4),
                                                inverse[:, :].unsqueeze(2).to_broadcast([F, H4, F // H4]), ALU.mult).then_inc(s["mean_full"], 1)
                        dve.wait_ge(s["mean_full"], t + 1)
                        wait(dve, s["grown_full"], t - 1)
                        nc.vector.tensor_scalar(low[v][:, :], mean[v][:, :], 0.0, None, ALU.min).then_inc(s["low_full"], 1)
                    if (ref := at(j, u, 1)) is not None:
                        t, v = tile(ref), ref[1] % 2
                        y = plane(D["Y"], ref, 0, F)
                        dve.wait_ge(s["low_full"], t + 1)
                        nc.vector.scalar_tensor_tensor(out=y, in0=mean[v][:, :], scalar=0.0, in1=y, op0=ALU.max, op1=ALU.add).then_inc(s["high_full"], 1)
                        dve.wait_ge(s["high_full"], t + 1)
                        dve.wait_ge(s["grown_full"], t + 1)
                        nc.vector.scalar_tensor_tensor(out=y, in0=grown[v][:, :], scalar=-1.0, in1=y, op0=ALU.add, op1=ALU.add).then_inc(s["y_full"], 1)
                        dve.wait_ge(s["y_full"], t + 1)
                        nc.vector.bn_stats(plane(D["stats"], ref, 0, 6), y).then_inc(s["stats_full"], 1)
                over_all_tiles(dve, step, 1)


def relation_sums(nc, io, W, D, name, table, w_rel):
    RG = 4
    groups = [(a, min(a + RG, RELATIONS)) for a in range(0, RELATIONS, RG)]
    with Phase(nc) as m:
        same = [m.sb(f"same{u}", [F, F]) for u in range(2)]
        rows = [m.sb(f"rows{u}", [F, F]) for u in range(UNROLL)]
        index = [m.sb(f"index{u}", [F, 1], i32) for u in range(UNROLL)]
        rowsT = [m.sb(f"rowsT{u}", [F, F]) for u in range(2)]
        shares = m.sb("shares", [F, RELATIONS, F])
        message = [m.sb(f"message{u}", [F, F]) for u in range(2)]
        w = m.sb("w_rel", [F, RELATIONS, F])
        p_T = m.pb("p_T", [F, 512])
        p_R = m.pb("p_R", [F, 512])
        p_w = [[m.pb(f"p_w{u}_{n}", [F, 4, F]) for n in range(len(groups))] for u in range(2)]
        gathered = D["moves"]
        s = m.named("waits_taken w_loaded index_ready transposed rowsT_full multiplied shares_full message_full same_full summed R_full")
        with nc.Block() as block:

            @block.sync
            def _(sp):
                sp.dma_start(w[:, :, :], w_rel.rearrange("r p f -> p r f")).then_inc(s["w_loaded"], 16)

            @block.gpsimd
            def _(pool):
                over_all_tiles(pool, lambda j, u: gather_rows(pool, s["waits_taken"], table, D["src_row"], index, s["index_ready"], rows, gathered,
                                                              s["transposed"], j, u), 0)

            @block.tensor
            def _(pe):
                pe.wait_ge(s["w_loaded"], 16)

                def step(j, u):
                    if (ref := at(j, u, 0)) is not None:
                        pe.wait_ge(gathered.sems[u], gathered.after(j + 1))
                        wait(pe, s["rowsT_full"], tile(ref))
                        nc.tensor.transpose(p_T[:, 0:F], rows[u][:, :], W["ident"][:, :]).then_inc(s["transposed"], 1)
                    if (ref := at(j, u, 1)) is not None:
                        t, v = tile(ref), ref[1] % 2
                        pe.wait_ge(s["rowsT_full"], t + 1)
                        wait(pe, s["shares_full"], t - 1)
                        for n, (a, b) in enumerate(groups):
                            last = nc.tensor.matmul(p_w[v][n][:, 0:b - a, :], rowsT[v][:, :], w[:, a:b, :], start=True, stop=True)
                        last.then_inc(s["multiplied"], 1)
                    if (ref := at(j, u, 3)) is not None:
                        t, v = tile(ref), ref[1] % 2
                        pe.wait_ge(s["message_full"], t + 1)
                        pe.wait_ge(s["same_full"], t + 1)
                        wait(pe, s["R_full"], t)
                        nc.tensor.matmul(p_R[:, 0:F], same[v][:, :], message[v][:, :], start=True, stop=True).then_inc(s["summed"], 1)
                over_all_tiles(pe, step, 3)

            @block.scalar
            def _(act):
                def step(j, u):
                    if (ref := at(j, u, 0)) is not None:
                        act.wait_ge(s["transposed"], tile(ref) + 1)
                        wait(act, s["multiplied"], tile(ref) - 1)
                        nc.scalar.copy(rowsT[u % 2][:, :], p_T[:, 0:F]).then_inc(s["rowsT_full"], 1)
                    if (ref := at(j, u, 3)) is not None:
                        act.wait_ge(s["summed"], tile(ref) + 1)
                        nc.scalar.copy(plane(D["R"], ref, 0, F), p_R[:, 0:F]).then_inc(s["R_full"], 1)
                over_all_tiles(act, step, 3)

            @block.vector
            def _(dve):
                def step(j, u):
                    if (ref := at(j, u, 2)) is not None:
                        t, v = tile(ref), ref[1] % 2
                        wait(dve, s["summed"], t - 1)
                        nc.vector.tensor_scalar(same[v][:, :], D["drow"][:, bass.ds(t * F, F)], column(D["dst_col"], ref),
                                                None, ALU.is_equal).then_inc(s["same_full"], 1)
                        dve.wait_ge(s["multiplied"], t + 1)
                        wait(dve, s["message_full"], t)
                        for n, (a, b) in enumerate(groups):
                            share = plane(D["share"], ref, a, b).unsqueeze(2).to_broadcast([F, b - a, F])
                            last = nc.vector.tensor_tensor(shares[:, a:b, :], p_w[v][n][:, 0:b - a, :], share, ALU.mult)
                        last.then_inc(s["shares_full"], 1)
                        dve.wait_ge(s["shares_full"], t + 1)
                        nc.vector.tensor_reduce(message[v][:, :], shares[:, :, :].rearrange("p r f -> p f r"), AX.X, ALU.add).then_inc(s["message_full"], 1)
                over_all_tiles(dve, step, 2)
        gathered.passes += PASSES
    ends_over_tiles(nc, io, D, F, name)


def gnn_kernel(nc, io):
    with ExitStack() as stack:
        W, D = {}, {}
        with Phase(nc) as m:
            prepare_weights(nc, Memory(nc, stack), m, io, W)
        edges = Memory(nc, stack)
        D["moves"], D["dst_moves"] = PoolMoves(edges, "pool_moved"), PoolMoves(edges, "pool_moved_dst")
        for name, shape, dt in (("dst_col", [F, T], fp32), ("src_col", [F, T], i32), ("dst_read", [F, T], i32),
                                ("dst_write", [F, T], i32), ("slot_row", [F, T], i32), ("src_row", [F, T], i32),
                                ("reach", [T, T, 2], fp32), ("relation", [F, T, RELATIONS], fp32),
                                ("end_keys", [HEADS, T, 2], fp32)):
            D[name] = edges.sb(name, shape, dt)
        with Phase(nc) as m:
            dense_phase(nc, m, io, W)
        for name, shape, dt in (("drow", [F, SLOTS], fp32), ("Y", [F, T, F], fp32), ("R", [F, T, F + HEADS + RELATIONS], fp32),
                                ("scores", [F, T, HEADS], fp32),
                                ("stats", [F, T, 6], fp32), ("dinv", [F, T], fp32), ("ends", [T, 2, F + HEADS + RELATIONS], fp32)):
            D[name] = edges.sb(name, shape, dt)
        D["count"] = D["share"] = edges.sb("count", [F, T, RELATIONS])
        prepare_edges(nc, io, W, D)
        map_sources(nc, io, D)
        attention_messages(nc, io, W, D)
        weights_of_edges(nc, io, W, D, "l0", (F // HEADS) ** -0.5)
        sums_in_tiles(nc, io, W, D, "l0", heads=HEADS, extra=D["relation"])
        attention_rows(nc, io, W, D)
        degrees(nc, io, W, D)
        normalise(nc, io, W, D, "l0", io["Z1"], scaled=True)
        sums_in_tiles(nc, io, W, D, "l1a", table=io["Z1"])
        hidden_rows(nc, io, W, D, 1)
        sums_in_tiles(nc, io, W, D, "l1b", table=io["H2"])
        summed_rows(nc, io, W, D, scaled=True)
        normalise(nc, io, W, D, "l1", io["X2"])
        gat_messages(nc, io, W, D)
        weights_of_edges(nc, io, W, D, "l2", 1.0)
        sums_in_tiles(nc, io, W, D, "l2", heads=GAT_HEADS)
        gat_rows(nc, io, W, D)
        normalise(nc, io, W, D, "l2", io["X3"])
        relation_sums(nc, io, W, D, "l3a", io["X3"], io["L3_gnn_w_rel1"])
        hidden_rows(nc, io, W, D, 3)
        relation_sums(nc, io, W, D, "l3b", io["H"], io["L3_gnn_w_rel2"])
        summed_rows(nc, io, W, D, scaled=False)
        normalise(nc, io, W, D, "l3")


_INS = ['x', 'edge_attr_42', 'L0_gnn_Wq', 'L0_gnn_bq', 'L0_gnn_Wk', 'L0_gnn_bk', 'L0_gnn_Wv', 'L0_gnn_bv', 'L0_gnn_Ws', 'L0_gnn_bs',
        'L1_gnn_W1', 'L1_gnn_b1', 'L1_gnn_W2', 'L1_gnn_b2', 'L2_gnn_W', 'L2_gnn_a_src', 'L2_gnn_a_dst',
        'L3_gnn_w_rel1', 'L3_gnn_root1', 'L3_gnn_b1', 'L3_gnn_w_rel2', 'L3_gnn_root2', 'L3_gnn_b2']


def kernel(**inputs):
    import numpy as _np
    import concourse.bacc as _bacc
    from concourse.bass_utils import run_bass_kernel_spmd as _run

    nc = _bacc.Bacc("TRN2", target_bir_lowering=False, num_devices=1)
    arrays = {name: _np.ascontiguousarray(inputs[name]) for name in _INS}
    arrays["src"] = _np.concatenate([inputs["src"], _np.zeros(SLOTS - E, _np.int32)])
    arrays["dst"] = _np.concatenate([inputs["dst"], _np.full(SLOTS + 1 - E, PAD_KEY, _np.int32)])
    io = {name: nc.dram_tensor(f"in_{name}", a.shape, mybir.dt.from_np(a.dtype), kind="ExternalInput").ap() for name, a in arrays.items()}
    for n in ("Z1", "H2", "X2", "X3", "H"):
        io[n] = nc.dram_tensor(n, (N + SLOTS, F), fp32, kind="Internal").ap()
    io["row_of"] = nc.dram_tensor("row_of", (N, 1), i32, kind="Internal").ap()
    io["dst_f"] = nc.dram_tensor("dst_keys", (SLOTS,), fp32, kind="Internal").ap()
    io["ends"] = nc.dram_tensor("tile_ends", (2, T, F + HEADS + RELATIONS), fp32, kind="Internal").ap()
    for n in ("max_ends", "max_ends_out"):
        io[n] = nc.dram_tensor(n + "_rows", (T * HEADS * 2,), fp32, kind="Internal").ap()
    io["out"] = nc.dram_tensor("out", (N, F), fp32, kind="ExternalOutput").ap()
    gnn_kernel(nc, io)
    r = _run(nc, [{f"in_{name}": a for name, a in arrays.items()}], core_ids=[0])
    return r.results[0]["out"]
```

```python
from contextlib import ExitStack

import numpy as np

import concourse.bass as bass
from concourse import mybir
from concourse.alu_op_type import AluOpType as ALU

fp32 = mybir.dt.float32
i32 = mybir.dt.int32
ACT = mybir.ActivationFunctionType
AX = mybir.AxisListType

N = 50000
E = 12500
F = 128
GROUPS = (N + 511) // 512
LAST_BASE = N - 512
EPS = 1e-5
HEADS = 8
GAT_HEADS = 4
ALPHA = 0.2
RELATIONS = 10
EMB = 16
BLOCKS, BLOCK = 10, 10
T = BLOCKS * BLOCK
SLOTS = T * F
UNROLL = 4
PASSES = T // UNROLL
PAD_KEY = 1 << 16
BEYOND = 1 << 20
FAR = 1e30


class Memory:

    def __init__(self, nc, stack, prefix=""):
        self.nc, self.stack, self.prefix = nc, stack, prefix

    def sb(self, name, shape, dt=fp32):
        return self.stack.enter_context(self.nc.sbuf_tensor(self.prefix + name, shape, dt))

    def pb(self, name, shape, dt=fp32):
        return self.stack.enter_context(self.nc.psum_tensor(self.prefix + name, shape, dt))

    def sem(self, name):
        return self.stack.enter_context(self.nc.semaphore(self.prefix + name))


def clear(nc, sems):
    numbers = sorted(s.num for s in sems)
    with nc.Block() as block:

        @block.gpsimd
        def _(pool):
            at_ = 0
            while at_ < len(numbers):
                end = at_
                while end + 1 < len(numbers) and numbers[end + 1] == numbers[end] + 1:
                    end += 1
                pool.sem_clear(range(numbers[at_], numbers[end] + 1))
                at_ = end + 1


class Phase(Memory):

    opened = 0

    def __init__(self, nc):
        Phase.opened += 1
        super().__init__(nc, ExitStack(), f"phase{Phase.opened}_")
        self.sems = []

    def sem(self, name):
        s = super().sem(name)
        self.sems.append(s)
        return s

    def named(self, names):
        return {n: self.sem(n) for n in names.split()}

    def __enter__(self):
        self.stack.__enter__()
        return self

    def __exit__(self, *e):
        if e[0] is None and self.sems:
            clear(self.nc, self.sems)
        return self.stack.__exit__(*e)


def at(j, u, k):
    jj, uu = j + (u - k) // UNROLL, (u - k) % UNROLL
    if isinstance(jj, int) and not 0 <= jj < PASSES:
        return None
    return jj, uu


def over_all_tiles(eng, step, lag):
    lead = 1 if lag == 0 else 2 if lag <= 5 else 3
    for k in range(lead * UNROLL):
        step(k // UNROLL, k % UNROLL)
    with eng.Fori(lead, PASSES) as j:
        for u in range(UNROLL):
            step(j, u)
    for k in range(lag):
        step(PASSES + k // UNROLL, k % UNROLL)


def tile(ref):
    return UNROLL * ref[0] + ref[1]


def column(m, ref):
    return m[:, bass.ds(tile(ref), 1)]


def plane(m, ref, a, b):
    return m[:, bass.ds(tile(ref), 1), a:b].rearrange("p a c -> p (a c)")


class PoolMoves:

    def __init__(self, mem, name):
        self.sems = [mem.sem(f"{name}{u}") for u in range(UNROLL)]
        self.passes = 0

    def after(self, j):
        return 16 * (self.passes + j) if isinstance(j, int) else (j + self.passes) * 16


def wait(eng, s, count):
    if not isinstance(count, int) or count > 0:
        eng.wait_ge(s, count)


def row_vector(v):
    return v.rearrange("(a n) -> a n", a=1).partition_broadcast(F)


def take_waits(eng, taken):
    eng.sem_inc(taken)


def prepare_weights(nc, mem, m, io, W):
    sb = mem.sb
    for name, shape in (("ident", [F, F]), ("eps", [F, 1]), ("Wsc", [F, F]), ("W1", [F, 2 * F]), ("W2c", [F, 2, F]),
                        ("root1", [F, F]), ("root2c", [F, F]), ("b_W1", [F, 2]), ("b_root1", [F, 1]),
                        ("bsc", [F, F]), ("b2c", [F, F]), ("b4c", [F, F]), ("one", [F, 1]), ("b_root1_rows", [F, F]),
                        ("Wq", [F, F]), ("Wkv", [F, 2, F]), ("bqk", [F, 2, F]), ("bv", [F, F]), ("Wgat", [F, GAT_HEADS, F // GAT_HEADS]),
                        ("w_src", [F, GAT_HEADS]), ("w_dst", [F, GAT_HEADS])):
        W[name] = sb(name, shape)
    mean, a_src, a_dst, prod = m.sb("mean", [F, 1]), m.sb("a_src", [F, F]), m.sb("a_dst", [F, F]), m.sb("a_prod", [F, F])
    loaded, ident_done, step_done = m.sem("loaded"), m.sem("ident_done"), m.sem("step_done")
    by_head = lambda w: w.rearrange("h p d -> p h d")
    heads = lambda m: m.rearrange("p (h d) -> p h d", h=HEADS)
    loads = [
        (heads(W["Wq"][:, :]), by_head(io["L0_gnn_Wq"])), (heads(W["Wkv"][:, 0, :]), by_head(io["L0_gnn_Wk"])),
        (heads(W["Wkv"][:, 1, :]), by_head(io["L0_gnn_Wv"])), (W["Wgat"][:, :, :], by_head(io["L2_gnn_W"])),
        (W["bqk"][:, 0, :], row_vector(io["L0_gnn_bq"].rearrange("h d -> (h d)"))),
        (W["bqk"][:, 1, :], row_vector(io["L0_gnn_bk"].rearrange("h d -> (h d)"))),
        (W["bv"][:, :], row_vector(io["L0_gnn_bv"].rearrange("h d -> (h d)"))),
        (a_src[:, :], row_vector(io["L2_gnn_a_src"].rearrange("h d -> (h d)"))),
        (a_dst[:, :], row_vector(io["L2_gnn_a_dst"].rearrange("h d -> (h d)"))),
        (W["b_root1_rows"][:, :], row_vector(io["L3_gnn_b1"])),
        (W["Wsc"][:, :], io["L0_gnn_Ws"]), (W["W1"][:, :], io["L1_gnn_W1"]),
        (W["W2c"][:, :, :], io["L1_gnn_W2"].rearrange("(k p) f -> p k f", k=2)),
        (W["root1"][:, :], io["L3_gnn_root1"]), (W["root2c"][:, :], io["L3_gnn_root2"]),
        (W["b_W1"][:, :], io["L1_gnn_b1"].rearrange("(k p) -> p k", k=2)),
        (W["b_root1"][:, :], io["L3_gnn_b1"].rearrange("(p a) -> p a", a=1)),
        (W["bsc"][:, :], row_vector(io["L0_gnn_bs"])), (W["b2c"][:, :], row_vector(io["L1_gnn_b2"])),
        (W["b4c"][:, :], row_vector(io["L3_gnn_b2"])),
    ]
    with nc.Block() as block:

        @block.sync
        def _(sp):
            for dst, src in loads:
                sp.dma_start(dst, src, allow_slow_non_contiguous=True).then_inc(loaded, 16)

        @block.gpsimd
        def _(pool):
            pool.memset(W["ident"][:, :], 0.0).then_inc(ident_done, 1)
            pool.memset(W["eps"][:, :], EPS)
            pool.memset(W["one"][:, :], 1.0).then_inc(ident_done, 1)
            pool.wait_ge(ident_done, 2)
            pool.affine_select(out=W["ident"][:, :], in_=W["ident"][:, :], compare_op=ALU.not_equal, fill=1.0,
                               base=0, pattern=[[-1, F]], channel_multiplier=1).then_inc(ident_done, 1)

        @block.vector
        def _(dve):
            done = 0

            def chained(ins):
                nonlocal done
                done += 1
                ins.then_inc(step_done, 1)
                dve.wait_ge(step_done, done)

            dve.wait_ge(loaded, 16 * len(loads))
            dve.wait_ge(ident_done, 3)
            chained(nc.vector.tensor_tensor(W["Wsc"][:, :], W["Wsc"][:, :], W["ident"][:, :], ALU.add))
            for m in (W["Wsc"][:, :], W["W2c"][:, 0, :], W["W2c"][:, 1, :], W["root2c"][:, :],
                      W["bsc"][:, :], W["b2c"][:, :], W["b4c"][:, :]):
                chained(nc.vector.tensor_reduce(mean[:, :], m, AX.X, ALU.add))
                chained(nc.vector.tensor_scalar(mean[:, :], mean[:, :], -1.0 / F, None, ALU.mult))
                chained(nc.vector.tensor_scalar(m, m, mean[:, 0:1], None, ALU.add))
            for a, w in ((a_src, W["w_src"]), (a_dst, W["w_dst"])):
                p = prod[:, :].rearrange("p (h d) -> p h d", h=GAT_HEADS)
                chained(nc.vector.tensor_tensor(p, W["Wgat"][:, :, :], a[:, :].rearrange("p (h d) -> p h d", h=GAT_HEADS), ALU.mult))
                chained(nc.vector.tensor_reduce(w[:, :], p, AX.X, ALU.add))


def dense_phase(nc, mem, io, W):
    sb, pb, sem = mem.sb, mem.pb, mem.sem
    ident, eps = W["ident"], W["eps"]
    RING = 4
    places = {"x": 4, "xT": 2, "y1": 4, "sq1": 2, "x1": 4, "x1b": 4, "x1T": 2, "g0": 2, "g1": 2, "h2": 4, "y2": 4, "sq2": 2,
              "x2": 4, "x3": 4, "x3b": 4, "x3T": 2, "hT": 2, "h": 4, "y4": 4, "sq4": 2, "o": 4}
    B = {n: [sb(f"{n}_{u}", [F, 4, F], fp32) for u in range(k)] for n, k in places.items()}
    stats = {"ss1": 2, "sd1": 2, "r1": 2, "ss2": 4, "sd2": 2, "r2": 4, "v2": 2, "q2": 2, "sd3": 2, "w2": 2, "r3": 2, "ss4": 2, "sd4": 2, "r4": 2}
    B.update({n: [sb(f"{n}_{u}", [F, 4], fp32) for u in range(k)] for n, k in stats.items()})

    p_xT, p_y1, p_x1T, p_g0, p_g1, p_h2, p_x3T, p_hT = (pb(f"P{b}", [F, 4, F], fp32) for b in range(8))
    p_h, p_y4 = p_x3T, p_hT

    from_pe = "p_xT p_y1 p_x1T p_g0 p_g1 p_h2 p_x3T p_hT p_h p_y4".split()
    S = {n: sem(f"d_{n}_full") for n in [*B, *from_pe] if n != "x"}
    x_loaded = [sem(f"d_x_loaded{u}") for u in range(RING)]
    tables = {"x1": "Z1", "h2": "H2", "x2": "X2", "x3": "X3", "h": "H", "o": "out"}
    stored = {n: [sem(f"d_{n}_stored{u}") for u in range(RING)] for n in tables}
    LEAD, END = 6, GROUPS // RING - 1

    def group(i, k):
        j, u = i
        jj, uu = j + (u - k) // RING, (u - k) % RING
        if isinstance(jj, int) and not 0 <= RING * jj + uu < GROUPS:
            return None
        return jj, uu

    def number(g):
        return RING * g[0] + g[1]

    def buf(n, g):
        return B[n][g[1] % len(B[n])]

    def rows(table, g):
        g = number(g)
        base = LAST_BASE if isinstance(g, int) and g == GROUPS - 1 else g * 512
        return table[bass.ds(base, 512), :].rearrange("(p t) f -> p t f", t=4)

    def run(eng, step, lag):
        for i in range(LEAD * RING):
            step((i // RING, i % RING))
        with eng.Fori(LEAD, END) as j:
            for u in range(RING):
                step((j, u))
        for i in range(END * RING, GROUPS + lag):
            step((i // RING, i % RING))

    over_tiles = lambda w: w[:, :].unsqueeze(1).to_broadcast([F, 4, F])
    over_rows = lambda r: r[:, :].unsqueeze(2).to_broadcast([F, 4, F])

    def made(eng, n, g, ahead=0):
        count = number(g) + 1 + ahead
        wait(eng, S[n], min(count, GROUPS) if isinstance(count, int) else count)

    def left(eng, out, by, g):
        made(eng, by, g, -len(B[out]))

    def left_by_store(eng, n, g):
        wait(eng, stored[n][g[1]], 16 * g[0])

    with nc.Block() as block:

        @block.sync
        def _(sp):
            def load(g):
                made(sp, "p_xT", g, -RING)
                sp.dma_start(buf("x", g)[:, :, :], rows(io["x"], g)).then_inc(x_loaded[g[1]], 16)

            def store(n, g):
                made(sp, n, g)
                if isinstance(g[0], int) and number(g) == GROUPS - 1:
                    sp.wait_ge(stored[n][g[1] - 1], 16 * (g[0] + 1))
                sp.dma_start(rows(io[tables[n]], g), buf(n, g)[:, :, :]).then_inc(stored[n][g[1]], 16)

            for u in range(3):
                load((0, u))

            def step(i):
                if (g := group(i, -3)) is not None:
                    load(g)
                for n, lag in (("x1", 5), ("h2", 8), ("x2", 12), ("x3", 13), ("h", 16), ("o", 19)):
                    if (g := group(i, lag)) is not None:
                        store(n, g)
            run(sp, step, 19)
            for n in stored:
                for u in range(RING):
                    sp.wait_ge(stored[n][u], 16 * len(range(u, GROUPS, RING)))

        @block.tensor
        def _(pe):
            def transposes(out, src, done):
                for t in range(4):
                    last = nc.tensor.transpose(out[:, t, :], src[:, t, :], ident[:, :])
                last.then_inc(S[done], 1)

            def products(out, lhsT, weight, done):
                for t in range(4):
                    last = nc.tensor.matmul(out[:, t, :], lhsT[:, t, :], W[weight][:, :], start=True, stop=True)
                last.then_inc(S[done], 1)

            def step(i):
                if (g := group(i, 15)) is not None:
                    made(pe, "hT", g)
                    made(pe, "x3T", g, 1)
                    transposes(p_h, buf("hT", g), "p_h")
                    products(p_y4, buf("hT", g), "root2c", "p_y4")
                if (g := group(i, 7)) is not None:
                    made(pe, "g0", g)
                    made(pe, "g1", g)
                    made(pe, "h2", g, -1)
                    for t in range(4):
                        for k in range(2):
                            last = nc.tensor.matmul(p_h2[:, t, :], buf(f"g{k}", g)[:, t, :], W["W2c"][:, k, :], start=(k == 0), stop=(k == 1))
                    last.then_inc(S["p_h2"], 1)
                if (g := group(i, 6)) is not None:
                    made(pe, "x1T", g)
                    for k in range(2):
                        made(pe, f"g{k}", g, -1)
                        nc.tensor.matmul((p_g0, p_g1)[k][:, :, :], W["W1"][:, k * F:(k + 1) * F], buf("x1T", g)[:, :, :],
                                         start=True, stop=True).then_inc(S[f"p_g{k}"], 1)
                if (g := group(i, 13)) is not None:
                    made(pe, "x3", g)
                    made(pe, "x3T", g, -1)
                    made(pe, "h", g, -2)
                    transposes(p_x3T, buf("x3", g), "p_x3T")
                if (g := group(i, 14)) is not None:
                    made(pe, "x3T", g)
                    made(pe, "hT", g, -1)
                    made(pe, "y4", g, -1)
                    nc.tensor.matmul(p_hT[:, :, :], W["root1"][:, :], buf("x3T", g)[:, :, :], start=True, stop=True).then_inc(S["p_hT"], 1)
                if (g := group(i, 5)) is not None:
                    made(pe, "x1", g)
                    made(pe, "x1T", g, -1)
                    transposes(p_x1T, buf("x1", g), "p_x1T")
                if (g := group(i, 1)) is not None:
                    made(pe, "xT", g)
                    made(pe, "y1", g, -1)
                    products(p_y1, buf("xT", g), "Wsc", "p_y1")
                if (g := group(i, 0)) is not None:
                    pe.wait_ge(x_loaded[g[1]], 16 * (g[0] + 1))
                    made(pe, "xT", g, -1)
                    transposes(p_xT, buf("x", g), "p_xT")
            run(pe, step, 15)

        @block.scalar
        def _(act):
            def square(dst, src, total, i, lag):
                if (g := group(i, lag)) is not None:
                    made(act, src, g)
                    left(act, dst, total, g)
                    nc.scalar.activation(buf(dst, g)[:, :, :], buf(src, g)[:, :, :], ACT.Square).then_inc(S[dst], 1)

            def root(dst, src, inverse, i, lag):
                if (g := group(i, lag)) is not None:
                    made(act, src, g)
                    left(act, dst, inverse, g)
                    nc.scalar.activation(buf(dst, g)[:, :], buf(src, g)[:, :], ACT.Sqrt, bias=eps[:, :], scale=1.0 / F).then_inc(S[dst], 1)

            def read_out(dst, bank, src, user, i, lag, **kw):
                if (g := group(i, lag)) is not None:
                    made(act, src, g)
                    left(act, dst, user, g)
                    if kw:
                        nc.scalar.activation(buf(dst, g)[:, :, :], bank[:, :, :], ACT.Relu, **kw).then_inc(S[dst], 1)
                    else:
                        nc.scalar.copy(buf(dst, g)[:, :, :], bank[:, :, :]).then_inc(S[dst], 1)

            def step(i):
                square("sq4", "y4", "ss4", i, 16)
                square("sq2", "y2", "ss2", i, 9)
                square("sq1", "y1", "ss1", i, 2)
                read_out("g0", p_g0, "p_g0", "p_h2", i, 6, bias=W["b_W1"][:, 0:1])
                read_out("g1", p_g1, "p_g1", "p_h2", i, 6, bias=W["b_W1"][:, 1:2])
                root("sd1", "ss1", "r1", i, 3)
                root("sd2", "ss2", "r2", i, 10)
                root("sd4", "ss4", "r4", i, 17)
                root("sd3", "q2", "w2", i, 11)
                read_out("x3T", p_x3T, "p_x3T", "p_hT", i, 13)
                read_out("hT", p_hT, "p_hT", "p_y4", i, 14, bias=W["b_root1"][:, :])
                read_out("xT", p_xT, "p_xT", "p_y1", i, 0)
            run(act, step, 17)

        @block.vector
        def _(dve):
            def total(dst, src, users, i, lag):
                if (g := group(i, lag)) is not None:
                    made(dve, src, g)
                    for by in users:
                        left(dve, dst, by, g)
                    nc.vector.tensor_reduce(buf(dst, g)[:, :], buf(src, g)[:, :, :], AX.X, ALU.add).then_inc(S[dst], 1)

            def inverse(dst, src, users, i, lag):
                if (g := group(i, lag)) is not None:
                    made(dve, src, g)
                    for by in users:
                        left(dve, dst, by, g)
                    nc.vector.reciprocal(buf(dst, g)[:, :], buf(src, g)[:, :]).then_inc(S[dst], 1)

            def times(dst, a, b, user, i, lag):
                if (g := group(i, lag)) is not None:
                    made(dve, a, g)
                    made(dve, b, g)
                    left(dve, dst, user, g)
                    nc.vector.tensor_tensor(buf(dst, g)[:, :], buf(a, g)[:, :], buf(b, g)[:, :], ALU.mult).then_inc(S[dst], 1)

            def step(i):
                inverse("w2", "sd3", ("r3",), i, 12)
                inverse("r1", "sd1", ("x1",), i, 4)
                inverse("r2", "sd2", ("x2", "r3"), i, 11)
                times("r3", "w2", "r2", "x3", i, 12)
                inverse("r4", "sd4", ("o",), i, 18)
                times("v2", "ss2", "r2", "q2", i, 11)
                if (g := group(i, 12)) is not None:
                    made(dve, "r3", g)
                    left(dve, "x3", "p_x3T", g)
                    left(dve, "x3", "x3b", g)
                    left_by_store(dve, "x3", g)
                    nc.vector.tensor_tensor(buf("x3", g)[:, :, :], buf("y2", g)[:, :, :], over_rows(buf("r3", g)), ALU.mult).then_inc(S["x3"], 1)
                times("q2", "v2", "r2", "sd3", i, 11)
                total("ss1", "sq1", ("sd1",), i, 3)
                total("ss2", "sq2", ("sd2", "v2"), i, 10)
                total("ss4", "sq4", ("sd4",), i, 17)
                if (g := group(i, 15)) is not None:
                    made(dve, "p_h", g)
                    left_by_store(dve, "h", g)
                    nc.vector.tensor_copy(buf("h", g)[:, :, :], p_h[:, :, :]).then_inc(S["h"], 1)
                    made(dve, "p_y4", g)
                    made(dve, "x3b", g)
                    left(dve, "y4", "sq4", g)
                    left(dve, "y4", "o", g)
                    nc.vector.tensor_tensor(buf("y4", g)[:, :, :], p_y4[:, :, :], buf("x3b", g)[:, :, :], ALU.add).then_inc(S["y4"], 1)
                if (g := group(i, 18)) is not None:
                    made(dve, "r4", g)
                    left_by_store(dve, "o", g)
                    nc.vector.tensor_tensor(buf("o", g)[:, :, :], buf("y4", g)[:, :, :], over_rows(buf("r4", g)), ALU.mult).then_inc(S["o"], 1)
                if (g := group(i, 7)) is not None:
                    made(dve, "p_h2", g)
                    left(dve, "h2", "y2", g)
                    left_by_store(dve, "h2", g)
                    nc.vector.tensor_copy(buf("h2", g)[:, :, :], p_h2[:, :, :]).then_inc(S["h2"], 1)
                if (g := group(i, 5)) is not None:
                    made(dve, "p_x1T", g)
                    left(dve, "x1T", "p_g1", g)
                    nc.vector.tensor_copy(buf("x1T", g)[:, :, :], p_x1T[:, :, :]).then_inc(S["x1T"], 1)
                if (g := group(i, 1)) is not None:
                    made(dve, "p_y1", g)
                    left(dve, "y1", "x1", g)
                    left(dve, "y1", "sq1", g)
                    nc.vector.tensor_tensor(buf("y1", g)[:, :, :], p_y1[:, :, :], over_tiles(W["bsc"]), ALU.add).then_inc(S["y1"], 1)
            run(dve, step, 18)

        @block.gpsimd
        def _(pool):
            def step(i):
                if (g := group(i, 13)) is not None:
                    made(pool, "x3", g)
                    left(pool, "x3b", "y4", g)
                    nc.gpsimd.tensor_tensor(buf("x3b", g)[:, :, :], buf("x3", g)[:, :, :], over_tiles(W["b4c"]), ALU.add).then_inc(S["x3b"], 1)
                if (g := group(i, 8)) is not None:
                    made(pool, "h2", g)
                    made(pool, "x1b", g)
                    left(pool, "y2", "sq2", g)
                    left(pool, "y2", "x2", g)
                    left(pool, "y2", "x3", g)
                    nc.gpsimd.tensor_tensor(buf("y2", g)[:, :, :], buf("h2", g)[:, :, :], buf("x1b", g)[:, :, :], ALU.add).then_inc(S["y2"], 1)
                if (g := group(i, 5)) is not None:
                    made(pool, "x1", g)
                    left(pool, "x1b", "y2", g)
                    nc.gpsimd.tensor_tensor(buf("x1b", g)[:, :, :], buf("x1", g)[:, :, :], over_tiles(W["b2c"]), ALU.add).then_inc(S["x1b"], 1)
                if (g := group(i, 4)) is not None:
                    made(pool, "r1", g)
                    left(pool, "x1", "p_x1T", g)
                    left(pool, "x1", "x1b", g)
                    left_by_store(pool, "x1", g)
                    nc.gpsimd.tensor_tensor(buf("x1", g)[:, :, :], buf("y1", g)[:, :, :], over_rows(buf("r1", g)), ALU.mult).then_inc(S["x1"], 1)
                if (g := group(i, 11)) is not None:
                    made(pool, "r2", g)
                    made(pool, "y2", g)
                    left_by_store(pool, "x2", g)
                    nc.gpsimd.tensor_tensor(buf("x2", g)[:, :, :], buf("y2", g)[:, :, :], over_rows(buf("r2", g)), ALU.mult).then_inc(S["x2"], 1)
            run(pool, step, 13)




def prepare_edges(nc, io, W, D):
    with Phase(nc) as m:
        dst_rows, next_rows, src_rows = (m.sb(n, [T, F], i32) for n in ("dst_rows", "next_rows", "src_rows"))
        next_f, src_f = m.sb("next_f", [T, F]), m.sb("src_f", [T, F])
        dst_f, end_keys_apart = m.sb("dst_f", [T, F]), m.sb("end_keys_apart", [HEADS, 2, T])
        node = m.sb("node", [125, N // 125], i32)
        attr = m.sb("attr", [F, T, RELATIONS])
        best, order, score = m.sb("best", [F, T]), m.sb("order", [F, RELATIONS]), m.sb("score", [F, T, RELATIONS])
        next_col, same_as_next, off = m.sb("next_col", [F, T]), m.sb("same_as_next", [F, T]), m.sb("off", [F, T])
        p_cols = m.pb("p_cols", [F, 3, F])
        s = m.named("rows_loaded attr_loaded attr_zeroed rows_converted cols_transposed dst_stored drow_loaded node_made node_stored "
                    "dst_col_full step_done")
        with nc.Block() as block:

            @block.sync
            def _(sp):
                for dst, src in ((dst_rows, io["dst"][0:SLOTS]), (next_rows, io["dst"][1:SLOTS + 1]), (src_rows, io["src"])):
                    sp.dma_start(dst[:, :], src.rearrange("(t e) -> t e", e=F)).then_inc(s["rows_loaded"], 16)
                sp.wait_ge(s["attr_zeroed"], 1)
                whole = E // F
                edges = io["edge_attr_42"][:, EMB:EMB + RELATIONS]
                sp.dma_start(attr[:, 0:whole, :], edges[0:whole * F, :].rearrange("(t e) r -> e t r", e=F),
                             allow_slow_non_contiguous=True).then_inc(s["attr_loaded"], 16)
                sp.dma_start(attr[0:E - whole * F, whole, :], edges[whole * F:E, :],
                             allow_slow_non_contiguous=True).then_inc(s["attr_loaded"], 16)
                sp.wait_ge(s["rows_converted"], 1)
                sp.dma_start(io["dst_f"].rearrange("(t e) -> t e", e=F), dst_f[:, :]).then_inc(s["dst_stored"], 16)
                sp.wait_ge(s["dst_stored"], 16)
                sp.dma_start(D["drow"][:, :], row_vector(io["dst_f"])).then_inc(s["drow_loaded"], 16)
                for end, c in enumerate((0, F - 1)):
                    edge_keys = io["dst_f"].rearrange("(t e) -> t e", e=F)[:, c:c + 1].rearrange("t a -> a t")
                    sp.dma_start(end_keys_apart[:, end, :], edge_keys.partition_broadcast(HEADS),
                                 allow_slow_non_contiguous=True).then_inc(s["drow_loaded"], 16)
                sp.wait_ge(s["node_made"], 1)
                sp.dma_start(io["row_of"].rearrange("(p n) a -> p (n a)", p=125), node[:, :]).then_inc(s["node_stored"], 16)
                sp.wait_ge(s["node_stored"], 16)
                sp.wait_ge(s["drow_loaded"], 48)

            @block.gpsimd
            def _(pool):
                pool.memset(attr[:, :, :], 0.0).then_inc(s["attr_zeroed"], 1)
                pool.iota(node[:, :], pattern=[[1, N // 125]], base=0, channel_multiplier=N // 125).then_inc(s["node_made"], 1)
                pool.iota(D["slot_row"][:, :], pattern=[[F, T]], base=N, channel_multiplier=1)
                pool.memset(D["link_key"][:, 0:1], -1.0)
                pool.memset(D["back_key"][:, T - 1:T], -1.0)
                pool.wait_ge(s["dst_col_full"], 1)
                pool.affine_select(out=D["link_key"][:, 1:T], in_=D["dst_col"][:, 0:T - 1], compare_op=ALU.is_equal, fill=-1.0,
                                   base=1 - F, pattern=[[0, T - 1]], channel_multiplier=1)
                pool.affine_select(out=D["back_key"][:, 0:T - 1], in_=D["dst_col"][:, 1:T], compare_op=ALU.is_equal, fill=-1.0,
                                   base=0, pattern=[[0, T - 1]], channel_multiplier=1)

            @block.tensor
            def _(pe):
                pe.wait_ge(s["rows_converted"], 3)
                for n, rows in enumerate((dst_f, next_f, src_f)):
                    last = nc.tensor.transpose(p_cols[:, n, 0:T], rows[:, :], W["ident"][0:T, 0:T])
                last.then_inc(s["cols_transposed"], 1)

            @block.vector
            def _(dve):
                done = 0

                def chained(ins):
                    nonlocal done
                    done += 1
                    ins.then_inc(s["step_done"], 1)
                    dve.wait_ge(s["step_done"], done)

                for r in range(RELATIONS):
                    chained(nc.vector.memset(order[:, r:r + 1], float(RELATIONS - r)))
                dve.wait_ge(s["rows_loaded"], 48)
                for f, i in ((dst_f, dst_rows), (next_f, next_rows), (src_f, src_rows)):
                    nc.vector.tensor_copy(f[:, :], i[:, :]).then_inc(s["rows_converted"], 1)
                dve.wait_ge(s["cols_transposed"], 1)
                nc.vector.tensor_copy(D["src_col"][:, :], p_cols[:, 2, 0:T])
                nc.vector.tensor_copy(D["dst_col"][:, :], p_cols[:, 0, 0:T]).then_inc(s["dst_col_full"], 1)
                dve.wait_ge(s["dst_col_full"], 1)
                chained(nc.vector.tensor_copy(next_col[:, :], p_cols[:, 1, 0:T]))
                chained(nc.vector.tensor_scalar(D["dst_read"][:, :], D["dst_col"][:, :], float(N - 1), None, ALU.min))
                chained(nc.vector.tensor_tensor(same_as_next[:, :], D["dst_col"][:, :], next_col[:, :], ALU.is_equal))
                chained(nc.vector.tensor_scalar(next_col[:, :], D["dst_col"][:, :], 1.0, None, ALU.add))
                chained(nc.vector.tensor_tensor(next_col[:, :], next_col[:, :], same_as_next[:, :], ALU.mult))
                chained(nc.vector.tensor_tensor(D["last_key"][:, :], D["dst_col"][:, :], next_col[:, :], ALU.subtract))
                chained(nc.vector.tensor_scalar(off[:, :], same_as_next[:, :], float(BEYOND), None, ALU.mult))
                chained(nc.vector.tensor_tensor(D["dst_write"][:, :], D["dst_col"][:, :], off[:, :], ALU.add))
                wide = lambda c: c[:, :].unsqueeze(2).to_broadcast([F, T, RELATIONS])
                dve.wait_ge(s["attr_loaded"], 32)
                chained(nc.vector.tensor_reduce(best[:, :], attr[:, :, :], AX.X, ALU.max))
                chained(nc.vector.tensor_tensor(score[:, :, :], attr[:, :, :], wide(best), ALU.is_equal))
                chained(nc.vector.tensor_tensor(score[:, :, :], score[:, :, :],
                                                order[:, :].unsqueeze(1).to_broadcast([F, T, RELATIONS]), ALU.mult))
                chained(nc.vector.tensor_reduce(best[:, :], score[:, :, :], AX.X, ALU.max))
                chained(nc.vector.tensor_tensor(D["relation"][:, :, :], score[:, :, :], wide(best), ALU.is_equal))
                dve.wait_ge(s["drow_loaded"], 48)
                chained(nc.vector.tensor_copy(D["end_keys"][:, :, :], end_keys_apart[:, :, :].rearrange("h s t -> h t s")))


def map_sources(nc, io, D):
    with Phase(nc) as m:
        index = [m.sb(f"index{u}", [F, 1], i32) for u in range(UNROLL)]
        value = [m.sb(f"value{u}", [F, 1], i32) for u in range(UNROLL)]
        moves = D["moves"]
        moved = moves.sems
        index_ready, value_ready, value_kept = m.sem("map_index_ready"), m.sem("map_value_ready"), m.sem("map_value_kept")
        taken = m.sem("waits_taken")
        with nc.Block() as block:

            @block.gpsimd
            def _(pool):
                def scatter(j, u):
                    wait(pool, moved[u], moves.after(j))
                    pool.tensor_copy(index[u][:, :], column(D["dst_write"], (j, u))).then_inc(index_ready, 1)
                    pool.tensor_copy(value[u][:, :], column(D["slot_row"], (j, u))).then_inc(value_ready, 1)
                    pool.wait_ge(index_ready, UNROLL * j + u + 1)
                    pool.wait_ge(value_ready, UNROLL * j + u + 1)
                    take_waits(pool, taken)
                    pool.indirect_dma_start(out=io["row_of"], out_offset=bass.IndirectOffsetOnAxis(ap=index[u][:, 0:1], axis=0),
                                            in_=value[u][:, :], in_offset=None, bounds_check=N - 1,
                                            oob_is_err=False).then_inc(moved[u], 16)
                over_all_tiles(pool, scatter, 0)

                for u in range(UNROLL):
                    pool.wait_ge(moved[u], moves.after(PASSES))

                def keep(ref):
                    j, u = ref
                    pool.wait_ge(moved[u], moves.after(j + PASSES + 1))
                    pool.tensor_copy(column(D["src_row"], ref), value[u][:, :]).then_inc(value_kept, 1)

                def gather(j, u):
                    if (ref := at(j, u, 3)) is not None:
                        keep(ref)
                    if (ref := at(j, u, 0)) is None:
                        return
                    wait(pool, value_kept, UNROLL * j + u - UNROLL + 1)
                    pool.tensor_copy(index[u][:, :], column(D["src_col"], (j, u))).then_inc(index_ready, 1)
                    pool.wait_ge(index_ready, T + UNROLL * j + u + 1)
                    take_waits(pool, taken)
                    pool.indirect_dma_start(out=value[u][:, :], out_offset=None, in_=io["row_of"],
                                            in_offset=bass.IndirectOffsetOnAxis(ap=index[u][:, 0:1], axis=0)).then_inc(moved[u], 16)
                over_all_tiles(pool, gather, 3)
        moves.passes += 2 * PASSES


def gather_rows(pool, taken, table, index_of, index, index_ready, rows, gathered, rows_used, j, u):
    wait(pool, rows_used, UNROLL * j + u - UNROLL + 1)
    wait(pool, gathered.sems[u], gathered.after(j))
    pool.tensor_copy(index[u][:, :], column(index_of, (j, u))).then_inc(index_ready, 1)
    pool.wait_ge(index_ready, UNROLL * j + u + 1)
    take_waits(pool, taken)
    pool.indirect_dma_start(out=rows[u][:, :], out_offset=None, in_=table,
                            in_offset=bass.IndirectOffsetOnAxis(ap=index[u][:, 0:1], axis=0)).then_inc(gathered.sems[u], 16)


def attention_messages(nc, io, W, D):
    with Phase(nc) as m:
        index, index_d = ([m.sb(f"{n}{u}", [F, 1], i32) for u in range(UNROLL)] for n in ("index_s", "index_d"))
        xs, xd = ([m.sb(f"{n}{u}", [F, F]) for u in range(UNROLL)] for n in ("xs", "xd"))
        xT = [m.sb(f"xT{u}", [F, 2, F]) for u in range(2)]
        qk = [m.sb(f"qk{u}", [F, 2, F]) for u in range(2)]
        prod = m.sb("prod", [F, F])
        p_xT = [m.pb(f"p_xT{u}", [F, 2, F]) for u in range(2)]
        p_qkvy = [m.pb(f"p_qkvy{u}", [F, 4, F]) for u in range(2)]
        got_s, got_d = D["moves"], D["dst_moves"]
        s = m.named("waits_taken xs_index_ready xd_index_ready xT_transposed xT_full qkvy_full qk_full v_kept y_kept prod_full scores_full")
        with nc.Block() as block:

            @block.gpsimd
            def _(pool):
                def step(j, u):
                    gather_rows(pool, s["waits_taken"], io["x"], D["src_col"], index, s["xs_index_ready"], xs, got_s, s["xT_transposed"], j, u)
                    gather_rows(pool, s["waits_taken"], io["x"], D["dst_read"], index_d, s["xd_index_ready"], xd, got_d, s["xT_transposed"], j, u)
                over_all_tiles(pool, step, 0)

            @block.tensor
            def _(pe):
                def step(j, u):
                    if (ref := at(j, u, 0)) is not None:
                        t = tile(ref)
                        pe.wait_ge(got_s.sems[u], got_s.after(j + 1))
                        pe.wait_ge(got_d.sems[u], got_d.after(j + 1))
                        wait(pe, s["xT_full"], t - 1)
                        nc.tensor.transpose(p_xT[u % 2][:, 0, :], xs[u][:, :], W["ident"][:, :])
                        nc.tensor.transpose(p_xT[u % 2][:, 1, :], xd[u][:, :], W["ident"][:, :]).then_inc(s["xT_transposed"], 1)
                    if (ref := at(j, u, 1)) is not None:
                        t, v = tile(ref), ref[1] % 2
                        pe.wait_ge(s["xT_full"], t + 1)
                        wait(pe, s["qk_full"], t - 1)
                        wait(pe, s["v_kept"], t - 1)
                        wait(pe, s["y_kept"], t - 1)
                        nc.tensor.matmul(p_qkvy[v][:, 1:3, :], xT[v][:, 0, :], W["Wkv"][:, :, :], start=True, stop=True)
                        nc.tensor.matmul(p_qkvy[v][:, 0, :], xT[v][:, 1, :], W["Wq"][:, :], start=True, stop=True)
                        nc.tensor.matmul(p_qkvy[v][:, 3, :], xT[v][:, 1, :], W["Wsc"][:, :], start=True, stop=True).then_inc(s["qkvy_full"], 1)
                over_all_tiles(pe, step, 1)

            @block.scalar
            def _(act):
                def step(j, u):
                    t = UNROLL * j + u
                    act.wait_ge(s["xT_transposed"], t + 1)
                    wait(act, s["qkvy_full"], t - 1)
                    nc.scalar.copy(xT[u % 2][:, :, :], p_xT[u % 2][:, 0:2, :]).then_inc(s["xT_full"], 1)
                over_all_tiles(act, step, 0)

            @block.vector
            def _(dve):
                def step(j, u):
                    t, v = UNROLL * j + u, u % 2
                    dve.wait_ge(s["qkvy_full"], t + 1)
                    wait(dve, s["prod_full"], t - 1)
                    nc.vector.tensor_tensor(qk[v][:, :, :], p_qkvy[v][:, 0:2, :], W["bqk"][:, :, :], ALU.add).then_inc(s["qk_full"], 1)
                    nc.vector.tensor_tensor(plane(D["R"], (j, u), 0, F), p_qkvy[v][:, 2, :], W["bv"][:, :], ALU.add).then_inc(s["v_kept"], 1)
                    nc.vector.tensor_tensor(plane(D["Y"], (j, u), 0, F), p_qkvy[v][:, 3, :], W["bsc"][:, :], ALU.add).then_inc(s["y_kept"], 1)
                    dve.wait_ge(s["qk_full"], t + 1)
                    wait(dve, s["scores_full"], t)
                    nc.vector.tensor_tensor(prod[:, :], qk[v][:, 0, :], qk[v][:, 1, :], ALU.mult).then_inc(s["prod_full"], 1)
                    dve.wait_ge(s["prod_full"], t + 1)
                    nc.vector.tensor_reduce(plane(D["scores"], (j, u), 0, HEADS), prod[:, :].rearrange("p (h d) -> p h d", h=HEADS),
                                            AX.X, ALU.add).then_inc(s["scores_full"], 1)
                over_all_tiles(dve, step, 0)
        got_s.passes += PASSES
        got_d.passes += PASSES


def weights_of_edges(nc, io, W, D, scale):
    P = BLOCK * HEADS
    with Phase(nc) as m:
        top, keys = m.sb("top", [P, BLOCKS, F]), m.sb("keys", [P, BLOCKS, F])
        fresh = m.sb("fresh", [P, BLOCKS * F + 1])
        off_first, off_last = fresh[:, 0:BLOCKS * F].rearrange("p (b e) -> p b e", e=F), keys
        keys8 = m.sb("keys8", [F, T, HEADS])
        ends, ends_out = m.sb("max_ends", [P, BLOCKS, 2]), m.sb("max_ends_out", [P, BLOCKS, 2])
        row = m.sb("row", [HEADS, 2 * T])
        row_fresh = m.sb("row_fresh", [HEADS, 2 * T + 1])
        p_sT, p_kT = m.pb("p_sT", [F, 12, F]), m.pb("p_kT", [F, 12, F])
        p_back = [m.pb(f"p_back{n}", [F, 512]) for n in range(2)]
        s = m.named("keys8_full scores_transposed keys_transposed step_done ends_ready ends_stored row_loaded row_ready row_stored "
                    "ends_loaded top_ready top_back shifted weights_ready")
        half = BLOCKS // 2
        with nc.Block() as block:

            @block.tensor
            def _(pe):
                pe.wait_ge(s["keys8_full"], 1)
                for src, out, done in ((D["scores"], p_sT, "scores_transposed"), (keys8, p_kT, "keys_transposed")):
                    for b in range(BLOCKS):
                        part = src[:, b * BLOCK:(b + 1) * BLOCK, :].rearrange("p t h -> p (t h)")
                        last = nc.tensor.transpose(out[0:P, b, :], part, W["ident"][:, :])
                    last.then_inc(s[done], 1)
                pe.wait_ge(s["top_ready"], 1)
                for b in range(BLOCKS):
                    at_ = (b % half) * P
                    last = nc.tensor.transpose(p_back[b // half][:, at_:at_ + P], top[:, b, :], W["ident"][0:P, 0:P])
                last.then_inc(s["top_back"], 1)

            @block.sync
            def _(sp):
                by_block = io["max_ends"].rearrange("(b p s) -> p b s", b=BLOCKS, s=2)
                by_head = io["max_ends"].rearrange("(t h s) -> h t s", h=HEADS, s=2)
                by_head2 = io["max_ends_out"].rearrange("(t h s) -> h t s", h=HEADS, s=2)
                by_block2 = io["max_ends_out"].rearrange("(b p s) -> p b s", b=BLOCKS, s=2)
                sp.wait_ge(s["ends_ready"], 2)
                sp.dma_start(by_block, ends[:, :, :]).then_inc(s["ends_stored"], 16)
                sp.wait_ge(s["ends_stored"], 16)
                sp.dma_start(row[:, :].rearrange("h (t s) -> h t s", s=2), by_head).then_inc(s["row_loaded"], 16)
                sp.wait_ge(s["row_ready"], 1)
                sp.dma_start(by_head2, row[:, :].rearrange("h (t s) -> h t s", s=2)).then_inc(s["row_stored"], 16)
                sp.wait_ge(s["row_stored"], 16)
                sp.dma_start(ends_out[:, :, :], by_block2).then_inc(s["ends_loaded"], 16)

            @block.vector
            def _(dve):
                done = 0

                def chained(ins):
                    nonlocal done
                    done += 1
                    ins.then_inc(s["step_done"], 1)
                    dve.wait_ge(s["step_done"], done)

                nc.vector.tensor_copy(keys8[:, :, :], D["dst_col"][:, :].unsqueeze(2).to_broadcast([F, T, HEADS])).then_inc(s["keys8_full"], 1)
                row_keys = D["end_keys"][:, :, :].rearrange("h t s -> h (t s)")
                chained(nc.vector.memset(row_fresh[:, :], 0.0))
                chained(nc.vector.tensor_tensor(row_fresh[:, 1:2 * T], row_keys[:, 1:2 * T], row_keys[:, 0:2 * T - 1], ALU.is_equal))
                chained(nc.vector.tensor_scalar(row_fresh[:, :], row_fresh[:, :], -1.0, FAR, ALU.add, ALU.mult))
                dve.wait_ge(s["keys_transposed"], 1)
                chained(nc.vector.tensor_copy(keys[:, :, :], p_kT[0:P, 0:BLOCKS, :]))
                flat = lambda t: t[:, :, :].rearrange("p b e -> p (b e)")
                W_ = BLOCKS * F
                chained(nc.vector.memset(fresh[:, :], 0.0))
                chained(nc.vector.tensor_tensor(fresh[:, 1:W_], flat(keys)[:, 1:W_], flat(keys)[:, 0:W_ - 1], ALU.is_equal))
                chained(nc.vector.memset(fresh[:, 0:W_].rearrange("p (b e) -> p b e", e=F)[:, :, 0:1], 0.0))
                chained(nc.vector.tensor_scalar(fresh[:, :], fresh[:, :], -1.0, FAR, ALU.add, ALU.mult))
                dve.wait_ge(s["scores_transposed"], 1)
                chained(nc.vector.tensor_tensor_scan(flat(top), fresh[:, 0:W_], p_sT[0:P, 0:BLOCKS, :].rearrange("p b e -> p (b e)"),
                                                     -FAR, ALU.add, ALU.max))
                chained(nc.vector.tensor_tensor_scan(flat(top)[:, ::-1], fresh[:, 1:W_ + 1][:, ::-1], flat(top)[:, ::-1], -FAR, ALU.add, ALU.max))
                nc.vector.tensor_copy(ends[:, :, 0:1], top[:, :, 0:1]).then_inc(s["ends_ready"], 1)
                nc.vector.tensor_copy(ends[:, :, 1:2], top[:, :, F - 1:F]).then_inc(s["ends_ready"], 1)
                for out, e in ((off_first, 0), (off_last, F - 1)):
                    chained(nc.vector.tensor_tensor(out[:, :, :], keys[:, :, :], keys[:, :, e:e + 1].to_broadcast([P, BLOCKS, F]), ALU.is_equal))
                    chained(nc.vector.tensor_scalar(out[:, :, :], out[:, :, :], -1.0, FAR, ALU.add, ALU.mult))
                dve.wait_ge(s["row_loaded"], 16)
                chained(nc.vector.tensor_tensor_scan(row[:, :], row_fresh[:, 0:2 * T], row[:, :], -FAR, ALU.add, ALU.max))
                nc.vector.tensor_tensor_scan(row[:, ::-1], row_fresh[:, 1:2 * T + 1][:, ::-1], row[:, ::-1], -FAR,
                                             ALU.add, ALU.max).then_inc(s["row_ready"], 1)
                dve.wait_ge(s["ends_loaded"], 16)
                for off, n in ((off_first, 0), (off_last, 1)):
                    chained(nc.vector.tensor_tensor(off[:, :, :], off[:, :, :], ends_out[:, :, n:n + 1].to_broadcast([P, BLOCKS, F]), ALU.add))
                    chained(nc.vector.tensor_tensor(top[:, :, :], top[:, :, :], off[:, :, :], ALU.max))
                nc.vector.tensor_copy(ends[:, :, 0:1], top[:, :, 0:1]).then_inc(s["top_ready"], 1)
                dve.wait_ge(s["top_back"], 1)
                for n in range(2):
                    part = D["scores"][:, n * T // 2:(n + 1) * T // 2, :].rearrange("p t h -> p (t h)")
                    nc.vector.tensor_tensor(part, part, p_back[n][:, 0:half * P], ALU.subtract).then_inc(s["shifted"], 1)

            @block.scalar
            def _(act):
                act.wait_ge(s["shifted"], 2)
                act.activation(D["scores"][:, :, :], D["scores"][:, :, :], ACT.Exp, scale=scale).then_inc(s["weights_ready"], 1)


def same_and_link(dve, nc, D, same, link, used, s, ref):
    t, v = tile(ref), ref[1] % 2
    keys = D["drow"][:, bass.ds(t * F, F)]
    wait(dve, used, t - 1)
    nc.vector.tensor_scalar(same[v][:, :], keys, column(D["dst_col"], ref), None, ALU.is_equal).then_inc(s["same_full"], 1)
    nc.vector.tensor_scalar(link[v][:, :], keys, column(D["link_key"], ref), None, ALU.is_equal).then_inc(s["link_full"], 1)


def sum_to_here(pe, nc, p_sum, same, link, parts, whole, width, s, ref):
    t, v = tile(ref), ref[1] % 2
    pe.wait_ge(s["same_full"], t + 1)
    pe.wait_ge(s["link_full"], t + 1)
    wait(pe, s["whole_full"], t)
    first = isinstance(t, int) and t == 0
    for c, values in parts:
        w = values.shape[-1]
        last = nc.tensor.matmul(p_sum[v][:, c:c + w], same[v][:, :], values, start=True, stop=first)
        if not first:
            last = nc.tensor.matmul(p_sum[v][:, c:c + w], link[v][:, :], whole[1 - v][:, c:c + w], start=False, stop=True)
    last.then_inc(s["summed"], 1)


SUMS = "same_full link_full summed whole_full "
NORM = "norm_waits_taken stats_full moments_full dev_full inverse_dev_full normal_full "


def sum_memory(m, width):
    two = lambda name, w: [m.sb(f"{name}{u}", [F, w]) for u in range(2)]
    return two("same", F), two("link", F), two("whole", width), [m.pb(f"p_sum{u}", [F, 512]) for u in range(2)]


class Norm:

    def __init__(self, nc, m, W, s):
        self.nc, self.W, self.s = nc, W, s
        self.stats, self.moments, self.dev, self.inverse = (
            [m.sb(f"norm_{n}{u}", [F, w]) for u in range(copies)] for n, w, copies in
            (("stats", 6, 2), ("moments", 2, UNROLL), ("dev", 1, 2), ("inverse", 1, 2)))

    def statistics(self, dve, y, ready, ref):
        t, v = tile(ref), ref[1] % 2
        dve.wait_ge(ready, t + 1)
        wait(dve, self.s["moments_full"], t - 1)
        self.nc.vector.bn_stats(self.stats[v][:, :], y).then_inc(self.s["stats_full"], 1)

    def aggregate(self, dve, ref):
        t, v = tile(ref), ref[1] % 2
        dve.wait_ge(self.s["stats_full"], t + 1)
        wait(dve, self.s["normal_full"], t - 3)
        take_waits(dve, self.s["norm_waits_taken"])
        self.nc.vector.bn_aggr(self.moments[ref[1]][:, :], self.stats[v][:, :]).then_inc(self.s["moments_full"], 1)

    def deviation(self, act, ref):
        s, t, v = self.s, tile(ref), ref[1] % 2
        act.wait_ge(s["moments_full"], t + 1)
        wait(act, s["inverse_dev_full"], t - 1)
        self.nc.scalar.activation(self.dev[v][:, :], self.moments[ref[1]][:, 1:2], ACT.Sqrt, bias=self.W["eps"][:, :]).then_inc(s["dev_full"], 1)

    def inverse_of(self, dve, ref):
        s, t, v = self.s, tile(ref), ref[1] % 2
        dve.wait_ge(s["dev_full"], t + 1)
        wait(dve, s["normal_full"], t - 1)
        self.nc.vector.reciprocal(self.inverse[v][:, :], self.dev[v][:, :]).then_inc(s["inverse_dev_full"], 1)

    def apply(self, dve, out, y, ref):
        s, t, v = self.s, tile(ref), ref[1] % 2
        dve.wait_ge(s["inverse_dev_full"], t + 1)
        self.nc.vector.tensor_scalar(out, y, self.moments[ref[1]][:, 0:1], self.inverse[v][:, 0:1], ALU.subtract, ALU.mult).then_inc(s["normal_full"], 1)

    def moments_of(self, dve, y, ready, ref):
        self.statistics(dve, y, ready, ref)
        self.aggregate(dve, ref)

    def rows_of(self, dve, out, y, ref):
        self.inverse_of(dve, ref)
        self.apply(dve, out, y, ref)


def store_slots(sp, table, src, ready, stored):
    for b in range(BLOCKS):
        sp.wait_ge(ready, BLOCK * (b + 1))
        a = N + b * BLOCK * F
        sp.dma_start(table[a:a + BLOCK * F, :].rearrange("(t p) f -> p t f", p=F), src[:, b * BLOCK:(b + 1) * BLOCK, :]).then_inc(stored, 16)
    sp.wait_ge(stored, 16 * BLOCKS)


def weighted(pool, nc, D, message, heads, s, ref):
    t, v = tile(ref), ref[1] % 2
    by_head = lambda a: a.rearrange("p (h d) -> p h d", h=heads)
    wait(pool, s["summed"], t - 1)
    nc.gpsimd.tensor_tensor(by_head(message[v][:, :]), by_head(plane(D["R"], ref, 0, F)),
                            plane(D["scores"], ref, 0, heads).unsqueeze(2).to_broadcast([F, heads, F // heads]),
                            ALU.mult).then_inc(s["weighted"], 1)


def attention_rows(nc, io, W, D):
    width = F + HEADS + RELATIONS
    with Phase(nc) as m:
        same, link, whole, p_sum = sum_memory(m, width)
        message, y = ([m.sb(f"{n}{u}", [F, F]) for u in range(2)] for n in ("message", "y"))
        inverse, mean = m.sb("inverse", [F, HEADS]), [m.sb(f"mean_value{u}", [F, F]) for u in range(2)]
        deg, root = ([m.sb(f"{n}{u}", [F, 1]) for u in range(2)] for n in ("deg", "root"))
        s = m.named(SUMS + NORM + "weighted inverse_full mean_full y_full deg_full root_full dinv_full count_kept scaled_full stored")
        norm = Norm(nc, m, W, s)
        by_head = lambda a: a.rearrange("p (h d) -> p h d", h=HEADS)
        with nc.Block() as block:

            @block.gpsimd
            def _(pool):
                def step(j, u):
                    if (ref := at(j, u, 0)) is not None:
                        weighted(pool, nc, D, message, HEADS, s, ref)
                    if (ref := at(j, u, 2)) is not None:
                        t, v = tile(ref), ref[1] % 2
                        pool.wait_ge(s["mean_full"], t + 1)
                        wait(pool, s["normal_full"], t - 1)
                        pool.tensor_tensor(y[v][:, :], plane(D["Y"], ref, 0, F), mean[v][:, :], ALU.add).then_inc(s["y_full"], 1)
                over_all_tiles(pool, step, 2)

            @block.tensor
            def _(pe):
                def step(j, u):
                    ref, v = (j, u), u % 2
                    pe.wait_ge(s["weighted"], tile(ref) + 1)
                    sum_to_here(pe, nc, p_sum, same, link, ((0, message[v][:, :]), (F, plane(D["scores"], ref, 0, HEADS)),
                                                            (F + HEADS, plane(D["relation"], ref, 0, RELATIONS))), whole, width, s, ref)
                over_all_tiles(pe, step, 0)

            @block.scalar
            def _(act):
                def step(j, u):
                    if (ref := at(j, u, 3)) is not None:
                        norm.deviation(act, ref)
                    if (ref := at(j, u, 4)) is not None:
                        t = tile(ref)
                        act.wait_ge(s["normal_full"], t + 1)
                        act.wait_ge(s["dinv_full"], t + 1)
                        act.activation(plane(D["R"], ref, 0, F), plane(D["Y"], ref, 0, F), ACT.Copy, scale=column(D["dinv"], ref)).then_inc(s["scaled_full"], 1)
                    if (ref := at(j, u, 1)) is not None:
                        t, v = tile(ref), ref[1] % 2
                        act.wait_ge(s["deg_full"], t + 1)
                        wait(act, s["dinv_full"], t - 1)
                        act.activation(root[v][:, :], deg[v][:, :], ACT.Sqrt, bias=W["one"][:, :]).then_inc(s["root_full"], 1)
                    if (ref := at(j, u, 0)) is not None:
                        t, v = tile(ref), ref[1] % 2
                        act.wait_ge(s["summed"], t + 1)
                        wait(act, s["mean_full"], t - 1)
                        wait(act, s["deg_full"], t - 1)
                        act.copy(whole[v][:, :], p_sum[v][:, 0:width]).then_inc(s["whole_full"], 1)
                        act.wait_ge(s["whole_full"], t + 1)
                        act.copy(plane(D["count"], ref, 0, RELATIONS), whole[v][:, F + HEADS:width]).then_inc(s["count_kept"], 1)
                over_all_tiles(act, step, 4)

            @block.vector
            def _(dve):
                def step(j, u):
                    if (ref := at(j, u, 0)) is not None:
                        same_and_link(dve, nc, D, same, link, s["summed"], s, ref)
                    if (ref := at(j, u, 1)) is not None:
                        t, v = tile(ref), ref[1] % 2
                        dve.wait_ge(s["whole_full"], t + 1)
                        wait(dve, s["root_full"], t - 1)
                        nc.vector.tensor_reduce(deg[v][:, :], whole[v][:, F + HEADS:width], AX.X, ALU.add).then_inc(s["deg_full"], 1)
                        wait(dve, s["mean_full"], t)
                        nc.vector.reciprocal(inverse[:, :], whole[v][:, F:F + HEADS]).then_inc(s["inverse_full"], 1)
                        dve.wait_ge(s["inverse_full"], t + 1)
                        wait(dve, s["y_full"], t - 1)
                        nc.vector.tensor_tensor(by_head(mean[v][:, :]), by_head(whole[v][:, 0:F]),
                                                inverse[:, :].unsqueeze(2).to_broadcast([F, HEADS, F // HEADS]), ALU.mult).then_inc(s["mean_full"], 1)
                    if (ref := at(j, u, 2)) is not None:
                        t, v = tile(ref), ref[1] % 2
                        dve.wait_ge(s["root_full"], t + 1)
                        nc.vector.reciprocal(column(D["dinv"], ref), root[v][:, :]).then_inc(s["dinv_full"], 1)
                    if (ref := at(j, u, 3)) is not None:
                        norm.moments_of(dve, y[ref[1] % 2][:, :], s["y_full"], ref)
                    if (ref := at(j, u, 4)) is not None:
                        norm.rows_of(dve, plane(D["Y"], ref, 0, F), y[ref[1] % 2][:, :], ref)
                over_all_tiles(dve, step, 4)

            @block.sync
            def _(sp):
                store_slots(sp, io["Z1"], D["R"], s["scaled_full"], s["stored"])


def hidden_rows(nc, io, W, D):
    with Phase(nc) as m:
        same, link, whole, p_sum = sum_memory(m, F)
        rows, index = [m.sb(f"rows{u}", [F, F]) for u in range(UNROLL)], [m.sb(f"index{u}", [F, 1], i32) for u in range(UNROLL)]
        mid, inner, innerT = m.sb("mid", [F, F]), *([m.sb(f"{n}{u}", [F, F]) for u in range(2)] for n in ("inner", "innerT"))
        gT = [m.sb(f"gT{u}", [F, 2, F]) for u in range(2)]
        p_T = [m.pb(f"p_T{u}", [F, 512]) for u in range(2)]
        p_g = [m.pb(f"p_g{u}", [F, 4, F]) for u in range(2)]
        p_out = [m.pb(f"p_out{u}", [F, 512]) for u in range(2)]
        gathered = D["moves"]
        s = m.named(SUMS + "waits_taken index_ready mid_full inner_full inner_transposed innerT_full g_multiplied gT_full "
                    "out_multiplied z_full y_full y_biased stored")
        with nc.Block() as block:

            @block.gpsimd
            def _(pool):
                def step(j, u):
                    if (ref := at(j, u, 0)) is not None:
                        gather_rows(pool, s["waits_taken"], io["Z1"], D["src_row"], index, s["index_ready"], rows, gathered, s["summed"], j, u)
                    if (ref := at(j, u, 4)) is not None:
                        pool.wait_ge(s["mid_full"], tile(ref) + 1)
                        y = plane(D["Y"], ref, 0, F)
                        pool.tensor_tensor(y, y, W["b2c"][:, :], ALU.add).then_inc(s["y_biased"], 1)
                over_all_tiles(pool, step, 4)

            @block.tensor
            def _(pe):
                def step(j, u):
                    if (ref := at(j, u, 3)) is not None:
                        t, v = tile(ref), ref[1] % 2
                        pe.wait_ge(s["gT_full"], t + 1)
                        wait(pe, s["z_full"], t - 1)
                        for k in range(2):
                            last = nc.tensor.matmul(p_out[v][:, 0:F], gT[v][:, k, :], W["W2c"][:, k, :], start=(k == 0), stop=(k == 1))
                        last.then_inc(s["out_multiplied"], 1)
                    if (ref := at(j, u, 2)) is not None:
                        t, v = tile(ref), ref[1] % 2
                        pe.wait_ge(s["innerT_full"], t + 1)
                        wait(pe, s["gT_full"], t - 1)
                        for k in range(2):
                            last = nc.tensor.matmul(p_g[v][:, k, :], W["W1"][:, k * F:(k + 1) * F], innerT[v][:, :], start=True, stop=True)
                        last.then_inc(s["g_multiplied"], 1)
                    if (ref := at(j, u, 1)) is not None:
                        t, v = tile(ref), ref[1] % 2
                        pe.wait_ge(s["inner_full"], t + 1)
                        wait(pe, s["innerT_full"], t - 1)
                        nc.tensor.transpose(p_T[v][:, 0:F], inner[v][:, :], W["ident"][:, :]).then_inc(s["inner_transposed"], 1)
                    if (ref := at(j, u, 0)) is not None:
                        pe.wait_ge(gathered.sems[u], gathered.after(j + 1))
                        sum_to_here(pe, nc, p_sum, same, link, ((0, rows[u][:, :]),), whole, F, s, ref)
                over_all_tiles(pe, step, 3)

            @block.scalar
            def _(act):
                def step(j, u):
                    if (ref := at(j, u, 2)) is not None:
                        t, v = tile(ref), ref[1] % 2
                        act.wait_ge(s["g_multiplied"], t + 1)
                        wait(act, s["out_multiplied"], t - 1)
                        for k in range(2):
                            last = act.activation(gT[v][:, k, :], p_g[v][:, k, :], ACT.Relu, bias=W["b_W1"][:, k:k + 1])
                        last.then_inc(s["gT_full"], 1)
                    if (ref := at(j, u, 1)) is not None:
                        t, v = tile(ref), ref[1] % 2
                        act.wait_ge(s["inner_transposed"], t + 1)
                        wait(act, s["g_multiplied"], t - 1)
                        act.copy(innerT[v][:, :], p_T[v][:, 0:F]).then_inc(s["innerT_full"], 1)
                    if (ref := at(j, u, 0)) is not None:
                        t, v = tile(ref), ref[1] % 2
                        act.wait_ge(s["summed"], t + 1)
                        wait(act, s["mid_full"], t - 1)
                        act.copy(whole[v][:, :], p_sum[v][:, 0:F]).then_inc(s["whole_full"], 1)
                over_all_tiles(act, step, 2)

            @block.vector
            def _(dve):
                def step(j, u):
                    if (ref := at(j, u, 0)) is not None:
                        same_and_link(dve, nc, D, same, link, s["summed"], s, ref)
                    if (ref := at(j, u, 3)) is not None:
                        t, v = tile(ref), ref[1] % 2
                        y, z, dinv = plane(D["Y"], ref, 0, F), plane(D["R"], ref, 0, F), column(D["dinv"], ref)
                        dve.wait_ge(s["out_multiplied"], t + 1)
                        nc.vector.tensor_scalar(z, p_out[v][:, 0:F], dinv, None, ALU.mult).then_inc(s["z_full"], 1)
                        dve.wait_ge(s["z_full"], t + 1)
                        dve.wait_ge(s["y_biased"], t + 1)
                        nc.vector.scalar_tensor_tensor(out=y, in0=z, scalar=dinv, in1=y, op0=ALU.mult, op1=ALU.add).then_inc(s["y_full"], 1)
                    if (ref := at(j, u, 1)) is not None:
                        t, v = tile(ref), ref[1] % 2
                        dinv = column(D["dinv"], ref)
                        dve.wait_ge(s["whole_full"], t + 1)
                        wait(dve, s["inner_full"], t)
                        nc.vector.scalar_tensor_tensor(out=mid[:, :], in0=plane(D["Y"], ref, 0, F), scalar=dinv, in1=whole[v][:, :],
                                                       op0=ALU.mult, op1=ALU.add).then_inc(s["mid_full"], 1)
                        dve.wait_ge(s["mid_full"], t + 1)
                        wait(dve, s["inner_transposed"], t - 1)
                        nc.vector.tensor_scalar(inner[v][:, :], mid[:, :], dinv, None, ALU.mult).then_inc(s["inner_full"], 1)
                over_all_tiles(dve, step, 3)

            @block.sync
            def _(sp):
                store_slots(sp, io["H2"], D["R"], s["z_full"], s["stored"])
        gathered.passes += PASSES


def output_rows(nc, io, W, D):
    with Phase(nc) as m:
        same, link, whole, p_sum = sum_memory(m, F)
        rows, index = [m.sb(f"rows{u}", [F, F]) for u in range(UNROLL)], [m.sb(f"index{u}", [F, 1], i32) for u in range(UNROLL)]
        y = [m.sb(f"y{u}", [F, F]) for u in range(2)]
        gathered = D["moves"]
        s = m.named(SUMS + NORM + "waits_taken index_ready y_full stored")
        norm = Norm(nc, m, W, s)
        with nc.Block() as block:

            @block.gpsimd
            def _(pool):
                over_all_tiles(pool, lambda j, u: gather_rows(pool, s["waits_taken"], io["H2"], D["src_row"], index, s["index_ready"], rows,
                                                              gathered, s["summed"], j, u), 0)

            @block.tensor
            def _(pe):
                def step(j, u):
                    pe.wait_ge(gathered.sems[u], gathered.after(j + 1))
                    sum_to_here(pe, nc, p_sum, same, link, ((0, rows[u][:, :]),), whole, F, s, (j, u))
                over_all_tiles(pe, step, 0)

            @block.scalar
            def _(act):
                def step(j, u):
                    if (ref := at(j, u, 1)) is not None:
                        norm.deviation(act, ref)
                    if (ref := at(j, u, 0)) is not None:
                        t, v = tile(ref), ref[1] % 2
                        act.wait_ge(s["summed"], t + 1)
                        wait(act, s["y_full"], t - 1)
                        act.copy(whole[v][:, :], p_sum[v][:, 0:F]).then_inc(s["whole_full"], 1)
                over_all_tiles(act, step, 1)

            @block.vector
            def _(dve):
                def step(j, u):
                    if (ref := at(j, u, 0)) is not None:
                        same_and_link(dve, nc, D, same, link, s["summed"], s, ref)
                    if (ref := at(j, u, 1)) is not None:
                        t, v = tile(ref), ref[1] % 2
                        dve.wait_ge(s["whole_full"], t + 1)
                        wait(dve, s["normal_full"], t - 1)
                        nc.vector.scalar_tensor_tensor(out=y[v][:, :], in0=whole[v][:, :], scalar=column(D["dinv"], ref), in1=plane(D["Y"], ref, 0, F),
                                                       op0=ALU.mult, op1=ALU.add).then_inc(s["y_full"], 1)
                        norm.moments_of(dve, y[v][:, :], s["y_full"], ref)
                    if (ref := at(j, u, 2)) is not None:
                        norm.rows_of(dve, plane(D["Y"], ref, 0, F), y[ref[1] % 2][:, :], ref)
                over_all_tiles(dve, step, 2)

            @block.sync
            def _(sp):
                store_slots(sp, io["X2"], D["Y"], s["normal_full"], s["stored"])
        gathered.passes += PASSES


def mirrored(ref):
    j, u = ref
    return (PASSES - 1) - j, UNROLL - 1 - u


def gat_messages(nc, io, W, D):
    H4 = GAT_HEADS
    w = H4 + RELATIONS
    with Phase(nc) as m:
        index = [m.sb(f"index{u}", [F, 1], i32) for u in range(UNROLL)]
        rows = [m.sb(f"rows{u}", [F, F]) for u in range(UNROLL)]
        own = [m.sb(f"own{u}", [F, F]) for u in range(2)]
        bothT = [m.sb(f"bothT{u}", [F, 2, F]) for u in range(2)]
        last, after = ([m.sb(f"{n}{u}", [F, F]) for u in range(2)] for n in ("last", "after"))
        held, spread = ([m.sb(f"{n}{u}", [F, w]) for u in range(2)] for n in ("held", "spread"))
        raw, at_least_one, inverse = m.sb("raw", [F, H4]), m.sb("at_least_one", [F, RELATIONS]), m.sb("inverse", [F, RELATIONS])
        p_T = [m.pb(f"p_T{u}", [F, 4, F]) for u in range(2)]
        p_h = [m.pb(f"p_h{u}", [F, 512]) for u in range(2)]
        p_spread = [m.pb(f"p_spread{u}", [F, 512]) for u in range(2)]
        gathered = D["moves"]
        s = m.named("waits_taken dve_waits_taken index_ready own_full transposed bothT_full multiplied h_kept counts_held scores_held last_full after_full "
                    "spread_multiplied spread_full raw_full scores_full at_least_one_full inverse_full share_full twice")
        with nc.Block() as block:

            @block.gpsimd
            def _(pool):
                def step(j, u):
                    wait(pool, s["transposed"], UNROLL * j + u - UNROLL + 1)
                    wait(pool, gathered.sems[u], gathered.after(j))
                    take_waits(pool, s["waits_taken"])
                    pool.tensor_copy(index[u][:, :], column(D["src_row"], mirrored((j, u)))).then_inc(s["index_ready"], 1)
                    pool.wait_ge(s["index_ready"], UNROLL * j + u + 1)
                    take_waits(pool, s["waits_taken"])
                    pool.indirect_dma_start(out=rows[u][:, :], out_offset=None, in_=io["X2"],
                                            in_offset=bass.IndirectOffsetOnAxis(ap=index[u][:, 0:1], axis=0)).then_inc(gathered.sems[u], 16)
                over_all_tiles(pool, step, 0)

            @block.tensor
            def _(pe):
                def step(j, u):
                    if (ref := at(j, u, 0)) is not None:
                        t = tile(ref)
                        pe.wait_ge(gathered.sems[u], gathered.after(j + 1))
                        wait(pe, s["bothT_full"], t - 1)
                        nc.tensor.transpose(p_T[u % 2][:, 0, :], rows[u][:, :], W["ident"][:, :])
                        pe.wait_ge(s["own_full"], t + 1)
                        nc.tensor.transpose(p_T[u % 2][:, 1, :], own[u % 2][:, :], W["ident"][:, :]).then_inc(s["transposed"], 1)
                    if (ref := at(j, u, 1)) is not None:
                        t, v = tile(ref), ref[1] % 2
                        pe.wait_ge(s["bothT_full"], t + 1)
                        wait(pe, s["raw_full"], t - 1)
                        nc.tensor.matmul(p_h[v][:, 0:F], bothT[v][:, 0, :], W["Wgat"][:, :, :], start=True, stop=True)
                        nc.tensor.matmul(p_h[v][:, F:F + H4], bothT[v][:, 0, :], W["w_src"][:, :], start=True, stop=True)
                        nc.tensor.matmul(p_h[v][:, F + H4:F + 2 * H4], bothT[v][:, 1, :], W["w_dst"][:, :], start=True, stop=True).then_inc(s["multiplied"], 1)
                    if (ref := at(j, u, 2)) is not None:
                        t, v = tile(ref), ref[1] % 2
                        pe.wait_ge(s["counts_held"], t + 1)
                        pe.wait_ge(s["scores_held"], t + 1)
                        pe.wait_ge(s["last_full"], t + 1)
                        pe.wait_ge(s["after_full"], t + 1)
                        wait(pe, s["spread_full"], t)
                        first = isinstance(t, int) and t == 0
                        step_ = nc.tensor.matmul(p_spread[v][:, 0:w], last[v][:, :], held[v][:, :], start=True, stop=first)
                        if not first:
                            step_ = nc.tensor.matmul(p_spread[v][:, 0:w], after[v][:, :], spread[1 - v][:, :], start=False, stop=True)
                        step_.then_inc(s["spread_multiplied"], 1)
                over_all_tiles(pe, step, 2)

            @block.scalar
            def _(act):
                def step(j, u):
                    if (ref := at(j, u, 0)) is not None:
                        wait(act, s["transposed"], tile(ref) - 1)
                        act.copy(own[u % 2][:, :], plane(D["Y"], mirrored(ref), 0, F)).then_inc(s["own_full"], 1)
                    if (ref := at(j, u, 2)) is not None:
                        t, v = tile(ref), ref[1] % 2
                        act.wait_ge(s["spread_multiplied"], t + 1)
                        wait(act, s["raw_full"], t - 1)
                        wait(act, s["at_least_one_full"], t - 1)
                        act.copy(spread[v][:, :], p_spread[v][:, 0:w]).then_inc(s["spread_full"], 1)
                    if (ref := at(j, u, 1)) is not None:
                        t, v = tile(ref), ref[1] % 2
                        act.wait_ge(s["multiplied"], t + 1)
                        wait(act, s["spread_multiplied"], t - 1)
                        act.copy(held[v][:, 0:H4], p_h[v][:, F + H4:F + 2 * H4]).then_inc(s["scores_held"], 1)
                        act.copy(held[v][:, H4:w], plane(D["count"], mirrored(ref), 0, RELATIONS)).then_inc(s["counts_held"], 1)
                        act.copy(plane(D["R"], mirrored(ref), 0, F), p_h[v][:, 0:F]).then_inc(s["h_kept"], 1)
                    if (ref := at(j, u, 0)) is not None:
                        t = tile(ref)
                        act.wait_ge(s["transposed"], t + 1)
                        wait(act, s["multiplied"], t - 1)
                        act.copy(bothT[u % 2][:, :, :], p_T[u % 2][:, 0:2, :]).then_inc(s["bothT_full"], 1)
                over_all_tiles(act, step, 2)

            @block.vector
            def _(dve):
                def step(j, u):
                    if (ref := at(j, u, 1)) is not None:
                        t, v, tile_ = tile(ref), ref[1] % 2, mirrored(ref)
                        keys = D["drow"][:, bass.ds(tile(tile_) * F, F)]
                        wait(dve, s["spread_multiplied"], t - 1)
                        take_waits(dve, s["dve_waits_taken"])
                        nc.vector.tensor_scalar(last[v][:, :], keys, column(D["last_key"], tile_), None, ALU.is_equal).then_inc(s["last_full"], 1)
                        nc.vector.tensor_scalar(after[v][:, :], keys, column(D["back_key"], tile_), None, ALU.is_equal).then_inc(s["after_full"], 1)
                    if (ref := at(j, u, 3)) is not None:
                        t, v, tile_ = tile(ref), ref[1] % 2, mirrored(ref)
                        dve.wait_ge(s["spread_full"], t + 1)
                        dve.wait_ge(s["h_kept"], t + 1)
                        wait(dve, s["scores_full"], t)
                        nc.vector.tensor_tensor(raw[:, :], p_h[v][:, F:F + H4], spread[v][:, 0:H4], ALU.add).then_inc(s["raw_full"], 1)
                        dve.wait_ge(s["raw_full"], t + 1)
                        take_waits(dve, s["dve_waits_taken"])
                        nc.vector.scalar_tensor_tensor(out=plane(D["scores"], tile_, 0, H4), in0=raw[:, :], scalar=ALPHA, in1=raw[:, :],
                                                       op0=ALU.mult, op1=ALU.max).then_inc(s["scores_full"], 1)
                        wait(dve, s["inverse_full"], t)
                        nc.vector.tensor_scalar(at_least_one[:, :], spread[v][:, H4:w], 1.0, None, ALU.max).then_inc(s["at_least_one_full"], 1)
                        dve.wait_ge(s["at_least_one_full"], t + 1)
                        wait(dve, s["share_full"], t)
                        nc.vector.reciprocal(inverse[:, :], at_least_one[:, :]).then_inc(s["inverse_full"], 1)
                        dve.wait_ge(s["inverse_full"], t + 1)
                        take_waits(dve, s["dve_waits_taken"])
                        share = plane(D["relation"], tile_, 0, RELATIONS)
                        nc.vector.tensor_tensor(share, inverse[:, :], share, ALU.mult).then_inc(s["share_full"], 1)
                over_all_tiles(dve, step, 3)
                dve.wait_ge(s["scores_full"], T)
                nc.vector.tensor_copy(D["scores"][:, :, H4:HEADS], D["scores"][:, :, 0:H4]).then_inc(s["twice"], 1)
                dve.wait_ge(s["twice"], 1)
        gathered.passes += PASSES


def gat_rows(nc, io, W, D):
    H4 = GAT_HEADS
    width = F + H4
    with Phase(nc) as m:
        same, link, whole, p_sum = sum_memory(m, width)
        two = lambda name: [m.sb(f"{name}{u}", [F, F]) for u in range(2)]
        message, mean, low, grown, y, x3, x3T = (two(n) for n in ("message", "mean_h", "low", "grown", "y", "x3", "x3T"))
        inverse = m.sb("inverse", [F, H4])
        p_T = [m.pb(f"p_T{u}", [F, 512]) for u in range(2)]
        p_root = [m.pb(f"p_root{u}", [F, 512]) for u in range(2)]
        s = m.named(SUMS + NORM + "weighted inverse_full mean_full low_full grown_full high_full y_full x3_kept stored x3_transposed x3T_full "
                    "root_multiplied root_full root_stored")
        norm = Norm(nc, m, W, s)
        by_head = lambda a: a.rearrange("p (h d) -> p h d", h=H4)
        with nc.Block() as block:

            @block.gpsimd
            def _(pool):
                def step(j, u):
                    if (ref := at(j, u, 0)) is not None:
                        weighted(pool, nc, D, message, H4, s, ref)
                    if (ref := at(j, u, 4)) is not None:
                        t, v = tile(ref), ref[1] % 2
                        pool.wait_ge(s["normal_full"], t + 1)
                        pool.tensor_copy(plane(D["Y"], ref, 0, F), x3[v][:, :]).then_inc(s["x3_kept"], 1)
                over_all_tiles(pool, step, 4)

            @block.tensor
            def _(pe):
                def step(j, u):
                    if (ref := at(j, u, 5)) is not None:
                        t, v = tile(ref), ref[1] % 2
                        pe.wait_ge(s["x3T_full"], t + 1)
                        wait(pe, s["root_full"], t - 1)
                        nc.tensor.matmul(p_root[v][:, 0:F], x3T[v][:, :], W["root1"][:, :], start=True, stop=True).then_inc(s["root_multiplied"], 1)
                    if (ref := at(j, u, 4)) is not None:
                        t, v = tile(ref), ref[1] % 2
                        pe.wait_ge(s["normal_full"], t + 1)
                        wait(pe, s["x3T_full"], t - 1)
                        nc.tensor.transpose(p_T[v][:, 0:F], x3[v][:, :], W["ident"][:, :]).then_inc(s["x3_transposed"], 1)
                    if (ref := at(j, u, 0)) is not None:
                        pe.wait_ge(s["weighted"], tile(ref) + 1)
                        sum_to_here(pe, nc, p_sum, same, link, ((0, message[u % 2][:, :]), (F, plane(D["scores"], ref, 0, H4))), whole, width, s, ref)
                over_all_tiles(pe, step, 5)

            @block.scalar
            def _(act):
                def step(j, u):
                    if (ref := at(j, u, 2)) is not None:
                        norm.deviation(act, ref)
                    if (ref := at(j, u, 4)) is not None:
                        t, v = tile(ref), ref[1] % 2
                        act.wait_ge(s["x3_transposed"], t + 1)
                        wait(act, s["root_multiplied"], t - 1)
                        act.copy(x3T[v][:, :], p_T[v][:, 0:F]).then_inc(s["x3T_full"], 1)
                    if (ref := at(j, u, 1)) is not None:
                        t, v = tile(ref), ref[1] % 2
                        act.wait_ge(s["low_full"], t + 1)
                        wait(act, s["y_full"], t - 1)
                        act.activation(grown[v][:, :], low[v][:, :], ACT.Exp).then_inc(s["grown_full"], 1)
                    if (ref := at(j, u, 0)) is not None:
                        t, v = tile(ref), ref[1] % 2
                        act.wait_ge(s["summed"], t + 1)
                        wait(act, s["mean_full"], t - 1)
                        act.copy(whole[v][:, :], p_sum[v][:, 0:width]).then_inc(s["whole_full"], 1)
                over_all_tiles(act, step, 4)

            @block.vector
            def _(dve):
                def step(j, u):
                    if (ref := at(j, u, 0)) is not None:
                        same_and_link(dve, nc, D, same, link, s["summed"], s, ref)
                    if (ref := at(j, u, 1)) is not None:
                        t, v = tile(ref), ref[1] % 2
                        dve.wait_ge(s["whole_full"], t + 1)
                        wait(dve, s["mean_full"], t)
                        nc.vector.reciprocal(inverse[:, :], whole[v][:, F:width]).then_inc(s["inverse_full"], 1)
                        dve.wait_ge(s["inverse_full"], t + 1)
                        wait(dve, s["high_full"], t - 1)
                        nc.vector.tensor_tensor(by_head(mean[v][:, :]), by_head(whole[v][:, 0:F]),
                                                inverse[:, :].unsqueeze(2).to_broadcast([F, H4, F // H4]), ALU.mult).then_inc(s["mean_full"], 1)
                        dve.wait_ge(s["mean_full"], t + 1)
                        wait(dve, s["grown_full"], t - 1)
                        nc.vector.tensor_scalar(low[v][:, :], mean[v][:, :], 0.0, None, ALU.min).then_inc(s["low_full"], 1)
                    if (ref := at(j, u, 2)) is not None:
                        t, v = tile(ref), ref[1] % 2
                        dve.wait_ge(s["low_full"], t + 1)
                        wait(dve, s["normal_full"], t - 1)
                        nc.vector.scalar_tensor_tensor(out=y[v][:, :], in0=mean[v][:, :], scalar=0.0, in1=plane(D["Y"], ref, 0, F),
                                                       op0=ALU.max, op1=ALU.add).then_inc(s["high_full"], 1)
                        dve.wait_ge(s["high_full"], t + 1)
                        dve.wait_ge(s["grown_full"], t + 1)
                        nc.vector.scalar_tensor_tensor(out=y[v][:, :], in0=grown[v][:, :], scalar=-1.0, in1=y[v][:, :],
                                                       op0=ALU.add, op1=ALU.add).then_inc(s["y_full"], 1)
                        norm.moments_of(dve, y[v][:, :], s["y_full"], ref)
                    if (ref := at(j, u, 3)) is not None:
                        t, v = tile(ref), ref[1] % 2
                        wait(dve, s["x3_kept"], t - 1)
                        wait(dve, s["x3_transposed"], t - 1)
                        norm.rows_of(dve, x3[v][:, :], y[v][:, :], ref)
                    if (ref := at(j, u, 6)) is not None:
                        dve.wait_ge(s["root_multiplied"], tile(ref) + 1)
                        nc.vector.tensor_tensor(plane(D["R"], ref, 0, F), p_root[ref[1] % 2][:, 0:F], W["b_root1_rows"][:, :], ALU.add).then_inc(s["root_full"], 1)
                over_all_tiles(dve, step, 6)

            @block.sync
            def _(sp):
                for b in range(BLOCKS):
                    a, tiles = N + b * BLOCK * F, slice(b * BLOCK, (b + 1) * BLOCK)
                    sp.wait_ge(s["x3_kept"], BLOCK * (b + 1))
                    sp.dma_start(io["X3"][a:a + BLOCK * F, :].rearrange("(t p) f -> p t f", p=F), D["Y"][:, tiles, :]).then_inc(s["stored"], 16)
                    sp.wait_ge(s["root_full"], BLOCK * (b + 1))
                    sp.dma_start(io["x_root"][:, tiles, :], D["R"][:, tiles, :]).then_inc(s["root_stored"], 16)
                sp.wait_ge(s["stored"], 16 * BLOCKS)
                sp.wait_ge(s["root_stored"], 16 * BLOCKS)


def relation_rows(nc, io, W, D, table, w_rel, hidden):
    RG = 4
    groups = [(a, min(a + RG, RELATIONS)) for a in range(0, RELATIONS, RG)]
    PARTS, BANKS = len(groups), 4
    with Phase(nc) as m:
        two = lambda name: [m.sb(f"{name}{u}", [F, F]) for u in range(2)]
        same, link, whole = two("same"), two("link"), two("whole")
        rows = [m.sb(f"rows{u}", [F, F]) for u in range(UNROLL)]
        index = [m.sb(f"index{u}", [F, 1], i32) for u in range(UNROLL)]
        rowsT, message = two("rowsT"), two("message")
        shares = m.sb("shares", [F, RELATIONS, F])
        w = m.sb("w_rel", [F, RELATIONS, F])
        p_w = [m.pb(f"p_w{n}", [F, RG, F]) for n in range(BANKS)]
        p_T, p_sum, p_hT, p_out = (m.pb(n, [F, 512]) for n in ("p_T", "p_sum", "p_hT", "p_out"))
        gathered, written = D["moves"], D["dst_moves"]
        s = m.named(SUMS + NORM + "waits_taken w_loaded index_ready transposed rowsT_full multiplied shares_full message_full "
                    "root_loaded0 root_loaded1 root_loaded2 root_loaded3 pre_full h_full h_kept h_transposed hT_full "
                    "out_multiplied y_full y_biased stored out_index_ready")
        if hidden:
            root = [m.sb(f"root{u}", [F, F]) for u in range(UNROLL)]
            h, hT, pre = [m.sb(f"h{u}", [F, F]) for u in range(UNROLL)], two("hT"), two("pre")
        else:
            y = [m.sb(f"y{u}", [F, F]) for u in range(UNROLL)]
            out_rows = [m.sb(f"out_rows{u}", [F, F]) for u in range(UNROLL)]
            out_index = [m.sb(f"out_index{u}", [F, 1], i32) for u in range(UNROLL)]
            norm = Norm(nc, m, W, s)
        with nc.Block() as block:

            @block.sync
            def _(sp):
                sp.dma_start(w[:, :, :], w_rel.rearrange("r p f -> p r f")).then_inc(s["w_loaded"], 16)
                if hidden:
                    def step(j, u):
                        wait(sp, s["pre_full"], UNROLL * j + u - UNROLL + 1)
                        sp.dma_start(root[u][:, :], plane(io["x_root"], (j, u), 0, F)).then_inc(s[f"root_loaded{u}"], 16)
                    over_all_tiles(sp, step, 0)
                    store_slots(sp, io["H"], D["R"], s["h_kept"], s["stored"])

            @block.gpsimd
            def _(pool):
                def step(j, u):
                    if (ref := at(j, u, 0)) is not None:
                        gather_rows(pool, s["waits_taken"], table, D["src_row"], index, s["index_ready"], rows, gathered, s["transposed"], j, u)
                    if hidden:
                        if (ref := at(j, u, 1)) is not None:
                            y_ = plane(D["Y"], ref, 0, F)
                            pool.tensor_tensor(y_, y_, W["b4c"][:, :], ALU.add).then_inc(s["y_biased"], 1)
                        if (ref := at(j, u, 8)) is not None:
                            pool.wait_ge(s["h_full"], tile(ref) + 1)
                            pool.tensor_copy(plane(D["R"], ref, 0, F), h[ref[1]][:, :]).then_inc(s["h_kept"], 1)
                    elif (ref := at(j, u, 8)) is not None:
                        t, v = tile(ref), ref[1]
                        wait(pool, written.sems[v], written.after(ref[0]))
                        pool.tensor_copy(out_index[v][:, :], column(D["dst_write"], ref)).then_inc(s["out_index_ready"], 1)
                        pool.wait_ge(s["out_index_ready"], t + 1)
                        pool.wait_ge(s["normal_full"], t + 1)
                        take_waits(pool, s["waits_taken"])
                        pool.indirect_dma_start(out=io["out"], out_offset=bass.IndirectOffsetOnAxis(ap=out_index[v][:, 0:1], axis=0),
                                                in_=out_rows[v][:, :], in_offset=None, bounds_check=N - 1,
                                                oob_is_err=False).then_inc(written.sems[v], 16)
                over_all_tiles(pool, step, 8)
                if not hidden:
                    for u in range(UNROLL):
                        pool.wait_ge(written.sems[u], written.after(PASSES))

            @block.tensor
            def _(pe):
                pe.wait_ge(s["w_loaded"], 16)

                def multiply(j, u, n):
                    if (ref := at(j, u, 1)) is None:
                        return
                    t, v, (a, b) = tile(ref), ref[1] % 2, groups[n]
                    if n == 0:
                        pe.wait_ge(s["rowsT_full"], t + 1)
                    wait(pe, s["shares_full"], PARTS * t + n - BANKS + 1)
                    nc.tensor.matmul(p_w[(PARTS * ref[1] + n) % BANKS][:, 0:b - a, :], rowsT[v][:, :], w[:, a:b, :],
                                     start=True, stop=True).then_inc(s["multiplied"], 1)

                def step(j, u):
                    multiply(j, u, 0)
                    if (ref := at(j, u, 0)) is not None:
                        pe.wait_ge(gathered.sems[u], gathered.after(j + 1))
                        wait(pe, s["rowsT_full"], tile(ref))
                        nc.tensor.transpose(p_T[:, 0:F], rows[u][:, :], W["ident"][:, :]).then_inc(s["transposed"], 1)
                    multiply(j, u, 1)
                    if (ref := at(j, u, 3)) is not None:
                        t, v = tile(ref), ref[1] % 2
                        pe.wait_ge(s["message_full"], t + 1)
                        pe.wait_ge(s["link_full"], t + 1)
                        wait(pe, s["whole_full"], t)
                        first = isinstance(t, int) and t == 0
                        last = nc.tensor.matmul(p_sum[:, 0:F], same[v][:, :], message[v][:, :], start=True, stop=first)
                        if not first:
                            last = nc.tensor.matmul(p_sum[:, 0:F], link[v][:, :], whole[1 - v][:, :], start=False, stop=True)
                        last.then_inc(s["summed"], 1)
                    multiply(j, u, 2)
                    if hidden and (ref := at(j, u, 7)) is not None:
                        t, v = tile(ref), ref[1] % 2
                        pe.wait_ge(s["hT_full"], t + 1)
                        wait(pe, s["y_full"], t)
                        nc.tensor.matmul(p_out[:, 0:F], hT[v][:, :], W["root2c"][:, :], start=True, stop=True).then_inc(s["out_multiplied"], 1)
                    if hidden and (ref := at(j, u, 6)) is not None:
                        t, v = tile(ref), ref[1] % 2
                        pe.wait_ge(s["h_full"], t + 1)
                        wait(pe, s["hT_full"], t)
                        nc.tensor.transpose(p_hT[:, 0:F], h[ref[1]][:, :], W["ident"][:, :]).then_inc(s["h_transposed"], 1)
                over_all_tiles(pe, step, 7 if hidden else 3)

            @block.scalar
            def _(act):
                def step(j, u):
                    if hidden and (ref := at(j, u, 5)) is not None:
                        t, v = tile(ref), ref[1] % 2
                        act.wait_ge(s["pre_full"], t + 1)
                        wait(act, s["h_transposed"], t - 3)
                        wait(act, s["h_kept"], t - 3)
                        act.activation(h[ref[1]][:, :], pre[v][:, :], ACT.Relu).then_inc(s["h_full"], 1)
                    if not hidden and (ref := at(j, u, 5)) is not None:
                        norm.deviation(act, ref)
                    if (ref := at(j, u, 0)) is not None:
                        t, v = tile(ref), u % 2
                        act.wait_ge(s["transposed"], t + 1)
                        wait(act, s["multiplied"], PARTS * (t - 1))
                        act.copy(rowsT[v][:, :], p_T[:, 0:F]).then_inc(s["rowsT_full"], 1)
                    if (ref := at(j, u, 3)) is not None:
                        t, v = tile(ref), ref[1] % 2
                        act.wait_ge(s["summed"], t + 1)
                        wait(act, s["pre_full" if hidden else "y_full"], t - 1)
                        act.copy(whole[v][:, :], p_sum[:, 0:F]).then_inc(s["whole_full"], 1)
                    if hidden and (ref := at(j, u, 6)) is not None:
                        t, v = tile(ref), ref[1] % 2
                        act.wait_ge(s["h_transposed"], t + 1)
                        wait(act, s["out_multiplied"], t - 1)
                        act.copy(hT[v][:, :], p_hT[:, 0:F]).then_inc(s["hT_full"], 1)
                over_all_tiles(act, step, 6 if hidden else 5)

            @block.vector
            def _(dve):
                def take_shares(j, u, n):
                    if (ref := at(j, u, 1)) is None:
                        return
                    t, (a, b) = tile(ref), groups[n]
                    dve.wait_ge(s["multiplied"], PARTS * t + n + 1)
                    if n == 0:
                        wait(dve, s["message_full"], t)
                    share = plane(D["relation"], ref, a, b).unsqueeze(2).to_broadcast([F, b - a, F])
                    nc.vector.tensor_tensor(shares[:, a:b, :], p_w[(PARTS * ref[1] + n) % BANKS][:, 0:b - a, :], share,
                                            ALU.mult).then_inc(s["shares_full"], 1)

                def step(j, u):
                    take_shares(j, u, 0)
                    if (ref := at(j, u, 4)) is not None:
                        t, v = tile(ref), ref[1] % 2
                        dve.wait_ge(s["whole_full"], t + 1)
                        if hidden:
                            dve.wait_ge(s[f"root_loaded{ref[1]}"], 16 * (ref[0] + 1))
                            wait(dve, s["h_full"], t - 1)
                            nc.vector.tensor_tensor(pre[v][:, :], whole[v][:, :], root[ref[1]][:, :], ALU.add).then_inc(s["pre_full"], 1)
                        else:
                            wait(dve, s["normal_full"], t - 3)
                            nc.vector.tensor_tensor(y[ref[1]][:, :], whole[v][:, :], plane(D["Y"], ref, 0, F), ALU.add).then_inc(s["y_full"], 1)
                    if (ref := at(j, u, 1)) is not None:
                        same_and_link(dve, nc, D, same, link, s["summed"], s, ref)
                    if hidden and (ref := at(j, u, 8)) is not None:
                        t = tile(ref)
                        dve.wait_ge(s["out_multiplied"], t + 1)
                        dve.wait_ge(s["y_biased"], t + 1)
                        y_ = plane(D["Y"], ref, 0, F)
                        nc.vector.tensor_tensor(y_, p_out[:, 0:F], y_, ALU.add).then_inc(s["y_full"], 1)
                    if not hidden and (ref := at(j, u, 4)) is not None:
                        norm.statistics(dve, y[ref[1]][:, :], s["y_full"], ref)
                    take_shares(j, u, 1)
                    if not hidden and (ref := at(j, u, 6)) is not None:
                        norm.inverse_of(dve, ref)
                    if not hidden and (ref := at(j, u, 4)) is not None:
                        norm.aggregate(dve, ref)
                    take_shares(j, u, 2)
                    if not hidden and (ref := at(j, u, 6)) is not None:
                        wait(dve, written.sems[ref[1]], written.after(ref[0]))
                        norm.apply(dve, out_rows[ref[1]][:, :], y[ref[1]][:, :], ref)
                    if (ref := at(j, u, 1)) is not None:
                        t, v = tile(ref), ref[1] % 2
                        dve.wait_ge(s["shares_full"], PARTS * (t + 1))
                        wait(dve, s["summed"], t - 1)
                        nc.vector.tensor_reduce(message[v][:, :], shares[:, :, :].rearrange("p r f -> p f r"), AX.X, ALU.add).then_inc(s["message_full"], 1)
                over_all_tiles(dve, step, 8 if hidden else 6)
        gathered.passes += PASSES
        if not hidden:
            written.passes += PASSES


def gnn_kernel(nc, io):
    with ExitStack() as stack:
        W, D = {}, {}
        with Phase(nc) as m:
            prepare_weights(nc, Memory(nc, stack), m, io, W)
        edges = Memory(nc, stack)
        D["moves"], D["dst_moves"] = PoolMoves(edges, "pool_moved"), PoolMoves(edges, "pool_moved_dst")
        for name, shape, dt in (("dst_col", [F, T], fp32), ("src_col", [F, T], i32), ("dst_read", [F, T], i32),
                                ("dst_write", [F, T], i32), ("slot_row", [F, T], i32), ("src_row", [F, T], i32),
                                ("link_key", [F, T], fp32), ("back_key", [F, T], fp32), ("last_key", [F, T], fp32), ("relation", [F, T, RELATIONS], fp32),
                                ("end_keys", [HEADS, T, 2], fp32)):
            D[name] = edges.sb(name, shape, dt)
        with Phase(nc) as m:
            dense_phase(nc, m, io, W)
        for name, shape in (("drow", [F, SLOTS]), ("Y", [F, T, F]), ("R", [F, T, F]), ("scores", [F, T, HEADS]),
                            ("dinv", [F, T]), ("count", [F, T, RELATIONS])):
            D[name] = edges.sb(name, shape)
        prepare_edges(nc, io, W, D)
        map_sources(nc, io, D)
        attention_messages(nc, io, W, D)
        weights_of_edges(nc, io, W, D, (F // HEADS) ** -0.5)
        attention_rows(nc, io, W, D)
        hidden_rows(nc, io, W, D)
        output_rows(nc, io, W, D)
        gat_messages(nc, io, W, D)
        weights_of_edges(nc, io, W, D, 1.0)
        gat_rows(nc, io, W, D)
        relation_rows(nc, io, W, D, io["X3"], io["L3_gnn_w_rel1"], hidden=True)
        relation_rows(nc, io, W, D, io["H"], io["L3_gnn_w_rel2"], hidden=False)


_INS = ['x', 'edge_attr_42', 'L0_gnn_Wq', 'L0_gnn_bq', 'L0_gnn_Wk', 'L0_gnn_bk', 'L0_gnn_Wv', 'L0_gnn_bv', 'L0_gnn_Ws', 'L0_gnn_bs',
        'L1_gnn_W1', 'L1_gnn_b1', 'L1_gnn_W2', 'L1_gnn_b2', 'L2_gnn_W', 'L2_gnn_a_src', 'L2_gnn_a_dst',
        'L3_gnn_w_rel1', 'L3_gnn_root1', 'L3_gnn_b1', 'L3_gnn_w_rel2', 'L3_gnn_root2', 'L3_gnn_b2']


def kernel(**inputs):
    import numpy as _np
    import concourse.bacc as _bacc
    from concourse.bass_utils import run_bass_kernel_spmd as _run

    nc = _bacc.Bacc("TRN2", target_bir_lowering=False, num_devices=1)
    arrays = {name: _np.ascontiguousarray(inputs[name]) for name in _INS}
    arrays["src"] = _np.concatenate([inputs["src"], _np.zeros(SLOTS - E, _np.int32)])
    arrays["dst"] = _np.concatenate([inputs["dst"], _np.full(SLOTS + 1 - E, PAD_KEY, _np.int32)])
    io = {name: nc.dram_tensor(f"in_{name}", a.shape, mybir.dt.from_np(a.dtype), kind="ExternalInput").ap() for name, a in arrays.items()}
    for n in ("Z1", "H2", "X2", "X3", "H"):
        io[n] = nc.dram_tensor(n, (N + SLOTS, F), fp32, kind="Internal").ap()
    io["row_of"] = nc.dram_tensor("row_of", (N, 1), i32, kind="Internal").ap()
    io["dst_f"] = nc.dram_tensor("dst_keys", (SLOTS,), fp32, kind="Internal").ap()
    io["x_root"] = nc.dram_tensor("x_root", (F, T, F), fp32, kind="Internal").ap()
    for n in ("max_ends", "max_ends_out"):
        io[n] = nc.dram_tensor(n + "_rows", (T * HEADS * 2,), fp32, kind="Internal").ap()
    io["out"] = nc.dram_tensor("out", (N, F), fp32, kind="ExternalOutput").ap()
    gnn_kernel(nc, io)
    r = _run(nc, [{f"in_{name}": a for name, a in arrays.items()}], core_ids=[0])
    return r.results[0]["out"]
```

```python
from contextlib import ExitStack

import numpy as np

import concourse.bass as bass
from concourse import mybir
from concourse.alu_op_type import AluOpType as ALU

fp32 = mybir.dt.float32
i32 = mybir.dt.int32
ACT = mybir.ActivationFunctionType
AX = mybir.AxisListType

N = 50000
E = 12500
F = 128
GROUPS = (N + 511) // 512
LAST_BASE = N - 512
EPS = 1e-5
HEADS = 8
GAT_HEADS = 4
ALPHA = 0.2
RELATIONS = 10
EMB = 16
BLOCKS, BLOCK = 10, 10
T = BLOCKS * BLOCK
SLOTS = T * F
UNROLL = 4
PASSES = T // UNROLL
PAD_KEY = 1 << 16
BEYOND = 1 << 20
FAR = 1e30


class Memory:

    def __init__(self, nc, stack, prefix=""):
        self.nc, self.stack, self.prefix = nc, stack, prefix

    def sb(self, name, shape, dt=fp32):
        return self.stack.enter_context(self.nc.sbuf_tensor(self.prefix + name, shape, dt))

    def pb(self, name, shape, dt=fp32):
        return self.stack.enter_context(self.nc.psum_tensor(self.prefix + name, shape, dt))

    def sem(self, name):
        return self.stack.enter_context(self.nc.semaphore(self.prefix + name))


def clear(nc, sems):
    numbers = sorted(s.num for s in sems)
    with nc.Block() as block:

        @block.gpsimd
        def _(pool):
            at_ = 0
            while at_ < len(numbers):
                end = at_
                while end + 1 < len(numbers) and numbers[end + 1] == numbers[end] + 1:
                    end += 1
                pool.sem_clear(range(numbers[at_], numbers[end] + 1))
                at_ = end + 1


class Phase(Memory):

    opened = 0

    def __init__(self, nc):
        Phase.opened += 1
        super().__init__(nc, ExitStack(), f"phase{Phase.opened}_")
        self.sems = []

    def sem(self, name):
        s = super().sem(name)
        self.sems.append(s)
        return s

    def named(self, names):
        return {n: self.sem(n) for n in names.split()}

    def __enter__(self):
        self.stack.__enter__()
        return self

    def __exit__(self, *e):
        if e[0] is None and self.sems:
            clear(self.nc, self.sems)
        return self.stack.__exit__(*e)


def at(j, u, k):
    jj, uu = j + (u - k) // UNROLL, (u - k) % UNROLL
    if isinstance(jj, int) and not 0 <= jj < PASSES:
        return None
    return jj, uu


def over_all_tiles(eng, step, lag):
    lead = (lag + UNROLL - 1) // UNROLL + 1
    for k in range(lead * UNROLL):
        step(k // UNROLL, k % UNROLL)
    with eng.Fori(lead, PASSES) as j:
        for u in range(UNROLL):
            step(j, u)
    for k in range(lag):
        step(PASSES + k // UNROLL, k % UNROLL)


def tile(ref):
    return UNROLL * ref[0] + ref[1]


def column(m, ref):
    return m[:, bass.ds(tile(ref), 1)]


def plane(m, ref, a, b):
    return m[:, bass.ds(tile(ref), 1), a:b].rearrange("p a c -> p (a c)")


class PoolMoves:

    def __init__(self, mem, name):
        self.sems = [mem.sem(f"{name}{u}") for u in range(UNROLL)]
        self.passes = 0

    def after(self, j):
        return 16 * (self.passes + j) if isinstance(j, int) else (j + self.passes) * 16


def wait(eng, s, count):
    if not isinstance(count, int) or count > 0:
        eng.wait_ge(s, count)


def row_vector(v):
    return v.rearrange("(a n) -> a n", a=1).partition_broadcast(F)


def take_waits(eng, taken):
    eng.sem_inc(taken)


def prepare_weights(nc, mem, m, io, W):
    sb = mem.sb
    for name, shape in (("ident", [F, F]), ("eps", [F, 1]), ("Wsc", [F, F]), ("W1", [F, 2 * F]), ("W2c", [F, 2, F]),
                        ("root1", [F, F]), ("root2c", [F, F]), ("b_W1", [F, 2]), ("b_root1", [F, 1]),
                        ("bsc", [F, F]), ("b2c", [F, F]), ("b4c", [F, F]), ("one", [F, 1]), ("b_root1_rows", [F, F]),
                        ("Wq", [F, F]), ("Wkv", [F, 2, F]), ("bqk", [F, 2, F]), ("bv", [F, F]), ("Wgat_src", [F, F + GAT_HEADS]), ("w_dst", [F, GAT_HEADS])):
        W[name] = sb(name, shape)
    Wgat, w_src = W["Wgat_src"][:, 0:F].rearrange("p (h d) -> p h d", h=GAT_HEADS), W["Wgat_src"][:, F:F + GAT_HEADS]
    mean, a_src, a_dst, prod = m.sb("mean", [F, 1]), m.sb("a_src", [F, F]), m.sb("a_dst", [F, F]), m.sb("a_prod", [F, F])
    loaded, ident_done, step_done = m.sem("loaded"), m.sem("ident_done"), m.sem("step_done")
    by_head = lambda w: w.rearrange("h p d -> p h d")
    heads = lambda m: m.rearrange("p (h d) -> p h d", h=HEADS)
    loads = [
        (heads(W["Wq"][:, :]), by_head(io["L0_gnn_Wq"])), (heads(W["Wkv"][:, 0, :]), by_head(io["L0_gnn_Wk"])),
        (heads(W["Wkv"][:, 1, :]), by_head(io["L0_gnn_Wv"])), (Wgat, by_head(io["L2_gnn_W"])),
        (W["bqk"][:, 0, :], row_vector(io["L0_gnn_bq"].rearrange("h d -> (h d)"))),
        (W["bqk"][:, 1, :], row_vector(io["L0_gnn_bk"].rearrange("h d -> (h d)"))),
        (W["bv"][:, :], row_vector(io["L0_gnn_bv"].rearrange("h d -> (h d)"))),
        (a_src[:, :], row_vector(io["L2_gnn_a_src"].rearrange("h d -> (h d)"))),
        (a_dst[:, :], row_vector(io["L2_gnn_a_dst"].rearrange("h d -> (h d)"))),
        (W["b_root1_rows"][:, :], row_vector(io["L3_gnn_b1"])),
        (W["Wsc"][:, :], io["L0_gnn_Ws"]), (W["W1"][:, :], io["L1_gnn_W1"]),
        (W["W2c"][:, :, :], io["L1_gnn_W2"].rearrange("(k p) f -> p k f", k=2)),
        (W["root1"][:, :], io["L3_gnn_root1"]), (W["root2c"][:, :], io["L3_gnn_root2"]),
        (W["b_W1"][:, :], io["L1_gnn_b1"].rearrange("(k p) -> p k", k=2)),
        (W["b_root1"][:, :], io["L3_gnn_b1"].rearrange("(p a) -> p a", a=1)),
        (W["bsc"][:, :], row_vector(io["L0_gnn_bs"])), (W["b2c"][:, :], row_vector(io["L1_gnn_b2"])),
        (W["b4c"][:, :], row_vector(io["L3_gnn_b2"])),
    ]
    with nc.Block() as block:

        @block.sync
        def _(sp):
            for dst, src in loads:
                sp.dma_start(dst, src, allow_slow_non_contiguous=True).then_inc(loaded, 16)

        @block.gpsimd
        def _(pool):
            pool.memset(W["ident"][:, :], 0.0).then_inc(ident_done, 1)
            pool.memset(W["eps"][:, :], EPS)
            pool.memset(W["one"][:, :], 1.0).then_inc(ident_done, 1)
            pool.wait_ge(ident_done, 2)
            pool.affine_select(out=W["ident"][:, :], in_=W["ident"][:, :], compare_op=ALU.not_equal, fill=1.0,
                               base=0, pattern=[[-1, F]], channel_multiplier=1).then_inc(ident_done, 1)

        @block.vector
        def _(dve):
            done = 0

            def chained(ins):
                nonlocal done
                done += 1
                ins.then_inc(step_done, 1)
                dve.wait_ge(step_done, done)

            dve.wait_ge(loaded, 16 * len(loads))
            dve.wait_ge(ident_done, 3)
            chained(nc.vector.tensor_tensor(W["Wsc"][:, :], W["Wsc"][:, :], W["ident"][:, :], ALU.add))
            for m in (W["Wsc"][:, :], W["W2c"][:, 0, :], W["W2c"][:, 1, :], W["root2c"][:, :],
                      W["bsc"][:, :], W["b2c"][:, :], W["b4c"][:, :]):
                chained(nc.vector.tensor_reduce(mean[:, :], m, AX.X, ALU.add))
                chained(nc.vector.tensor_scalar(mean[:, :], mean[:, :], -1.0 / F, None, ALU.mult))
                chained(nc.vector.tensor_scalar(m, m, mean[:, 0:1], None, ALU.add))
            for a, w in ((a_src, w_src), (a_dst, W["w_dst"][:, :])):
                p = prod[:, :].rearrange("p (h d) -> p h d", h=GAT_HEADS)
                chained(nc.vector.tensor_tensor(p, Wgat, a[:, :].rearrange("p (h d) -> p h d", h=GAT_HEADS), ALU.mult))
                chained(nc.vector.tensor_reduce(w, p, AX.X, ALU.add))


def dense_phase(nc, mem, io, W, row_map):
    sb, pb, sem = mem.sb, mem.pb, mem.sem
    ident, eps = W["ident"], W["eps"]
    RING = 4
    places = {"xT": 4, "y1": 4, "sq1": 2, "x1": 4, "x1b": 4, "x1T": 2, "g0": 2, "g1": 2, "h2": 4, "y2": 4, "sq2": 2,
              "x2": 4, "x3": 4, "x3b": 4, "x3T": 2, "hT": 2, "h": 4, "y4": 4, "sq4": 2, "o": 4}
    B = {n: [sb(f"{n}_{u}", [F, 4, F], fp32) for u in range(k)] for n, k in places.items()}
    stats = {"ss1": 2, "sd1": 2, "r1": 2, "ss2": 4, "sd2": 2, "r2": 4, "v2": 2, "q2": 2, "sd3": 2, "w2": 2, "r3": 2, "ss4": 2, "sd4": 2, "r4": 2}
    B.update({n: [sb(f"{n}_{u}", [F, 4], fp32) for u in range(k)] for n, k in stats.items()})

    p_y1, p_x1T, p_g0, p_g1, p_h2, p_x3T, p_hT = (pb(f"P{b}", [F, 4, F], fp32) for b in range(1, 8))
    p_h, p_y4 = p_x3T, p_hT

    from_pe = "p_y1 p_x1T p_g0 p_g1 p_h2 p_x3T p_hT p_h p_y4".split()
    S = {n: sem(f"d_{n}_full") for n in [*B, *from_pe] if n != "xT"}
    xT_loaded = [sem(f"d_xT_loaded{u}") for u in range(RING)]
    tables = {"x1": "Z1", "h2": "H2", "x2": "X2", "x3": "X3", "h": "H", "o": "out"}
    stored = {n: [sem(f"d_{n}_stored{u}") for u in range(RING)] for n in tables}
    LEAD, END = 6, GROUPS // RING - 1

    def group(i, k):
        j, u = i
        jj, uu = j + (u - k) // RING, (u - k) % RING
        if isinstance(jj, int) and not 0 <= RING * jj + uu < GROUPS:
            return None
        return jj, uu

    def number(g):
        return RING * g[0] + g[1]

    def buf(n, g):
        return B[n][g[1] % len(B[n])]

    def rows(table, g):
        g = number(g)
        base = LAST_BASE if isinstance(g, int) and g == GROUPS - 1 else g * 512
        return table[bass.ds(base, 512), :].rearrange("(p t) f -> p t f", t=4)

    def run(eng, step, lag):
        for i in range(LEAD * RING):
            step((i // RING, i % RING))
        with eng.Fori(LEAD, END) as j:
            for u in range(RING):
                step((j, u))
        for i in range(END * RING, GROUPS + lag):
            step((i // RING, i % RING))

    over_tiles = lambda w: w[:, :].unsqueeze(1).to_broadcast([F, 4, F])
    over_rows = lambda r: r[:, :].unsqueeze(2).to_broadcast([F, 4, F])

    def made(eng, n, g, ahead=0):
        count = number(g) + 1 + ahead
        wait(eng, S[n], min(count, GROUPS) if isinstance(count, int) else count)

    def left(eng, out, by, g):
        made(eng, by, g, -len(B[out]))

    def left_by_store(eng, n, g):
        wait(eng, stored[n][g[1]], 16 * g[0])

    with nc.Block() as block:

        @block.sync
        def _(sp):
            def load(g):
                made(sp, "p_y1", g, -RING)
                columns = io["x_columns"][bass.ds(number(g) * F, F), :].rearrange("f (t p) -> f t p", t=4)
                sp.dma_start(buf("xT", g)[:, :, :], columns).then_inc(xT_loaded[g[1]], 16)

            def store(n, g):
                made(sp, n, g)
                if isinstance(g[0], int) and number(g) == GROUPS - 1:
                    sp.wait_ge(stored[n][g[1] - 1], 16 * (g[0] + 1))
                sp.dma_start(rows(io[tables[n]], g), buf(n, g)[:, :, :]).then_inc(stored[n][g[1]], 16)

            for u in range(3):
                load((0, u))

            def step(i):
                if (g := group(i, -3)) is not None:
                    load(g)
                for n, lag in (("x1", 5), ("h2", 8), ("x2", 12), ("x3", 13), ("h", 16), ("o", 19)):
                    if (g := group(i, lag)) is not None:
                        store(n, g)
            run(sp, step, 19)
            for n in stored:
                for u in range(RING):
                    sp.wait_ge(stored[n][u], 16 * len(range(u, GROUPS, RING)))

        @block.tensor
        def _(pe):
            def transposes(out, src, done):
                for t in range(4):
                    last = nc.tensor.transpose(out[:, t, :], src[:, t, :], ident[:, :])
                last.then_inc(S[done], 1)

            def products(out, lhsT, weight, done):
                for t in range(4):
                    last = nc.tensor.matmul(out[:, t, :], lhsT[:, t, :], W[weight][:, :], start=True, stop=True)
                last.then_inc(S[done], 1)

            def step(i):
                if (g := group(i, 15)) is not None:
                    made(pe, "hT", g)
                    made(pe, "x3T", g, 1)
                    transposes(p_h, buf("hT", g), "p_h")
                    products(p_y4, buf("hT", g), "root2c", "p_y4")
                if (g := group(i, 7)) is not None:
                    made(pe, "g0", g)
                    made(pe, "g1", g)
                    made(pe, "h2", g, -1)
                    for t in range(4):
                        for k in range(2):
                            last = nc.tensor.matmul(p_h2[:, t, :], buf(f"g{k}", g)[:, t, :], W["W2c"][:, k, :], start=(k == 0), stop=(k == 1))
                    last.then_inc(S["p_h2"], 1)
                if (g := group(i, 6)) is not None:
                    made(pe, "x1T", g)
                    for k in range(2):
                        made(pe, f"g{k}", g, -1)
                        nc.tensor.matmul((p_g0, p_g1)[k][:, :, :], W["W1"][:, k * F:(k + 1) * F], buf("x1T", g)[:, :, :],
                                         start=True, stop=True).then_inc(S[f"p_g{k}"], 1)
                if (g := group(i, 13)) is not None:
                    made(pe, "x3", g)
                    made(pe, "x3T", g, -1)
                    made(pe, "h", g, -2)
                    transposes(p_x3T, buf("x3", g), "p_x3T")
                if (g := group(i, 14)) is not None:
                    made(pe, "x3T", g)
                    made(pe, "hT", g, -1)
                    made(pe, "y4", g, -1)
                    nc.tensor.matmul(p_hT[:, :, :], W["root1"][:, :], buf("x3T", g)[:, :, :], start=True, stop=True).then_inc(S["p_hT"], 1)
                if (g := group(i, 5)) is not None:
                    made(pe, "x1", g)
                    made(pe, "x1T", g, -1)
                    transposes(p_x1T, buf("x1", g), "p_x1T")
                if (g := group(i, 1)) is not None:
                    pe.wait_ge(xT_loaded[g[1]], 16 * (g[0] + 1))
                    made(pe, "y1", g, -1)
                    products(p_y1, buf("xT", g), "Wsc", "p_y1")
            run(pe, step, 15)

        @block.scalar
        def _(act):
            def square(dst, src, total, i, lag):
                if (g := group(i, lag)) is not None:
                    made(act, src, g)
                    left(act, dst, total, g)
                    nc.scalar.activation(buf(dst, g)[:, :, :], buf(src, g)[:, :, :], ACT.Square).then_inc(S[dst], 1)

            def root(dst, src, inverse, i, lag):
                if (g := group(i, lag)) is not None:
                    made(act, src, g)
                    left(act, dst, inverse, g)
                    nc.scalar.activation(buf(dst, g)[:, :], buf(src, g)[:, :], ACT.Sqrt, bias=eps[:, :], scale=1.0 / F).then_inc(S[dst], 1)

            def read_out(dst, bank, src, user, i, lag, **kw):
                if (g := group(i, lag)) is not None:
                    made(act, src, g)
                    left(act, dst, user, g)
                    if kw:
                        nc.scalar.activation(buf(dst, g)[:, :, :], bank[:, :, :], ACT.Relu, **kw).then_inc(S[dst], 1)
                    else:
                        nc.scalar.copy(buf(dst, g)[:, :, :], bank[:, :, :]).then_inc(S[dst], 1)

            def step(i):
                square("sq4", "y4", "ss4", i, 16)
                square("sq2", "y2", "ss2", i, 9)
                square("sq1", "y1", "ss1", i, 2)
                read_out("g0", p_g0, "p_g0", "p_h2", i, 6, bias=W["b_W1"][:, 0:1])
                read_out("g1", p_g1, "p_g1", "p_h2", i, 6, bias=W["b_W1"][:, 1:2])
                root("sd1", "ss1", "r1", i, 3)
                root("sd2", "ss2", "r2", i, 10)
                root("sd4", "ss4", "r4", i, 17)
                root("sd3", "q2", "w2", i, 11)
                read_out("x3T", p_x3T, "p_x3T", "p_hT", i, 13)
                read_out("hT", p_hT, "p_hT", "p_y4", i, 14, bias=W["b_root1"][:, :])
            run(act, step, 17)

        @block.vector
        def _(dve):
            def total(dst, src, users, i, lag):
                if (g := group(i, lag)) is not None:
                    made(dve, src, g)
                    for by in users:
                        left(dve, dst, by, g)
                    nc.vector.tensor_reduce(buf(dst, g)[:, :], buf(src, g)[:, :, :], AX.X, ALU.add).then_inc(S[dst], 1)

            def inverse(dst, src, users, i, lag):
                if (g := group(i, lag)) is not None:
                    made(dve, src, g)
                    for by in users:
                        left(dve, dst, by, g)
                    nc.vector.reciprocal(buf(dst, g)[:, :], buf(src, g)[:, :]).then_inc(S[dst], 1)

            def times(dst, a, b, user, i, lag):
                if (g := group(i, lag)) is not None:
                    made(dve, a, g)
                    made(dve, b, g)
                    left(dve, dst, user, g)
                    nc.vector.tensor_tensor(buf(dst, g)[:, :], buf(a, g)[:, :], buf(b, g)[:, :], ALU.mult).then_inc(S[dst], 1)

            def step(i):
                inverse("w2", "sd3", ("r3",), i, 12)
                inverse("r1", "sd1", ("x1",), i, 4)
                inverse("r2", "sd2", ("x2", "r3"), i, 11)
                times("r3", "w2", "r2", "x3", i, 12)
                inverse("r4", "sd4", ("o",), i, 18)
                times("v2", "ss2", "r2", "q2", i, 11)
                if (g := group(i, 12)) is not None:
                    made(dve, "r3", g)
                    left(dve, "x3", "p_x3T", g)
                    left(dve, "x3", "x3b", g)
                    left_by_store(dve, "x3", g)
                    nc.vector.tensor_tensor(buf("x3", g)[:, :, :], buf("y2", g)[:, :, :], over_rows(buf("r3", g)), ALU.mult).then_inc(S["x3"], 1)
                times("q2", "v2", "r2", "sd3", i, 11)
                total("ss1", "sq1", ("sd1",), i, 3)
                total("ss2", "sq2", ("sd2", "v2"), i, 10)
                total("ss4", "sq4", ("sd4",), i, 17)
                if (g := group(i, 15)) is not None:
                    made(dve, "p_h", g)
                    left_by_store(dve, "h", g)
                    nc.vector.tensor_copy(buf("h", g)[:, :, :], p_h[:, :, :]).then_inc(S["h"], 1)
                    made(dve, "p_y4", g)
                    made(dve, "x3b", g)
                    left(dve, "y4", "sq4", g)
                    left(dve, "y4", "o", g)
                    nc.vector.tensor_tensor(buf("y4", g)[:, :, :], p_y4[:, :, :], buf("x3b", g)[:, :, :], ALU.add).then_inc(S["y4"], 1)
                if (g := group(i, 18)) is not None:
                    made(dve, "r4", g)
                    left_by_store(dve, "o", g)
                    nc.vector.tensor_tensor(buf("o", g)[:, :, :], buf("y4", g)[:, :, :], over_rows(buf("r4", g)), ALU.mult).then_inc(S["o"], 1)
                if (g := group(i, 7)) is not None:
                    made(dve, "p_h2", g)
                    left(dve, "h2", "y2", g)
                    left_by_store(dve, "h2", g)
                    nc.vector.tensor_copy(buf("h2", g)[:, :, :], p_h2[:, :, :]).then_inc(S["h2"], 1)
                if (g := group(i, 5)) is not None:
                    made(dve, "p_x1T", g)
                    left(dve, "x1T", "p_g1", g)
                    nc.vector.tensor_copy(buf("x1T", g)[:, :, :], p_x1T[:, :, :]).then_inc(S["x1T"], 1)
                if (g := group(i, 1)) is not None:
                    made(dve, "p_y1", g)
                    left(dve, "y1", "x1", g)
                    left(dve, "y1", "sq1", g)
                    nc.vector.tensor_tensor(buf("y1", g)[:, :, :], p_y1[:, :, :], over_tiles(W["bsc"]), ALU.add).then_inc(S["y1"], 1)
            run(dve, step, 18)

        @block.gpsimd
        def _(pool):
            def step(i):
                has_tile = not isinstance(i[0], int) or number(i) < T
                if has_tile:
                    row_map.prepare_scatter(pool, *i)
                if (g := group(i, 13)) is not None:
                    made(pool, "x3", g)
                    left(pool, "x3b", "y4", g)
                    nc.gpsimd.tensor_tensor(buf("x3b", g)[:, :, :], buf("x3", g)[:, :, :], over_tiles(W["b4c"]), ALU.add).then_inc(S["x3b"], 1)
                if (g := group(i, 8)) is not None:
                    made(pool, "h2", g)
                    made(pool, "x1b", g)
                    left(pool, "y2", "sq2", g)
                    left(pool, "y2", "x2", g)
                    left(pool, "y2", "x3", g)
                    nc.gpsimd.tensor_tensor(buf("y2", g)[:, :, :], buf("h2", g)[:, :, :], buf("x1b", g)[:, :, :], ALU.add).then_inc(S["y2"], 1)
                if (g := group(i, 5)) is not None:
                    made(pool, "x1", g)
                    left(pool, "x1b", "y2", g)
                    nc.gpsimd.tensor_tensor(buf("x1b", g)[:, :, :], buf("x1", g)[:, :, :], over_tiles(W["b2c"]), ALU.add).then_inc(S["x1b"], 1)
                if (g := group(i, 4)) is not None:
                    made(pool, "r1", g)
                    left(pool, "x1", "p_x1T", g)
                    left(pool, "x1", "x1b", g)
                    left_by_store(pool, "x1", g)
                    nc.gpsimd.tensor_tensor(buf("x1", g)[:, :, :], buf("y1", g)[:, :, :], over_rows(buf("r1", g)), ALU.mult).then_inc(S["x1"], 1)
                if (g := group(i, 11)) is not None:
                    made(pool, "r2", g)
                    made(pool, "y2", g)
                    left_by_store(pool, "x2", g)
                    nc.gpsimd.tensor_tensor(buf("x2", g)[:, :, :], buf("y2", g)[:, :, :], over_rows(buf("r2", g)), ALU.mult).then_inc(S["x2"], 1)
                if has_tile:
                    row_map.scatter(pool, *i)
            run(pool, step, 13)
            for u in range(RING):
                pool.wait_ge(row_map.moves.sems[u], row_map.moves.after(PASSES))
    row_map.moves.passes += PASSES




def prepare_edges(nc, io, W, D):
    with Phase(nc) as m:
        dst_rows, next_rows, src_rows = (m.sb(n, [T, F], i32) for n in ("dst_rows", "next_rows", "src_rows"))
        beside, beside_f = m.sb("beside", [T, 2, 1], i32), m.sb("beside_f", [T, 2])
        link_rows, back_rows = m.sb("link_rows", [T, F]), m.sb("back_rows", [T, F])
        next_f, src_f = m.sb("next_f", [T, F]), m.sb("src_f", [T, F])
        dst_f, end_keys_apart = m.sb("dst_f", [T, F]), m.sb("end_keys_apart", [HEADS, 2, T])
        node = m.sb("node", [125, N // 125], i32)
        attr = m.sb("attr", [F, T, RELATIONS])
        best, order, score = m.sb("best", [F, T]), m.sb("order", [F, RELATIONS]), m.sb("score", [F, T, RELATIONS])
        next_col, same_as_next, off = m.sb("next_col", [F, T]), m.sb("same_as_next", [F, T]), m.sb("off", [F, T])
        p_cols = m.pb("p_cols", [F, 3, F])
        s = m.named("beside_cleared beside_loaded beside_converted marks_full marks_stored rows_loaded attr_loaded attr_zeroed rows_converted cols_transposed dst_stored ends_loaded node_made node_stored "
                    "dst_col_full step_done")
        with nc.Block() as block:

            @block.sync
            def _(sp):
                for dst, src in ((dst_rows, io["dst"][0:SLOTS]), (next_rows, io["dst"][1:SLOTS + 1]), (src_rows, io["src"])):
                    sp.dma_start(dst[:, :], src.rearrange("(t e) -> t e", e=F)).then_inc(s["rows_loaded"], 16)
                sp.wait_ge(s["beside_cleared"], 1)
                sp.dma_start(beside[1:T, 0, :], io["dst"][F - 1:F - 1 + (T - 1) * F].rearrange("(t e) -> t e", e=F)[:, 0:1],
                             allow_slow_non_contiguous=True).then_inc(s["beside_loaded"], 16)
                sp.dma_start(beside[:, 1, :], io["dst"][1:SLOTS + 1].rearrange("(t e) -> t e", e=F)[:, F - 1:F],
                             allow_slow_non_contiguous=True).then_inc(s["beside_loaded"], 16)
                sp.wait_ge(s["attr_zeroed"], 1)
                whole = E // F
                edges = io["edge_attr_42"][:, EMB:EMB + RELATIONS]
                sp.dma_start(attr[:, 0:whole, :], edges[0:whole * F, :].rearrange("(t e) r -> e t r", e=F),
                             allow_slow_non_contiguous=True).then_inc(s["attr_loaded"], 16)
                sp.dma_start(attr[0:E - whole * F, whole, :], edges[whole * F:E, :],
                             allow_slow_non_contiguous=True).then_inc(s["attr_loaded"], 16)
                sp.wait_ge(s["rows_converted"], 1)
                sp.dma_start(io["dst_f"].rearrange("(t e) -> t e", e=F), dst_f[:, :]).then_inc(s["dst_stored"], 16)
                sp.wait_ge(s["marks_full"], 2)
                for table, marks in ((io["link_rows"], link_rows), (io["back_rows"], back_rows)):
                    sp.dma_start(table, marks[:, :]).then_inc(s["marks_stored"], 16)
                sp.wait_ge(s["dst_stored"], 16)
                for end, c in enumerate((0, F - 1)):
                    edge_keys = io["dst_f"].rearrange("(t e) -> t e", e=F)[:, c:c + 1].rearrange("t a -> a t")
                    sp.dma_start(end_keys_apart[:, end, :], edge_keys.partition_broadcast(HEADS),
                                 allow_slow_non_contiguous=True).then_inc(s["ends_loaded"], 16)
                sp.wait_ge(s["node_made"], 1)
                sp.dma_start(io["row_of"].rearrange("(p n) a -> p (n a)", p=125), node[:, :]).then_inc(s["node_stored"], 16)
                sp.wait_ge(s["node_stored"], 16)
                sp.wait_ge(s["ends_loaded"], 32)
                sp.wait_ge(s["marks_stored"], 32)

            @block.gpsimd
            def _(pool):
                pool.memset(attr[:, :, :], 0.0).then_inc(s["attr_zeroed"], 1)
                pool.iota(node[:, :], pattern=[[1, N // 125]], base=0, channel_multiplier=N // 125).then_inc(s["node_made"], 1)
                pool.memset(beside[:, :, :], -1).then_inc(s["beside_cleared"], 1)
                pool.iota(D["slot_row"][:, :], pattern=[[F, T]], base=N, channel_multiplier=1)

            @block.tensor
            def _(pe):
                pe.wait_ge(s["rows_converted"], 3)
                for n, rows in enumerate((dst_f, next_f, src_f)):
                    last = nc.tensor.transpose(p_cols[:, n, 0:T], rows[:, :], W["ident"][0:T, 0:T])
                last.then_inc(s["cols_transposed"], 1)

            @block.vector
            def _(dve):
                done = 0

                def chained(ins):
                    nonlocal done
                    done += 1
                    ins.then_inc(s["step_done"], 1)
                    dve.wait_ge(s["step_done"], done)

                for r in range(RELATIONS):
                    chained(nc.vector.memset(order[:, r:r + 1], float(RELATIONS - r)))
                dve.wait_ge(s["rows_loaded"], 48)
                for f, i in ((dst_f, dst_rows), (next_f, next_rows), (src_f, src_rows)):
                    nc.vector.tensor_copy(f[:, :], i[:, :]).then_inc(s["rows_converted"], 1)
                dve.wait_ge(s["beside_loaded"], 32)
                nc.vector.tensor_copy(beside_f[:, :], beside[:, :, :].rearrange("t s a -> t (s a)")).then_inc(s["beside_converted"], 1)
                dve.wait_ge(s["beside_converted"], 1)
                dve.wait_ge(s["rows_converted"], 3)
                for n, marks in enumerate((link_rows, back_rows)):
                    nc.vector.tensor_scalar(marks[:, :], dst_f[:, :], beside_f[:, n:n + 1], None, ALU.is_equal).then_inc(s["marks_full"], 1)
                dve.wait_ge(s["cols_transposed"], 1)
                nc.vector.tensor_copy(D["src_col"][:, :], p_cols[:, 2, 0:T])
                nc.vector.tensor_copy(D["dst_col"][:, :], p_cols[:, 0, 0:T]).then_inc(s["dst_col_full"], 1)
                dve.wait_ge(s["dst_col_full"], 1)
                chained(nc.vector.tensor_copy(next_col[:, :], p_cols[:, 1, 0:T]))
                chained(nc.vector.tensor_scalar(D["dst_read"][:, :], D["dst_col"][:, :], float(N - 1), None, ALU.min))
                chained(nc.vector.tensor_tensor(same_as_next[:, :], D["dst_col"][:, :], next_col[:, :], ALU.is_equal))
                chained(nc.vector.tensor_scalar(next_col[:, :], D["dst_col"][:, :], 1.0, None, ALU.add))
                chained(nc.vector.tensor_tensor(next_col[:, :], next_col[:, :], same_as_next[:, :], ALU.mult))
                chained(nc.vector.tensor_tensor(D["last_key"][:, :], D["dst_col"][:, :], next_col[:, :], ALU.subtract))
                chained(nc.vector.tensor_scalar(off[:, :], same_as_next[:, :], float(BEYOND), None, ALU.mult))
                chained(nc.vector.tensor_tensor(D["dst_write"][:, :], D["dst_col"][:, :], off[:, :], ALU.add))
                wide = lambda c: c[:, :].unsqueeze(2).to_broadcast([F, T, RELATIONS])
                dve.wait_ge(s["attr_loaded"], 32)
                chained(nc.vector.tensor_reduce(best[:, :], attr[:, :, :], AX.X, ALU.max))
                chained(nc.vector.tensor_tensor(score[:, :, :], attr[:, :, :], wide(best), ALU.is_equal))
                chained(nc.vector.tensor_tensor(score[:, :, :], score[:, :, :],
                                                order[:, :].unsqueeze(1).to_broadcast([F, T, RELATIONS]), ALU.mult))
                chained(nc.vector.tensor_reduce(best[:, :], score[:, :, :], AX.X, ALU.max))
                chained(nc.vector.tensor_tensor(D["relation"][:, :, :], score[:, :, :], wide(best), ALU.is_equal))
                dve.wait_ge(s["ends_loaded"], 32)
                chained(nc.vector.tensor_copy(D["end_keys"][:, :, :], end_keys_apart[:, :, :].rearrange("h s t -> h t s")))


class RowMap:

    def __init__(self, nc, m, io, D):
        self.nc, self.io, self.D = nc, io, D
        self.index, self.value = ([m.sb(f"map_{n}{u}", [F, 1], i32) for u in range(UNROLL)] for n in ("index", "value"))
        self.moves = D["moves"]
        self.ready, self.kept, self.taken = m.sem("map_index_ready"), m.sem("map_value_kept"), m.sem("map_waits_taken")

    def prepare_scatter(self, pool, j, u):
        wait(pool, self.moves.sems[u], self.moves.after(j))
        pool.tensor_copy(self.index[u][:, :], column(self.D["dst_write"], (j, u))).then_inc(self.ready, 1)
        pool.tensor_copy(self.value[u][:, :], column(self.D["slot_row"], (j, u))).then_inc(self.ready, 1)

    def scatter(self, pool, j, u):
        pool.wait_ge(self.ready, 2 * (UNROLL * j + u) + 2)
        take_waits(pool, self.taken)
        pool.indirect_dma_start(out=self.io["row_of"], out_offset=bass.IndirectOffsetOnAxis(ap=self.index[u][:, 0:1], axis=0),
                                in_=self.value[u][:, :], in_offset=None, bounds_check=N - 1,
                                oob_is_err=False).then_inc(self.moves.sems[u], 16)

    def prepare_gather(self, pool, j, u):
        wait(pool, self.kept, UNROLL * j + u - UNROLL + 1)
        pool.tensor_copy(self.index[u][:, :], column(self.D["src_col"], (j, u))).then_inc(self.ready, 1)

    def gather(self, pool, j, u):
        pool.wait_ge(self.ready, UNROLL * j + u + 1)
        take_waits(pool, self.taken)
        pool.indirect_dma_start(out=self.value[u][:, :], out_offset=None, in_=self.io["row_of"],
                                in_offset=bass.IndirectOffsetOnAxis(ap=self.index[u][:, 0:1], axis=0)).then_inc(self.moves.sems[u], 16)

    def keep(self, pool, ref):
        j, u = ref
        pool.wait_ge(self.moves.sems[u], self.moves.after(j + 1))
        pool.tensor_copy(column(self.D["src_row"], ref), self.value[u][:, :]).then_inc(self.kept, 1)


def gather_rows(pool, taken, table, index_of, index, index_ready, rows, gathered, rows_used, j, u, place=lambda ref: ref):
    if (ref := at(j, u, 1)) is not None:
        wait(pool, rows_used, tile(ref) - UNROLL + 1)
        pool.wait_ge(index_ready, tile(ref) + 1)
        take_waits(pool, taken)
        v = ref[1]
        pool.indirect_dma_start(out=rows[v][:, :], out_offset=None, in_=table,
                                in_offset=bass.IndirectOffsetOnAxis(ap=index[v][:, 0:1], axis=0)).then_inc(gathered.sems[v], 16)
    if (ref := at(j, u, 0)) is not None:
        wait(pool, gathered.sems[u], gathered.after(j))
        take_waits(pool, taken)
        pool.tensor_copy(index[u][:, :], column(index_of, place(ref))).then_inc(index_ready, 1)


def attention_messages(nc, io, W, D):
    with Phase(nc) as m:
        index, index_d = ([m.sb(f"{n}{u}", [F, 1], i32) for u in range(UNROLL)] for n in ("index_s", "index_d"))
        xs, xd = ([m.sb(f"{n}{u}", [F, F]) for u in range(UNROLL)] for n in ("xs", "xd"))
        xT = [m.sb(f"xT{u}", [F, 2, F]) for u in range(2)]
        qk = [m.sb(f"qk{u}", [F, 2, F]) for u in range(2)]
        prod = m.sb("prod", [F, F])
        p_xT = [m.pb(f"p_xT{u}", [F, 2, F]) for u in range(2)]
        p_qkvy = [m.pb(f"p_qkvy{u}", [F, 4, F]) for u in range(2)]
        got_s, got_d = D["moves"], D["dst_moves"]
        s = m.named("waits_taken xs_index_ready xd_index_ready xT_transposed xT_full qkvy_full qk_full v_kept y_kept prod_full scores_full "
                    "drow_loaded")
        with nc.Block() as block:

            @block.sync
            def _(sp):
                sp.dma_start(D["drow"][:, :], row_vector(io["dst_f"])).then_inc(s["drow_loaded"], 16)
                sp.wait_ge(s["drow_loaded"], 16)

            @block.gpsimd
            def _(pool):
                def step(j, u):
                    gather_rows(pool, s["waits_taken"], io["x"], D["src_col"], index, s["xs_index_ready"], xs, got_s, s["xT_transposed"], j, u)
                    gather_rows(pool, s["waits_taken"], io["x"], D["dst_read"], index_d, s["xd_index_ready"], xd, got_d, s["xT_transposed"], j, u)
                over_all_tiles(pool, step, 1)

            @block.tensor
            def _(pe):
                def step(j, u):
                    if (ref := at(j, u, 0)) is not None:
                        t = tile(ref)
                        pe.wait_ge(got_s.sems[u], got_s.after(j + 1))
                        pe.wait_ge(got_d.sems[u], got_d.after(j + 1))
                        wait(pe, s["xT_full"], t - 1)
                        nc.tensor.transpose(p_xT[u % 2][:, 0, :], xs[u][:, :], W["ident"][:, :])
                        nc.tensor.transpose(p_xT[u % 2][:, 1, :], xd[u][:, :], W["ident"][:, :]).then_inc(s["xT_transposed"], 1)
                    if (ref := at(j, u, 1)) is not None:
                        t, v = tile(ref), ref[1] % 2
                        pe.wait_ge(s["xT_full"], t + 1)
                        wait(pe, s["qk_full"], t - 1)
                        wait(pe, s["v_kept"], t - 1)
                        wait(pe, s["y_kept"], t - 1)
                        nc.tensor.matmul(p_qkvy[v][:, 1:3, :], xT[v][:, 0, :], W["Wkv"][:, :, :], start=True, stop=True)
                        nc.tensor.matmul(p_qkvy[v][:, 0, :], xT[v][:, 1, :], W["Wq"][:, :], start=True, stop=True)
                        nc.tensor.matmul(p_qkvy[v][:, 3, :], xT[v][:, 1, :], W["Wsc"][:, :], start=True, stop=True).then_inc(s["qkvy_full"], 1)
                over_all_tiles(pe, step, 1)

            @block.scalar
            def _(act):
                def step(j, u):
                    t = UNROLL * j + u
                    act.wait_ge(s["xT_transposed"], t + 1)
                    wait(act, s["qkvy_full"], t - 1)
                    nc.scalar.copy(xT[u % 2][:, :, :], p_xT[u % 2][:, 0:2, :]).then_inc(s["xT_full"], 1)
                over_all_tiles(act, step, 0)

            @block.vector
            def _(dve):
                def step(j, u):
                    t, v = UNROLL * j + u, u % 2
                    dve.wait_ge(s["qkvy_full"], t + 1)
                    wait(dve, s["prod_full"], t - 1)
                    nc.vector.tensor_tensor(qk[v][:, :, :], p_qkvy[v][:, 0:2, :], W["bqk"][:, :, :], ALU.add).then_inc(s["qk_full"], 1)
                    nc.vector.tensor_tensor(plane(D["R"], (j, u), 0, F), p_qkvy[v][:, 2, :], W["bv"][:, :], ALU.add).then_inc(s["v_kept"], 1)
                    nc.vector.tensor_tensor(plane(D["Y"], (j, u), 0, F), p_qkvy[v][:, 3, :], W["bsc"][:, :], ALU.add).then_inc(s["y_kept"], 1)
                    dve.wait_ge(s["qk_full"], t + 1)
                    wait(dve, s["scores_full"], t)
                    nc.vector.tensor_tensor(prod[:, :], qk[v][:, 0, :], qk[v][:, 1, :], ALU.mult).then_inc(s["prod_full"], 1)
                    dve.wait_ge(s["prod_full"], t + 1)
                    nc.vector.tensor_reduce(plane(D["scores"], (j, u), 0, HEADS), prod[:, :].rearrange("p (h d) -> p h d", h=HEADS),
                                            AX.X, ALU.add).then_inc(s["scores_full"], 1)
                over_all_tiles(dve, step, 0)
        got_s.passes += PASSES
        got_d.passes += PASSES


def weights_of_edges(nc, io, W, D, scale):
    P = BLOCK * HEADS
    with Phase(nc) as m:
        top, keys = m.sb("top", [P, BLOCKS, F]), m.sb("keys", [P, BLOCKS, F])
        fresh = m.sb("fresh", [P, BLOCKS * F + 1])
        off_first, off_last = fresh[:, 0:BLOCKS * F].rearrange("p (b e) -> p b e", e=F), keys
        keys8 = m.sb("keys8", [F, T, HEADS])
        ends, ends_out = m.sb("max_ends", [P, BLOCKS, 2]), m.sb("max_ends_out", [P, BLOCKS, 2])
        row = m.sb("row", [HEADS, 2 * T])
        row_fresh = m.sb("row_fresh", [HEADS, 2 * T + 1])
        p_sT, p_kT = m.pb("p_sT", [F, 12, F]), m.pb("p_kT", [F, 12, F])
        p_back = [m.pb(f"p_back{n}", [F, 512]) for n in range(2)]
        s = m.named("keys8_full scores_transposed keys_transposed step_done ends_ready ends_stored row_loaded row_ready row_stored "
                    "ends_loaded top_ready top_back shifted weights_ready")
        half = BLOCKS // 2
        with nc.Block() as block:

            @block.tensor
            def _(pe):
                pe.wait_ge(s["keys8_full"], 1)
                for src, out, done in ((D["scores"], p_sT, "scores_transposed"), (keys8, p_kT, "keys_transposed")):
                    for b in range(BLOCKS):
                        part = src[:, b * BLOCK:(b + 1) * BLOCK, :].rearrange("p t h -> p (t h)")
                        last = nc.tensor.transpose(out[0:P, b, :], part, W["ident"][:, :])
                    last.then_inc(s[done], 1)
                pe.wait_ge(s["top_ready"], 1)
                for b in range(BLOCKS):
                    at_ = (b % half) * P
                    last = nc.tensor.transpose(p_back[b // half][:, at_:at_ + P], top[:, b, :], W["ident"][0:P, 0:P])
                last.then_inc(s["top_back"], 1)

            @block.sync
            def _(sp):
                by_block = io["max_ends"].rearrange("(b p s) -> p b s", b=BLOCKS, s=2)
                by_head = io["max_ends"].rearrange("(t h s) -> h t s", h=HEADS, s=2)
                by_head2 = io["max_ends_out"].rearrange("(t h s) -> h t s", h=HEADS, s=2)
                by_block2 = io["max_ends_out"].rearrange("(b p s) -> p b s", b=BLOCKS, s=2)
                sp.wait_ge(s["ends_ready"], 2)
                sp.dma_start(by_block, ends[:, :, :]).then_inc(s["ends_stored"], 16)
                sp.wait_ge(s["ends_stored"], 16)
                sp.dma_start(row[:, :].rearrange("h (t s) -> h t s", s=2), by_head).then_inc(s["row_loaded"], 16)
                sp.wait_ge(s["row_ready"], 1)
                sp.dma_start(by_head2, row[:, :].rearrange("h (t s) -> h t s", s=2)).then_inc(s["row_stored"], 16)
                sp.wait_ge(s["row_stored"], 16)
                sp.dma_start(ends_out[:, :, :], by_block2).then_inc(s["ends_loaded"], 16)

            @block.vector
            def _(dve):
                done = 0

                def chained(ins):
                    nonlocal done
                    done += 1
                    ins.then_inc(s["step_done"], 1)
                    dve.wait_ge(s["step_done"], done)

                nc.vector.tensor_copy(keys8[:, :, :], D["dst_col"][:, :].unsqueeze(2).to_broadcast([F, T, HEADS])).then_inc(s["keys8_full"], 1)
                row_keys = D["end_keys"][:, :, :].rearrange("h t s -> h (t s)")
                chained(nc.vector.memset(row_fresh[:, :], 0.0))
                chained(nc.vector.tensor_tensor(row_fresh[:, 1:2 * T], row_keys[:, 1:2 * T], row_keys[:, 0:2 * T - 1], ALU.is_equal))
                chained(nc.vector.tensor_scalar(row_fresh[:, :], row_fresh[:, :], -1.0, FAR, ALU.add, ALU.mult))
                dve.wait_ge(s["keys_transposed"], 1)
                chained(nc.vector.tensor_copy(keys[:, :, :], p_kT[0:P, 0:BLOCKS, :]))
                flat = lambda t: t[:, :, :].rearrange("p b e -> p (b e)")
                W_ = BLOCKS * F
                chained(nc.vector.memset(fresh[:, :], 0.0))
                chained(nc.vector.tensor_tensor(fresh[:, 1:W_], flat(keys)[:, 1:W_], flat(keys)[:, 0:W_ - 1], ALU.is_equal))
                chained(nc.vector.memset(fresh[:, 0:W_].rearrange("p (b e) -> p b e", e=F)[:, :, 0:1], 0.0))
                chained(nc.vector.tensor_scalar(fresh[:, :], fresh[:, :], -1.0, FAR, ALU.add, ALU.mult))
                dve.wait_ge(s["scores_transposed"], 1)
                chained(nc.vector.tensor_tensor_scan(flat(top), fresh[:, 0:W_], p_sT[0:P, 0:BLOCKS, :].rearrange("p b e -> p (b e)"),
                                                     -FAR, ALU.add, ALU.max))
                chained(nc.vector.tensor_tensor_scan(flat(top)[:, ::-1], fresh[:, 1:W_ + 1][:, ::-1], flat(top)[:, ::-1], -FAR, ALU.add, ALU.max))
                nc.vector.tensor_copy(ends[:, :, 0:1], top[:, :, 0:1]).then_inc(s["ends_ready"], 1)
                nc.vector.tensor_copy(ends[:, :, 1:2], top[:, :, F - 1:F]).then_inc(s["ends_ready"], 1)
                for out, e in ((off_first, 0), (off_last, F - 1)):
                    chained(nc.vector.tensor_tensor(out[:, :, :], keys[:, :, :], keys[:, :, e:e + 1].to_broadcast([P, BLOCKS, F]), ALU.is_equal))
                    chained(nc.vector.tensor_scalar(out[:, :, :], out[:, :, :], -1.0, FAR, ALU.add, ALU.mult))
                dve.wait_ge(s["row_loaded"], 16)
                chained(nc.vector.tensor_tensor_scan(row[:, :], row_fresh[:, 0:2 * T], row[:, :], -FAR, ALU.add, ALU.max))
                nc.vector.tensor_tensor_scan(row[:, ::-1], row_fresh[:, 1:2 * T + 1][:, ::-1], row[:, ::-1], -FAR,
                                             ALU.add, ALU.max).then_inc(s["row_ready"], 1)
                dve.wait_ge(s["ends_loaded"], 16)
                for off, n in ((off_first, 0), (off_last, 1)):
                    chained(nc.vector.tensor_tensor(off[:, :, :], off[:, :, :], ends_out[:, :, n:n + 1].to_broadcast([P, BLOCKS, F]), ALU.add))
                    chained(nc.vector.tensor_tensor(top[:, :, :], top[:, :, :], off[:, :, :], ALU.max))
                nc.vector.tensor_copy(ends[:, :, 0:1], top[:, :, 0:1]).then_inc(s["top_ready"], 1)
                dve.wait_ge(s["top_back"], 1)
                for n in range(2):
                    part = D["scores"][:, n * T // 2:(n + 1) * T // 2, :].rearrange("p t h -> p (t h)")
                    nc.vector.tensor_tensor(part, part, p_back[n][:, 0:half * P], ALU.subtract).then_inc(s["shifted"], 1)

            @block.scalar
            def _(act):
                act.wait_ge(s["shifted"], 2)
                act.activation(D["scores"][:, :, :], D["scores"][:, :, :], ACT.Exp, scale=scale).then_inc(s["weights_ready"], 1)


def mark_same(dve, nc, D, same, used, s, ref):
    t, v = tile(ref), ref[1] % 2
    wait(dve, used, t - 1)
    nc.vector.tensor_scalar(same[v][:, :], D["drow"][:, bass.ds(t * F, F)], column(D["dst_col"], ref), None, ALU.is_equal).then_inc(s["same_full"], 1)


def clear_link(pool, link, s):
    for m in link:
        pool.memset(m[:, :], 0.0).then_inc(s["link_cleared"], 1)


def load_link(sp, row, link, slot, used, s, ref):
    u = ref[1]
    if isinstance(ref[0], int) and ref == (0, 0):
        sp.wait_ge(s["link_cleared"], UNROLL)
    wait(sp, used, tile(ref) - UNROLL + 1)
    take_waits(sp, s["link_waits_taken"])
    sp.dma_start(link[u][slot:slot + 1, :], row).then_inc(s[f"link_loaded{u}"], 16)


def store_pass(sp, taken, table, src, ready, stored, ref):
    j, u = ref
    if u == UNROLL - 1:
        sp.wait_ge(ready, UNROLL * (j + 1))
        take_waits(sp, taken)
        sp.dma_start(table[bass.ds(N + j * (UNROLL * F), UNROLL * F), :].rearrange("(t p) f -> p t f", p=F),
                     src[:, bass.ds(j * UNROLL, UNROLL), :]).then_inc(stored, 16)


def sum_to_here(pe, nc, p_sum, same, link, values, whole, width, s, ref):
    t, v = tile(ref), ref[1] % 2
    pe.wait_ge(s["same_full"], t + 1)
    pe.wait_ge(s[f"link_loaded{ref[1]}"], 16 * (ref[0] + 1))
    wait(pe, s["whole_full"], t - 1)
    first = isinstance(t, int) and t == 0
    last = nc.tensor.matmul(p_sum[v][:, 0:width], same[v][:, :], values, start=True, stop=first)
    if not first:
        wait(pe, s["whole_full"], t)
        last = nc.tensor.matmul(p_sum[v][:, 0:width], link[ref[1]][:, :], whole[1 - v][:, 0:width], start=False, stop=True)
    last.then_inc(s["summed"], 1)


LINKS = "link_cleared link_waits_taken " + " ".join(f"link_loaded{u}" for u in range(UNROLL)) + " "
SUMS = LINKS + "same_full summed whole_full "
NORM = "norm_waits_taken stats_full moments_full moments_kept dev_full inverse_dev_full normal_full "


def sum_memory(m, width):
    some = lambda name, w, k: [m.sb(f"{name}{u}", [F, w]) for u in range(k)]
    return some("same", F, 2), some("link", F, UNROLL), some("whole", width, 2), [m.pb(f"p_sum{u}", [F, 512]) for u in range(2)]


class Norm:

    def __init__(self, nc, m, W, s):
        self.nc, self.W, self.s = nc, W, s
        self.stats = [m.sb(f"norm_stats{u}", [F, 6]) for u in range(2)]
        self.moments, self.kept = (m.sb(f"norm_{n}", [F, UNROLL, 2]) for n in ("moments", "moments_kept"))
        self.dev, self.inverse = (m.sb(f"norm_{n}", [F, UNROLL]) for n in ("dev", "inverse"))

    def statistics(self, dve, y, ready, ref):
        t, v = tile(ref), ref[1] % 2
        dve.wait_ge(ready, t + 1)
        wait(dve, self.s["moments_full"], t - 1)
        take_waits(dve, self.s["norm_waits_taken"])
        self.nc.vector.bn_stats(self.stats[v][:, :], y).then_inc(self.s["stats_full"], 1)

    def aggregate(self, dve, ref):
        s, (j, u) = self.s, ref
        dve.wait_ge(s["stats_full"], tile(ref) + 1)
        wait(dve, s["moments_kept"], j)
        take_waits(dve, s["norm_waits_taken"])
        self.nc.vector.bn_aggr(self.moments[:, u, :], self.stats[u % 2][:, :]).then_inc(s["moments_full"], 1)

    def keep(self, dve, ref):
        s, (j, u) = self.s, ref
        if u == UNROLL - 1:
            dve.wait_ge(s["moments_full"], UNROLL * j + UNROLL)
            wait(dve, s["normal_full"], UNROLL * j)
            wait(dve, s["dev_full"], j)
            self.nc.vector.tensor_copy(self.kept[:, :, :], self.moments[:, :, :]).then_inc(s["moments_kept"], 1)

    def deviation(self, act, ref):
        s, (j, u) = self.s, ref
        if u == UNROLL - 1:
            act.wait_ge(s["moments_kept"], j + 1)
            wait(act, s["inverse_dev_full"], j)
            self.nc.scalar.activation(self.dev[:, :], self.kept[:, :, 1:2].rearrange("p t a -> p (t a)"), ACT.Sqrt,
                                      bias=self.W["eps"][:, :]).then_inc(s["dev_full"], 1)

    def rows_of(self, dve, out, y, ref):
        s, (j, u) = self.s, ref
        dve.wait_ge(s["inverse_dev_full"], j + 1)
        self.nc.vector.tensor_scalar(out, y, self.kept[:, u, 0:1], self.inverse[:, u:u + 1], ALU.subtract, ALU.mult).then_inc(s["normal_full"], 1)

    def invert(self, dve, ref):
        s, (j, u) = self.s, ref
        if u == 0:
            dve.wait_ge(s["dev_full"], j + 1)
            wait(dve, s["normal_full"], UNROLL * j)
            self.nc.vector.reciprocal(self.inverse[:, :], self.dev[:, :]).then_inc(s["inverse_dev_full"], 1)


def weighted(pool, nc, D, message, heads, s, ref):
    t, v = tile(ref), ref[1] % 2
    by_head = lambda a: a.rearrange("p (h d) -> p h d", h=heads)
    wait(pool, s["summed"], t - 1)
    nc.gpsimd.tensor_tensor(by_head(message[v][:, 0:F]), by_head(plane(D["R"], ref, 0, F)),
                            plane(D["scores"], ref, 0, heads).unsqueeze(2).to_broadcast([F, heads, F // heads]),
                            ALU.mult).then_inc(s["weighted"], 1)


def attention_rows(nc, io, W, D):
    width = F + HEADS + RELATIONS
    with Phase(nc) as m:
        same, link, whole, p_sum = sum_memory(m, width)
        message = [m.sb(f"message{u}", [F, width]) for u in range(2)]
        inverse, mean = m.sb("inverse", [F, HEADS]), [m.sb(f"mean_value{u}", [F, F]) for u in range(2)]
        deg, root = m.sb("deg", [F, UNROLL]), m.sb("root", [F, UNROLL])
        s = m.named(SUMS + NORM + "weighted joined inverse_full mean_full y_full deg_full root_full dinv_full count_kept scaled_full stored")
        norm = Norm(nc, m, W, s)
        row_map = RowMap(nc, m, io, D)
        by_head = lambda a: a.rearrange("p (h d) -> p h d", h=HEADS)
        with nc.Block() as block:

            @block.gpsimd
            def _(pool):
                clear_link(pool, link, s)

                def step(j, u):
                    if (ref := at(j, u, 0)) is not None:
                        row_map.prepare_gather(pool, j, u)
                        weighted(pool, nc, D, message, HEADS, s, ref)
                        row_map.gather(pool, j, u)
                    if (ref := at(j, u, 3)) is not None:
                        row_map.keep(pool, ref)
                over_all_tiles(pool, step, 3)

            @block.tensor
            def _(pe):
                def step(j, u):
                    if (ref := at(j, u, 1)) is not None:
                        pe.wait_ge(s["weighted"], tile(ref) + 1)
                        pe.wait_ge(s["joined"], 2 * tile(ref) + 2)
                        sum_to_here(pe, nc, p_sum, same, link, message[ref[1] % 2][:, :], whole, width, s, ref)
                over_all_tiles(pe, step, 1)

            @block.scalar
            def _(act):
                def step(j, u):
                    if (ref := at(j, u, 3)) is not None and ref[1] == UNROLL - 1:
                        act.wait_ge(s["deg_full"], tile(ref) + 1)
                        wait(act, s["dinv_full"], ref[0])
                        act.activation(root[:, :], deg[:, :], ACT.Sqrt, bias=W["one"][:, :]).then_inc(s["root_full"], 1)
                    if (ref := at(j, u, 0)) is not None:
                        wait(act, s["summed"], tile(ref) - 1)
                        act.copy(message[u % 2][:, F:F + HEADS], plane(D["scores"], ref, 0, HEADS)).then_inc(s["joined"], 1)
                        act.copy(message[u % 2][:, F + HEADS:width], plane(D["relation"], ref, 0, RELATIONS)).then_inc(s["joined"], 1)
                    if (ref := at(j, u, 4)) is not None:
                        norm.deviation(act, ref)
                    if (ref := at(j, u, 2)) is not None:
                        act.wait_ge(s["whole_full"], tile(ref) + 1)
                        act.copy(plane(D["count"], ref, 0, RELATIONS), whole[ref[1] % 2][:, F + HEADS:width]).then_inc(s["count_kept"], 1)
                    if (ref := at(j, u, 9)) is not None:
                        act.wait_ge(s["normal_full"], tile(ref) + 1)
                        act.wait_ge(s["dinv_full"], ref[0] + 1)
                        act.activation(plane(D["R"], ref, 0, F), plane(D["Y"], ref, 0, F), ACT.Copy, scale=column(D["dinv"], ref)).then_inc(s["scaled_full"], 1)
                    if (ref := at(j, u, 1)) is not None:
                        t, v = tile(ref), ref[1] % 2
                        act.wait_ge(s["summed"], t + 1)
                        wait(act, s["mean_full"], t - 1)
                        wait(act, s["deg_full"], t - 1)
                        wait(act, s["count_kept"], t - 1)
                        act.copy(whole[v][:, :], p_sum[v][:, 0:width]).then_inc(s["whole_full"], 1)
                over_all_tiles(act, step, 9)

            @block.vector
            def _(dve):
                def step(j, u):
                    if (ref := at(j, u, 8)) is not None:
                        norm.invert(dve, ref)
                    if (ref := at(j, u, 3)) is not None:
                        y = plane(D["Y"], ref, 0, F)
                        dve.wait_ge(s["mean_full"], tile(ref) + 1)
                        nc.vector.tensor_tensor(y, y, mean[ref[1] % 2][:, :], ALU.add).then_inc(s["y_full"], 1)
                    if (ref := at(j, u, 2)) is not None:
                        t, v = tile(ref), ref[1] % 2
                        dve.wait_ge(s["whole_full"], t + 1)
                        wait(dve, s["mean_full"], t)
                        nc.vector.reciprocal(inverse[:, :], whole[v][:, F:F + HEADS]).then_inc(s["inverse_full"], 1)
                    if (ref := at(j, u, 8)) is not None:
                        y = plane(D["Y"], ref, 0, F)
                        norm.rows_of(dve, y, y, ref)
                    if (ref := at(j, u, 4)) is not None:
                        norm.keep(dve, ref)
                    if (ref := at(j, u, 3)) is not None:
                        norm.statistics(dve, plane(D["Y"], ref, 0, F), s["y_full"], ref)
                    if (ref := at(j, u, 2)) is not None:
                        t, v = tile(ref), ref[1] % 2
                        dve.wait_ge(s["inverse_full"], t + 1)
                        wait(dve, s["y_full"], t - 1)
                        nc.vector.tensor_tensor(by_head(mean[v][:, :]), by_head(whole[v][:, 0:F]),
                                                inverse[:, :].unsqueeze(2).to_broadcast([F, HEADS, F // HEADS]), ALU.mult).then_inc(s["mean_full"], 1)
                    if (ref := at(j, u, 0)) is not None:
                        mark_same(dve, nc, D, same, s["summed"], s, ref)
                    if (ref := at(j, u, 2)) is not None:
                        v = ref[1] % 2
                        wait(dve, s["root_full"], ref[0])
                        nc.vector.tensor_reduce(deg[:, ref[1]:ref[1] + 1], whole[v][:, F + HEADS:width], AX.X, ALU.add).then_inc(s["deg_full"], 1)
                    if (ref := at(j, u, 3)) is not None:
                        norm.aggregate(dve, ref)
                    if (ref := at(j, u, 4)) is not None and ref[1] == UNROLL - 1:
                        dve.wait_ge(s["root_full"], ref[0] + 1)
                        nc.vector.reciprocal(D["dinv"][:, bass.ds(ref[0] * UNROLL, UNROLL)], root[:, :]).then_inc(s["dinv_full"], 1)
                over_all_tiles(dve, step, 8)

            @block.sync
            def _(sp):
                def step(j, u):
                    if (ref := at(j, u, 0)) is not None:
                        load_link(sp, io["link_rows"][bass.ds(tile(ref), 1), :], link, F - 1, s["summed"], s, ref)
                    if (ref := at(j, u, 13)) is not None:
                        store_pass(sp, s["link_waits_taken"], io["Z1"], D["R"], s["scaled_full"], s["stored"], ref)
                over_all_tiles(sp, step, 13)
                sp.wait_ge(s["stored"], 16 * PASSES)
        D["moves"].passes += PASSES


def hidden_rows(nc, io, W, D):
    with Phase(nc) as m:
        same, link, whole, p_sum = sum_memory(m, F)
        rows, index = [m.sb(f"rows{u}", [F, F]) for u in range(UNROLL)], [m.sb(f"index{u}", [F, 1], i32) for u in range(UNROLL)]
        mid, inner, innerT = ([m.sb(f"{n}{u}", [F, F]) for u in range(2)] for n in ("mid", "inner", "innerT"))
        gT = [m.sb(f"gT{u}", [F, 2, F]) for u in range(2)]
        p_T = [m.pb(f"p_T{u}", [F, 512]) for u in range(2)]
        p_g = [m.pb(f"p_g{u}", [F, 4, F]) for u in range(2)]
        p_out = [m.pb(f"p_out{u}", [F, 512]) for u in range(2)]
        gathered = D["moves"]
        s = m.named(SUMS + "waits_taken index_ready mid_full inner_full inner_transposed innerT_full g_multiplied gT_full "
                    "out_multiplied z_full y_full y_biased stored")
        with nc.Block() as block:

            @block.gpsimd
            def _(pool):
                clear_link(pool, link, s)

                def step(j, u):
                    gather_rows(pool, s["waits_taken"], io["Z1"], D["src_row"], index, s["index_ready"], rows, gathered, s["summed"], j, u)
                over_all_tiles(pool, step, 1)

            @block.tensor
            def _(pe):
                def step(j, u):
                    if (ref := at(j, u, 1)) is not None:
                        pe.wait_ge(gathered.sems[ref[1]], gathered.after(ref[0] + 1))
                        sum_to_here(pe, nc, p_sum, same, link, rows[ref[1]][:, :], whole, F, s, ref)
                    if (ref := at(j, u, 6)) is not None:
                        t, v = tile(ref), ref[1] % 2
                        pe.wait_ge(s["gT_full"], t + 1)
                        wait(pe, s["z_full"], t - 1)
                        for k in range(2):
                            last = nc.tensor.matmul(p_out[v][:, 0:F], gT[v][:, k, :], W["W2c"][:, k, :], start=(k == 0), stop=(k == 1))
                        last.then_inc(s["out_multiplied"], 1)
                    if (ref := at(j, u, 5)) is not None:
                        t, v = tile(ref), ref[1] % 2
                        pe.wait_ge(s["innerT_full"], t + 1)
                        wait(pe, s["gT_full"], t - 1)
                        for k in range(2):
                            last = nc.tensor.matmul(p_g[v][:, k, :], W["W1"][:, k * F:(k + 1) * F], innerT[v][:, :], start=True, stop=True)
                        last.then_inc(s["g_multiplied"], 1)
                    if (ref := at(j, u, 4)) is not None:
                        t, v = tile(ref), ref[1] % 2
                        pe.wait_ge(s["inner_full"], t + 1)
                        wait(pe, s["innerT_full"], t - 1)
                        nc.tensor.transpose(p_T[v][:, 0:F], inner[v][:, :], W["ident"][:, :]).then_inc(s["inner_transposed"], 1)
                over_all_tiles(pe, step, 6)

            @block.scalar
            def _(act):
                def step(j, u):
                    if (ref := at(j, u, 1)) is not None:
                        t, v = tile(ref), ref[1] % 2
                        act.wait_ge(s["summed"], t + 1)
                        wait(act, s["mid_full"], t - 1)
                        act.copy(whole[v][:, :], p_sum[v][:, 0:F]).then_inc(s["whole_full"], 1)
                    if (ref := at(j, u, 5)) is not None:
                        t, v = tile(ref), ref[1] % 2
                        act.wait_ge(s["g_multiplied"], t + 1)
                        wait(act, s["out_multiplied"], t - 1)
                        for k in range(2):
                            last = act.activation(gT[v][:, k, :], p_g[v][:, k, :], ACT.Relu, bias=W["b_W1"][:, k:k + 1])
                        last.then_inc(s["gT_full"], 1)
                    if (ref := at(j, u, 4)) is not None:
                        t, v = tile(ref), ref[1] % 2
                        act.wait_ge(s["inner_transposed"], t + 1)
                        wait(act, s["g_multiplied"], t - 1)
                        act.copy(innerT[v][:, :], p_T[v][:, 0:F]).then_inc(s["innerT_full"], 1)
                over_all_tiles(act, step, 5)

            @block.vector
            def _(dve):
                def step(j, u):
                    if (ref := at(j, u, 2)) is not None:
                        t, v = tile(ref), ref[1] % 2
                        dve.wait_ge(s["whole_full"], t + 1)
                        wait(dve, s["inner_full"], t - 1)
                        nc.vector.scalar_tensor_tensor(out=mid[v][:, :], in0=plane(D["Y"], ref, 0, F), scalar=column(D["dinv"], ref), in1=whole[v][:, :],
                                                       op0=ALU.mult, op1=ALU.add).then_inc(s["mid_full"], 1)
                    if (ref := at(j, u, 7)) is not None:
                        dve.wait_ge(s["out_multiplied"], tile(ref) + 1)
                        nc.vector.tensor_scalar(plane(D["R"], ref, 0, F), p_out[ref[1] % 2][:, 0:F], column(D["dinv"], ref), None,
                                                ALU.mult).then_inc(s["z_full"], 1)
                    if (ref := at(j, u, 0)) is not None:
                        mark_same(dve, nc, D, same, s["summed"], s, ref)
                    if (ref := at(j, u, 3)) is not None:
                        t, v = tile(ref), ref[1] % 2
                        dve.wait_ge(s["mid_full"], t + 1)
                        wait(dve, s["inner_transposed"], t - 1)
                        nc.vector.tensor_scalar(inner[v][:, :], mid[v][:, :], column(D["dinv"], ref), None, ALU.mult).then_inc(s["inner_full"], 1)
                    if (ref := at(j, u, 3)) is not None:
                        y = plane(D["Y"], ref, 0, F)
                        dve.wait_ge(s["mid_full"], tile(ref) + 1)
                        nc.vector.tensor_tensor(y, y, W["b2c"][:, :], ALU.add).then_inc(s["y_biased"], 1)
                    if (ref := at(j, u, 7)) is not None:
                        t, y = tile(ref), plane(D["Y"], ref, 0, F)
                        dve.wait_ge(s["z_full"], t + 1)
                        dve.wait_ge(s["y_biased"], t + 1)
                        nc.vector.scalar_tensor_tensor(out=y, in0=plane(D["R"], ref, 0, F), scalar=column(D["dinv"], ref), in1=y,
                                                       op0=ALU.mult, op1=ALU.add).then_inc(s["y_full"], 1)
                over_all_tiles(dve, step, 7)

            @block.sync
            def _(sp):
                def step(j, u):
                    if (ref := at(j, u, 0)) is not None:
                        load_link(sp, io["link_rows"][bass.ds(tile(ref), 1), :], link, F - 1, s["summed"], s, ref)
                    if (ref := at(j, u, 11)) is not None:
                        store_pass(sp, s["link_waits_taken"], io["H2"], D["R"], s["z_full"], s["stored"], ref)
                over_all_tiles(sp, step, 11)
                sp.wait_ge(s["stored"], 16 * PASSES)
        gathered.passes += PASSES


def output_rows(nc, io, W, D):
    with Phase(nc) as m:
        same, link, whole, p_sum = sum_memory(m, F)
        rows, index = [m.sb(f"rows{u}", [F, F]) for u in range(UNROLL)], [m.sb(f"index{u}", [F, 1], i32) for u in range(UNROLL)]
        gathered = D["moves"]
        s = m.named(SUMS + NORM + "waits_taken index_ready y_full stored")
        norm = Norm(nc, m, W, s)
        with nc.Block() as block:

            @block.gpsimd
            def _(pool):
                clear_link(pool, link, s)

                over_all_tiles(pool, lambda j, u: gather_rows(pool, s["waits_taken"], io["H2"], D["src_row"], index, s["index_ready"], rows,
                                                              gathered, s["summed"], j, u), 1)

            @block.tensor
            def _(pe):
                def step(j, u):
                    if (ref := at(j, u, 1)) is not None:
                        pe.wait_ge(gathered.sems[ref[1]], gathered.after(ref[0] + 1))
                        sum_to_here(pe, nc, p_sum, same, link, rows[ref[1]][:, :], whole, F, s, ref)
                over_all_tiles(pe, step, 1)

            @block.scalar
            def _(act):
                def step(j, u):
                    if (ref := at(j, u, 3)) is not None:
                        norm.deviation(act, ref)
                    if (ref := at(j, u, 1)) is not None:
                        t, v = tile(ref), ref[1] % 2
                        act.wait_ge(s["summed"], t + 1)
                        wait(act, s["y_full"], t - 1)
                        act.copy(whole[v][:, :], p_sum[v][:, 0:F]).then_inc(s["whole_full"], 1)
                over_all_tiles(act, step, 3)

            @block.vector
            def _(dve):
                def step(j, u):
                    if (ref := at(j, u, 7)) is not None:
                        norm.invert(dve, ref)
                    if (ref := at(j, u, 2)) is not None:
                        t, v, y = tile(ref), ref[1] % 2, plane(D["Y"], ref, 0, F)
                        dve.wait_ge(s["whole_full"], t + 1)
                        nc.vector.scalar_tensor_tensor(out=y, in0=whole[v][:, :], scalar=column(D["dinv"], ref), in1=y,
                                                       op0=ALU.mult, op1=ALU.add).then_inc(s["y_full"], 1)
                    if (ref := at(j, u, 0)) is not None:
                        mark_same(dve, nc, D, same, s["summed"], s, ref)
                    if (ref := at(j, u, 2)) is not None:
                        norm.statistics(dve, plane(D["Y"], ref, 0, F), s["y_full"], ref)
                    if (ref := at(j, u, 7)) is not None:
                        y = plane(D["Y"], ref, 0, F)
                        norm.rows_of(dve, y, y, ref)
                    if (ref := at(j, u, 3)) is not None:
                        norm.keep(dve, ref)
                    if (ref := at(j, u, 2)) is not None:
                        norm.aggregate(dve, ref)
                over_all_tiles(dve, step, 7)

            @block.sync
            def _(sp):
                def step(j, u):
                    if (ref := at(j, u, 0)) is not None:
                        load_link(sp, io["link_rows"][bass.ds(tile(ref), 1), :], link, F - 1, s["summed"], s, ref)
                    if (ref := at(j, u, 11)) is not None:
                        store_pass(sp, s["link_waits_taken"], io["X2"], D["Y"], s["normal_full"], s["stored"], ref)
                over_all_tiles(sp, step, 11)
                sp.wait_ge(s["stored"], 16 * PASSES)
        gathered.passes += PASSES


def mirrored(ref):
    j, u = ref
    return (PASSES - 1) - j, UNROLL - 1 - u


def gat_messages(nc, io, W, D):
    H4 = GAT_HEADS
    w = H4 + RELATIONS
    with Phase(nc) as m:
        index = [m.sb(f"index{u}", [F, 1], i32) for u in range(UNROLL)]
        rows = [m.sb(f"rows{u}", [F, F]) for u in range(UNROLL)]
        own = [m.sb(f"own{u}", [F, F]) for u in range(2)]
        bothT = [m.sb(f"bothT{u}", [F, 2, F]) for u in range(2)]
        last, link = ([m.sb(f"{n}{u}", [F, F]) for u in range(k)] for n, k in (("last", 2), ("after", UNROLL)))
        held, spread = ([m.sb(f"{n}{u}", [F, c]) for u in range(k)] for n, c, k in (("held", H4 + w, UNROLL), ("spread", w, 2)))
        raw, at_least_one, inverse = m.sb("raw", [F, H4]), m.sb("at_least_one", [F, RELATIONS]), m.sb("inverse", [F, RELATIONS])
        p_T = [m.pb(f"p_T{u}", [F, 4, F]) for u in range(2)]
        p_h = [m.pb(f"p_h{u}", [F, 512]) for u in range(2)]
        p_spread = [m.pb(f"p_spread{u}", [F, 512]) for u in range(2)]
        gathered = D["moves"]
        s = m.named(LINKS + "waits_taken dve_waits_taken index_ready own_full transposed bothT_full multiplied h_kept counts_held scores_held last_full "
                    "spread_multiplied spread_full raw_full scores_full at_least_one_full inverse_full share_full twice")
        with nc.Block() as block:

            @block.gpsimd
            def _(pool):
                clear_link(pool, link, s)

                def step(j, u):
                    gather_rows(pool, s["waits_taken"], io["X2"], D["src_row"], index, s["index_ready"], rows, gathered, s["transposed"], j, u, mirrored)
                over_all_tiles(pool, step, 1)

            @block.sync
            def _(sp):
                def step(j, u):
                    load_link(sp, io["back_rows"][bass.ds(tile(mirrored((j, u))), 1), :], link, 0, s["spread_multiplied"], s, (j, u))
                over_all_tiles(sp, step, 0)

            @block.tensor
            def _(pe):
                def step(j, u):
                    if (ref := at(j, u, 1)) is not None:
                        t, v = tile(ref), ref[1] % 2
                        pe.wait_ge(gathered.sems[ref[1]], gathered.after(ref[0] + 1))
                        pe.wait_ge(s["own_full"], t + 1)
                        wait(pe, s["bothT_full"], t - 1)
                        nc.tensor.transpose(p_T[v][:, 0, :], rows[ref[1]][:, :], W["ident"][:, :])
                        nc.tensor.transpose(p_T[v][:, 1, :], own[v][:, :], W["ident"][:, :]).then_inc(s["transposed"], 1)
                    if (ref := at(j, u, 3)) is not None:
                        t, v = tile(ref), ref[1] % 2
                        pe.wait_ge(s["counts_held"], t + 1)
                        pe.wait_ge(s["scores_held"], t + 1)
                        pe.wait_ge(s["last_full"], t + 1)
                        pe.wait_ge(s[f"link_loaded{ref[1]}"], 16 * (ref[0] + 1))
                        wait(pe, s["spread_full"], t)
                        first = isinstance(t, int) and t == 0
                        step_ = nc.tensor.matmul(p_spread[v][:, 0:w], last[v][:, :], held[ref[1]][:, H4:H4 + w], start=True, stop=first)
                        if not first:
                            step_ = nc.tensor.matmul(p_spread[v][:, 0:w], link[ref[1]][:, :], spread[1 - v][:, :], start=False, stop=True)
                        step_.then_inc(s["spread_multiplied"], 1)
                    if (ref := at(j, u, 2)) is not None:
                        t, v = tile(ref), ref[1] % 2
                        pe.wait_ge(s["bothT_full"], t + 1)
                        wait(pe, s["h_kept"], t - 1)
                        nc.tensor.matmul(p_h[v][:, 0:F + H4], bothT[v][:, 0, :], W["Wgat_src"][:, :], start=True, stop=True)
                        nc.tensor.matmul(p_h[v][:, F + H4:F + 2 * H4], bothT[v][:, 1, :], W["w_dst"][:, :], start=True, stop=True).then_inc(s["multiplied"], 1)
                over_all_tiles(pe, step, 3)

            @block.scalar
            def _(act):
                def step(j, u):
                    if (ref := at(j, u, 0)) is not None:
                        wait(act, s["transposed"], tile(ref) - 1)
                        act.copy(own[u % 2][:, :], plane(D["Y"], mirrored(ref), 0, F)).then_inc(s["own_full"], 1)
                        wait(act, s["spread_multiplied"], tile(ref) - 3)
                        wait(act, s["raw_full"], tile(ref) - 3)
                        act.copy(held[u][:, 2 * H4:H4 + w], plane(D["count"], mirrored(ref), 0, RELATIONS)).then_inc(s["counts_held"], 1)
                    if (ref := at(j, u, 3)) is not None:
                        t, v = tile(ref), ref[1] % 2
                        act.wait_ge(s["spread_multiplied"], t + 1)
                        wait(act, s["raw_full"], t - 1)
                        wait(act, s["at_least_one_full"], t - 1)
                        act.copy(spread[v][:, :], p_spread[v][:, 0:w]).then_inc(s["spread_full"], 1)
                    if (ref := at(j, u, 2)) is not None:
                        t, v = tile(ref), ref[1] % 2
                        act.wait_ge(s["multiplied"], t + 1)
                        wait(act, s["spread_multiplied"], t - 3)
                        wait(act, s["raw_full"], t - 3)
                        act.copy(held[ref[1]][:, 0:2 * H4], p_h[v][:, F:F + 2 * H4]).then_inc(s["scores_held"], 1)
                        act.copy(plane(D["R"], mirrored(ref), 0, F), p_h[v][:, 0:F]).then_inc(s["h_kept"], 1)
                    if (ref := at(j, u, 1)) is not None:
                        t, v = tile(ref), ref[1] % 2
                        act.wait_ge(s["transposed"], t + 1)
                        wait(act, s["multiplied"], t - 1)
                        act.copy(bothT[v][:, :, :], p_T[v][:, 0:2, :]).then_inc(s["bothT_full"], 1)
                over_all_tiles(act, step, 3)

            @block.vector
            def _(dve):
                def step(j, u):
                    if (ref := at(j, u, 4)) is not None:
                        t, v, tile_ = tile(ref), ref[1] % 2, mirrored(ref)
                        dve.wait_ge(s["spread_full"], t + 1)
                        wait(dve, s["scores_full"], t)
                        nc.vector.tensor_tensor(raw[:, :], held[ref[1]][:, 0:H4], spread[v][:, 0:H4], ALU.add).then_inc(s["raw_full"], 1)
                        wait(dve, s["inverse_full"], t)
                        nc.vector.tensor_scalar(at_least_one[:, :], spread[v][:, H4:w], 1.0, None, ALU.max).then_inc(s["at_least_one_full"], 1)
                    if (ref := at(j, u, 2)) is not None:
                        t, v, tile_ = tile(ref), ref[1] % 2, mirrored(ref)
                        keys = D["drow"][:, bass.ds(tile(tile_) * F, F)]
                        wait(dve, s["spread_multiplied"], t - 1)
                        take_waits(dve, s["dve_waits_taken"])
                        nc.vector.tensor_scalar(last[v][:, :], keys, column(D["last_key"], tile_), None, ALU.is_equal).then_inc(s["last_full"], 1)
                    if (ref := at(j, u, 4)) is not None:
                        t, v, tile_ = tile(ref), ref[1] % 2, mirrored(ref)
                        dve.wait_ge(s["at_least_one_full"], t + 1)
                        wait(dve, s["share_full"], t)
                        nc.vector.reciprocal(inverse[:, :], at_least_one[:, :]).then_inc(s["inverse_full"], 1)
                        dve.wait_ge(s["raw_full"], t + 1)
                        take_waits(dve, s["dve_waits_taken"])
                        nc.vector.scalar_tensor_tensor(out=plane(D["scores"], tile_, 0, H4), in0=raw[:, :], scalar=ALPHA, in1=raw[:, :],
                                                       op0=ALU.mult, op1=ALU.max).then_inc(s["scores_full"], 1)
                    if (ref := at(j, u, 4)) is not None:
                        dve.wait_ge(s["inverse_full"], tile(ref) + 1)
                        take_waits(dve, s["dve_waits_taken"])
                        share = plane(D["relation"], mirrored(ref), 0, RELATIONS)
                        nc.vector.tensor_tensor(share, inverse[:, :], share, ALU.mult).then_inc(s["share_full"], 1)
                over_all_tiles(dve, step, 4)
                dve.wait_ge(s["scores_full"], T)
                nc.vector.tensor_copy(D["scores"][:, :, H4:HEADS], D["scores"][:, :, 0:H4]).then_inc(s["twice"], 1)
                dve.wait_ge(s["twice"], 1)
        gathered.passes += PASSES


def gat_rows(nc, io, W, D):
    H4 = GAT_HEADS
    width = F + H4
    with Phase(nc) as m:
        same, link, whole, p_sum = sum_memory(m, width)
        two = lambda name: [m.sb(f"{name}{u}", [F, F]) for u in range(2)]
        mean, low, grown, x3T = (two(n) for n in ("mean_h", "low", "grown", "x3T"))
        message = [m.sb(f"message{u}", [F, width]) for u in range(2)]
        x3 = [m.sb(f"x3_{u}", [F, F]) for u in range(UNROLL)]
        inverse = m.sb("inverse", [F, H4])
        p_T = [m.pb(f"p_T{u}", [F, 512]) for u in range(2)]
        p_root = [m.pb(f"p_root{u}", [F, 512]) for u in range(2)]
        s = m.named(SUMS + NORM + "weighted joined inverse_full mean_full low_full grown_full high_full y_full x3_kept stored x3_transposed x3T_full "
                    "root_multiplied root_full root_stored")
        norm = Norm(nc, m, W, s)
        by_head = lambda a: a.rearrange("p (h d) -> p h d", h=H4)
        with nc.Block() as block:

            @block.gpsimd
            def _(pool):
                clear_link(pool, link, s)

                def step(j, u):
                    if (ref := at(j, u, 0)) is not None:
                        weighted(pool, nc, D, message, H4, s, ref)
                    if (ref := at(j, u, 11)) is not None:
                        pool.wait_ge(s["normal_full"], tile(ref) + 1)
                        pool.tensor_copy(plane(D["Y"], ref, 0, F), x3[ref[1]][:, :]).then_inc(s["x3_kept"], 1)
                over_all_tiles(pool, step, 11)

            @block.tensor
            def _(pe):
                def step(j, u):
                    if (ref := at(j, u, 1)) is not None:
                        pe.wait_ge(s["weighted"], tile(ref) + 1)
                        pe.wait_ge(s["joined"], tile(ref) + 1)
                        sum_to_here(pe, nc, p_sum, same, link, message[ref[1] % 2][:, :], whole, width, s, ref)
                    if (ref := at(j, u, 11)) is not None:
                        t, v = tile(ref), ref[1] % 2
                        pe.wait_ge(s["x3T_full"], t + 1)
                        wait(pe, s["root_full"], t - 1)
                        nc.tensor.matmul(p_root[v][:, 0:F], x3T[v][:, :], W["root1"][:, :], start=True, stop=True).then_inc(s["root_multiplied"], 1)
                    if (ref := at(j, u, 10)) is not None:
                        t, v = tile(ref), ref[1] % 2
                        pe.wait_ge(s["normal_full"], t + 1)
                        wait(pe, s["x3T_full"], t - 1)
                        nc.tensor.transpose(p_T[v][:, 0:F], x3[ref[1]][:, :], W["ident"][:, :]).then_inc(s["x3_transposed"], 1)
                over_all_tiles(pe, step, 11)

            @block.scalar
            def _(act):
                def step(j, u):
                    if (ref := at(j, u, 3)) is not None:
                        t, v = tile(ref), ref[1] % 2
                        act.wait_ge(s["low_full"], t + 1)
                        wait(act, s["y_full"], t - 1)
                        act.activation(grown[v][:, :], low[v][:, :], ACT.Exp).then_inc(s["grown_full"], 1)
                    if (ref := at(j, u, 0)) is not None:
                        wait(act, s["summed"], tile(ref) - 1)
                        act.copy(message[u % 2][:, F:width], plane(D["scores"], ref, 0, H4)).then_inc(s["joined"], 1)
                    if (ref := at(j, u, 1)) is not None:
                        t, v = tile(ref), ref[1] % 2
                        act.wait_ge(s["summed"], t + 1)
                        wait(act, s["mean_full"], t - 1)
                        act.copy(whole[v][:, :], p_sum[v][:, 0:width]).then_inc(s["whole_full"], 1)
                    if (ref := at(j, u, 10)) is not None:
                        t, v = tile(ref), ref[1] % 2
                        act.wait_ge(s["x3_transposed"], t + 1)
                        wait(act, s["root_multiplied"], t - 1)
                        act.copy(x3T[v][:, :], p_T[v][:, 0:F]).then_inc(s["x3T_full"], 1)
                    if (ref := at(j, u, 5)) is not None:
                        norm.deviation(act, ref)
                over_all_tiles(act, step, 10)

            @block.vector
            def _(dve):
                def step(j, u):
                    if (ref := at(j, u, 9)) is not None:
                        norm.invert(dve, ref)
                    if (ref := at(j, u, 2)) is not None:
                        t, v = tile(ref), ref[1] % 2
                        dve.wait_ge(s["whole_full"], t + 1)
                        wait(dve, s["mean_full"], t)
                        nc.vector.reciprocal(inverse[:, :], whole[v][:, F:width]).then_inc(s["inverse_full"], 1)
                    if (ref := at(j, u, 4)) is not None:
                        t, v, y = tile(ref), ref[1] % 2, plane(D["Y"], ref, 0, F)
                        dve.wait_ge(s["grown_full"], t + 1)
                        dve.wait_ge(s["high_full"], t + 1)
                        nc.vector.scalar_tensor_tensor(out=y, in0=grown[v][:, :], scalar=-1.0, in1=y, op0=ALU.add, op1=ALU.add).then_inc(s["y_full"], 1)
                    if (ref := at(j, u, 9)) is not None:
                        wait(dve, s["x3_kept"], tile(ref) - 3)
                        wait(dve, s["x3_transposed"], tile(ref) - 3)
                        norm.rows_of(dve, x3[ref[1]][:, :], plane(D["Y"], ref, 0, F), ref)
                    if (ref := at(j, u, 5)) is not None:
                        norm.keep(dve, ref)
                    if (ref := at(j, u, 3)) is not None:
                        t, v, y = tile(ref), ref[1] % 2, plane(D["Y"], ref, 0, F)
                        dve.wait_ge(s["mean_full"], t + 1)
                        nc.vector.scalar_tensor_tensor(out=y, in0=mean[v][:, :], scalar=0.0, in1=y, op0=ALU.max, op1=ALU.add).then_inc(s["high_full"], 1)
                    if (ref := at(j, u, 2)) is not None:
                        t, v = tile(ref), ref[1] % 2
                        dve.wait_ge(s["inverse_full"], t + 1)
                        wait(dve, s["high_full"], t - 1)
                        wait(dve, s["low_full"], t - 1)
                        nc.vector.tensor_tensor(by_head(mean[v][:, :]), by_head(whole[v][:, 0:F]),
                                                inverse[:, :].unsqueeze(2).to_broadcast([F, H4, F // H4]), ALU.mult).then_inc(s["mean_full"], 1)
                    if (ref := at(j, u, 4)) is not None:
                        norm.statistics(dve, plane(D["Y"], ref, 0, F), s["y_full"], ref)
                    if (ref := at(j, u, 0)) is not None:
                        mark_same(dve, nc, D, same, s["summed"], s, ref)
                    if (ref := at(j, u, 2)) is not None:
                        t, v = tile(ref), ref[1] % 2
                        dve.wait_ge(s["mean_full"], t + 1)
                        wait(dve, s["grown_full"], t - 1)
                        nc.vector.tensor_scalar(low[v][:, :], mean[v][:, :], 0.0, None, ALU.min).then_inc(s["low_full"], 1)
                    if (ref := at(j, u, 4)) is not None:
                        norm.aggregate(dve, ref)
                    if (ref := at(j, u, 12)) is not None:
                        dve.wait_ge(s["root_multiplied"], tile(ref) + 1)
                        nc.vector.tensor_tensor(plane(D["R"], ref, 0, F), p_root[ref[1] % 2][:, 0:F], W["b_root1_rows"][:, :], ALU.add).then_inc(s["root_full"], 1)
                over_all_tiles(dve, step, 12)

            @block.sync
            def _(sp):
                def step(j, u):
                    if (ref := at(j, u, 0)) is not None:
                        load_link(sp, io["link_rows"][bass.ds(tile(ref), 1), :], link, F - 1, s["summed"], s, ref)
                    if (ref := at(j, u, 15)) is not None:
                        store_pass(sp, s["link_waits_taken"], io["X3"], D["Y"], s["x3_kept"], s["stored"], ref)
                    if (ref := at(j, u, 16)) is not None and ref[1] == UNROLL - 1:
                        tiles = bass.ds(ref[0] * UNROLL, UNROLL)
                        sp.wait_ge(s["root_full"], tile(ref) + 1)
                        take_waits(sp, s["link_waits_taken"])
                        sp.dma_start(io["x_root"][:, tiles, :], D["R"][:, tiles, :]).then_inc(s["root_stored"], 16)
                over_all_tiles(sp, step, 16)
                sp.wait_ge(s["stored"], 16 * PASSES)
                sp.wait_ge(s["root_stored"], 16 * PASSES)


def relation_rows(nc, io, W, D, table, w_rel, hidden):
    RG, PAIR = 4, RELATIONS - 2
    groups = ((PAIR, RELATIONS), (0, RG), (RG, PAIR))
    PARTS = len(groups)
    BANKS = 4 if hidden else 2 * PARTS
    with Phase(nc) as m:
        two = lambda name: [m.sb(f"{name}{u}", [F, F]) for u in range(2)]
        same, whole = two("same"), two("whole")
        link = [m.sb(f"link{u}", [F, F]) for u in range(UNROLL)]
        rows = [m.sb(f"rows{u}", [F, F]) for u in range(UNROLL)]
        index = [m.sb(f"index{u}", [F, 1], i32) for u in range(UNROLL)]
        rowsT = two("rowsT")
        begun = [m.sb(f"begun{u}", [F, 2, F]) for u in range(2)]
        added = [[m.sb(f"added{u}{r}", [F, F]) for r in range(2)] for u in range(2)]
        w = m.sb("w_rel", [F, RELATIONS, F])
        p_w = [m.pb(f"p_w{n}", [F, RG, F]) for n in range(BANKS)]
        p_T, p_sum = m.pb("p_T", [F, 512]), m.pb("p_sum", [F, 512])
        gathered, written = D["moves"], D["dst_moves"]
        s = m.named(SUMS + NORM + "waits_taken w_loaded index_ready transposed rowsT_full multiplied begun_full added_full "
                    "root_loaded0 root_loaded1 root_loaded2 root_loaded3 pre_full h_full h_kept h_transposed hT_full "
                    "out_multiplied y_full y_biased stored out_index_ready")
        if hidden:
            root = [m.sb(f"root{u}", [F, F]) for u in range(UNROLL)]
            p_hT, p_out = m.pb("p_hT", [F, 512]), m.pb("p_out", [F, 512])
            h, hT, pre = [m.sb(f"h{u}", [F, F]) for u in range(UNROLL)], two("hT"), two("pre")
        else:
            out_rows = [m.sb(f"out_rows{u}", [F, F]) for u in range(UNROLL)]
            out_index = [m.sb(f"out_index{u}", [F, 1], i32) for u in range(UNROLL)]
            norm = Norm(nc, m, W, s)
        with nc.Block() as block:

            @block.sync
            def _(sp):
                sp.dma_start(w[:, :, :], w_rel.rearrange("r p f -> p r f")).then_inc(s["w_loaded"], 16)

                def step(j, u):
                    if (ref := at(j, u, 0)) is not None:
                        load_link(sp, io["link_rows"][bass.ds(tile(ref), 1), :], link, F - 1, s["summed"], s, ref)
                        if hidden:
                            wait(sp, s["pre_full"], tile(ref) - UNROLL + 1)
                            take_waits(sp, s["link_waits_taken"])
                            sp.dma_start(root[u][:, :], plane(io["x_root"], ref, 0, F)).then_inc(s[f"root_loaded{u}"], 16)
                    if hidden and (ref := at(j, u, 10)) is not None:
                        store_pass(sp, s["link_waits_taken"], io["H"], D["R"], s["h_kept"], s["stored"], ref)
                over_all_tiles(sp, step, 10 if hidden else 0)
                if hidden:
                    sp.wait_ge(s["stored"], 16 * PASSES)

            @block.gpsimd
            def _(pool):
                clear_link(pool, link, s)

                def step(j, u):
                    gather_rows(pool, s["waits_taken"], table, D["src_row"], index, s["index_ready"], rows, gathered, s["transposed"], j, u)
                    if hidden:
                        if (ref := at(j, u, 1)) is not None:
                            y_ = plane(D["Y"], ref, 0, F)
                            pool.tensor_tensor(y_, y_, W["b4c"][:, :], ALU.add).then_inc(s["y_biased"], 1)
                        if (ref := at(j, u, 8)) is not None:
                            pool.wait_ge(s["h_full"], tile(ref) + 1)
                            pool.tensor_copy(plane(D["R"], ref, 0, F), h[ref[1]][:, :]).then_inc(s["h_kept"], 1)
                    else:
                        if (ref := at(j, u, 12)) is not None:
                            t, v = tile(ref), ref[1]
                            pool.wait_ge(s["out_index_ready"], t + 1)
                            pool.wait_ge(s["normal_full"], t + 1)
                            take_waits(pool, s["waits_taken"])
                            pool.indirect_dma_start(out=io["out"], out_offset=bass.IndirectOffsetOnAxis(ap=out_index[v][:, 0:1], axis=0),
                                                    in_=out_rows[v][:, :], in_offset=None, bounds_check=N - 1,
                                                    oob_is_err=False).then_inc(written.sems[v], 16)
                        if (ref := at(j, u, 11)) is not None:
                            v = ref[1]
                            wait(pool, written.sems[v], written.after(ref[0]))
                            take_waits(pool, s["waits_taken"])
                            pool.tensor_copy(out_index[v][:, :], column(D["dst_write"], ref)).then_inc(s["out_index_ready"], 1)
                over_all_tiles(pool, step, 8 if hidden else 12)
                if not hidden:
                    for u in range(UNROLL):
                        pool.wait_ge(written.sems[u], written.after(PASSES))

            @block.tensor
            def _(pe):
                pe.wait_ge(s["w_loaded"], 16)

                def multiply(j, u, n):
                    if (ref := at(j, u, 1)) is None:
                        return
                    t, v, (a, b) = tile(ref), ref[1] % 2, groups[n]
                    if n == 0:
                        pe.wait_ge(s["rowsT_full"], t + 1)
                    if not hidden:
                        wait(pe, s["begun_full" if n == 0 else "added_full"], (2, PAIR, PAIR)[n] * (t - 1) - (0, RG, 0)[n])
                    elif n == 0:
                        wait(pe, s["added_full"], PAIR * (t - 1))
                    elif n == 1:
                        wait(pe, s["begun_full"], 2 * t)
                    else:
                        wait(pe, s["added_full"], PAIR * (t - 1) + RG)
                    nc.tensor.matmul(p_w[(PARTS * ref[1] + n) % BANKS][:, 0:b - a, :], rowsT[v][:, :], w[:, a:b, :],
                                     start=True, stop=True).then_inc(s["multiplied"], 1)

                def step(j, u):
                    multiply(j, u, 0)
                    if (ref := at(j, u, 0)) is not None:
                        pe.wait_ge(gathered.sems[u], gathered.after(j + 1))
                        wait(pe, s["rowsT_full"], tile(ref))
                        nc.tensor.transpose(p_T[:, 0:F], rows[u][:, :], W["ident"][:, :]).then_inc(s["transposed"], 1)
                    multiply(j, u, 1)
                    if (ref := at(j, u, 2)) is not None:
                        t, v = tile(ref), ref[1] % 2
                        pe.wait_ge(s["added_full"], PAIR * (t + 1))
                        pe.wait_ge(s["same_full"], t + 1)
                        pe.wait_ge(s[f"link_loaded{ref[1]}"], 16 * (ref[0] + 1))
                        wait(pe, s["whole_full"], t)
                        first = isinstance(t, int) and t == 0
                        nc.tensor.matmul(p_sum[:, 0:F], same[v][:, :], added[v][0][:, :], start=True, stop=False)
                        last = nc.tensor.matmul(p_sum[:, 0:F], same[v][:, :], added[v][1][:, :], start=False, stop=first)
                        if not first:
                            last = nc.tensor.matmul(p_sum[:, 0:F], link[ref[1]][:, :], whole[1 - v][:, :], start=False, stop=True)
                        last.then_inc(s["summed"], 1)
                    multiply(j, u, 2)
                    if hidden and (ref := at(j, u, 6)) is not None:
                        t, v = tile(ref), ref[1] % 2
                        pe.wait_ge(s["hT_full"], t + 1)
                        wait(pe, s["y_full"], t)
                        nc.tensor.matmul(p_out[:, 0:F], hT[v][:, :], W["root2c"][:, :], start=True, stop=True).then_inc(s["out_multiplied"], 1)
                    if hidden and (ref := at(j, u, 5)) is not None:
                        t, v = tile(ref), ref[1] % 2
                        pe.wait_ge(s["h_full"], t + 1)
                        wait(pe, s["hT_full"], t)
                        nc.tensor.transpose(p_hT[:, 0:F], h[ref[1]][:, :], W["ident"][:, :]).then_inc(s["h_transposed"], 1)
                over_all_tiles(pe, step, 6 if hidden else 2)

            @block.scalar
            def _(act):
                def step(j, u):
                    if hidden and (ref := at(j, u, 4)) is not None:
                        t, v = tile(ref), ref[1] % 2
                        act.wait_ge(s["pre_full"], t + 1)
                        wait(act, s["h_transposed"], t - 3)
                        wait(act, s["h_kept"], t - 3)
                        act.activation(h[ref[1]][:, :], pre[v][:, :], ACT.Relu).then_inc(s["h_full"], 1)
                    if (ref := at(j, u, 1)) is not None:
                        t, v = tile(ref), ref[1] % 2
                        act.wait_ge(s["multiplied"], PARTS * t + 1)
                        wait(act, s["added_full"], PAIR * (t - 1))
                        for r in range(2):
                            act.activation(begun[v][:, r, :], p_w[PARTS * ref[1] % BANKS][:, r, :], ACT.Copy,
                                           scale=plane(D["relation"], ref, PAIR + r, PAIR + r + 1)).then_inc(s["begun_full"], 1)
                    if not hidden and (ref := at(j, u, 4)) is not None:
                        norm.deviation(act, ref)
                    if (ref := at(j, u, 0)) is not None:
                        t, v = tile(ref), u % 2
                        act.wait_ge(s["transposed"], t + 1)
                        wait(act, s["multiplied"], PARTS * (t - 1))
                        act.copy(rowsT[v][:, :], p_T[:, 0:F]).then_inc(s["rowsT_full"], 1)
                    if (ref := at(j, u, 2)) is not None:
                        t, v = tile(ref), ref[1] % 2
                        act.wait_ge(s["summed"], t + 1)
                        wait(act, s["pre_full" if hidden else "y_full"], t - 1)
                        act.copy(whole[v][:, :], p_sum[:, 0:F]).then_inc(s["whole_full"], 1)
                    if hidden and (ref := at(j, u, 5)) is not None:
                        t, v = tile(ref), ref[1] % 2
                        act.wait_ge(s["h_transposed"], t + 1)
                        wait(act, s["out_multiplied"], t - 1)
                        act.copy(hT[v][:, :], p_hT[:, 0:F]).then_inc(s["hT_full"], 1)
                over_all_tiles(act, step, 5 if hidden else 4)

            @block.vector
            def _(dve):
                def add_relations(j, u, a, b):
                    if (ref := at(j, u, 1)) is None:
                        return
                    t, v = tile(ref), ref[1] % 2
                    for r in range(a, b):
                        n = 1 + r // RG
                        if r % RG == 0:
                            dve.wait_ge(s["multiplied"], PARTS * t + n + 1)
                        if r == 0:
                            dve.wait_ge(s["begun_full"], 2 * t + 2)
                            wait(dve, s["summed"], t - 1)
                        if r >= 2:
                            dve.wait_ge(s["added_full"], PAIR * t + r - 1)
                        before = begun[v][:, r, :] if r < 2 else added[v][r % 2][:, :]
                        nc.vector.scalar_tensor_tensor(out=added[v][r % 2][:, :], in0=p_w[(PARTS * ref[1] + n) % BANKS][:, r % RG, :],
                                                       scalar=plane(D["relation"], ref, r, r + 1), in1=before,
                                                       op0=ALU.mult, op1=ALU.add).then_inc(s["added_full"], 1)

                def step(j, u):
                    if hidden and (ref := at(j, u, 7)) is not None:
                        t = tile(ref)
                        dve.wait_ge(s["out_multiplied"], t + 1)
                        dve.wait_ge(s["y_biased"], t + 1)
                        y_ = plane(D["Y"], ref, 0, F)
                        nc.vector.tensor_tensor(y_, p_out[:, 0:F], y_, ALU.add).then_inc(s["y_full"], 1)
                    add_relations(j, u, 0, 4)
                    if not hidden and (ref := at(j, u, 8)) is not None:
                        norm.invert(dve, ref)
                        wait(dve, written.sems[ref[1]], written.after(ref[0]))
                        norm.rows_of(dve, out_rows[ref[1]][:, :], plane(D["Y"], ref, 0, F), ref)
                    if not hidden and (ref := at(j, u, 4)) is not None:
                        norm.keep(dve, ref)
                    if (ref := at(j, u, 3)) is not None:
                        t, v = tile(ref), ref[1] % 2
                        dve.wait_ge(s["whole_full"], t + 1)
                        if hidden:
                            dve.wait_ge(s[f"root_loaded{ref[1]}"], 16 * (ref[0] + 1))
                            wait(dve, s["h_full"], t - 1)
                            nc.vector.tensor_tensor(pre[v][:, :], whole[v][:, :], root[ref[1]][:, :], ALU.add).then_inc(s["pre_full"], 1)
                        else:
                            y = plane(D["Y"], ref, 0, F)
                            nc.vector.tensor_tensor(y, whole[v][:, :], y, ALU.add).then_inc(s["y_full"], 1)
                    if (ref := at(j, u, 1)) is not None:
                        mark_same(dve, nc, D, same, s["summed"], s, ref)
                    if not hidden and (ref := at(j, u, 3)) is not None:
                        norm.statistics(dve, plane(D["Y"], ref, 0, F), s["y_full"], ref)
                    add_relations(j, u, 4, 6)
                    if not hidden and (ref := at(j, u, 3)) is not None:
                        norm.aggregate(dve, ref)
                    add_relations(j, u, 6, 8)
                over_all_tiles(dve, step, 7 if hidden else 8)
        gathered.passes += PASSES
        if not hidden:
            written.passes += PASSES


def gnn_kernel(nc, io):
    with ExitStack() as stack:
        W, D = {}, {}
        with Phase(nc) as m:
            prepare_weights(nc, Memory(nc, stack), m, io, W)
        edges = Memory(nc, stack)
        D["moves"], D["dst_moves"] = PoolMoves(edges, "pool_moved"), PoolMoves(edges, "pool_moved_dst")
        for name, shape, dt in (("dst_col", [F, T], fp32), ("src_col", [F, T], i32), ("dst_read", [F, T], i32),
                                ("dst_write", [F, T], i32), ("slot_row", [F, T], i32), ("src_row", [F, T], i32),
                                ("last_key", [F, T], fp32), ("relation", [F, T, RELATIONS], fp32),
                                ("end_keys", [HEADS, T, 2], fp32)):
            D[name] = edges.sb(name, shape, dt)
        prepare_edges(nc, io, W, D)
        with Phase(nc) as m:
            dense_phase(nc, m, io, W, RowMap(nc, m, io, D))
        for name, shape in (("drow", [F, SLOTS]), ("Y", [F, T, F]), ("R", [F, T, F]), ("scores", [F, T, HEADS]),
                            ("dinv", [F, T]), ("count", [F, T, RELATIONS])):
            D[name] = edges.sb(name, shape)
        attention_messages(nc, io, W, D)
        weights_of_edges(nc, io, W, D, (F // HEADS) ** -0.5)
        attention_rows(nc, io, W, D)
        hidden_rows(nc, io, W, D)
        output_rows(nc, io, W, D)
        gat_messages(nc, io, W, D)
        weights_of_edges(nc, io, W, D, 1.0)
        gat_rows(nc, io, W, D)
        relation_rows(nc, io, W, D, io["X3"], io["L3_gnn_w_rel1"], hidden=True)
        relation_rows(nc, io, W, D, io["H"], io["L3_gnn_w_rel2"], hidden=False)


_INS = ['x', 'edge_attr_42', 'L0_gnn_Wq', 'L0_gnn_bq', 'L0_gnn_Wk', 'L0_gnn_bk', 'L0_gnn_Wv', 'L0_gnn_bv', 'L0_gnn_Ws', 'L0_gnn_bs',
        'L1_gnn_W1', 'L1_gnn_b1', 'L1_gnn_W2', 'L1_gnn_b2', 'L2_gnn_W', 'L2_gnn_a_src', 'L2_gnn_a_dst',
        'L3_gnn_w_rel1', 'L3_gnn_root1', 'L3_gnn_b1', 'L3_gnn_w_rel2', 'L3_gnn_root2', 'L3_gnn_b2']


def kernel(**inputs):
    import numpy as _np
    import concourse.bacc as _bacc
    from concourse.bass_utils import run_bass_kernel_spmd as _run

    nc = _bacc.Bacc("TRN2", target_bir_lowering=False, num_devices=1)
    arrays = {name: _np.ascontiguousarray(inputs[name]) for name in _INS}
    arrays["src"] = _np.concatenate([inputs["src"], _np.zeros(SLOTS - E, _np.int32)])
    arrays["dst"] = _np.concatenate([inputs["dst"], _np.full(SLOTS + 1 - E, PAD_KEY, _np.int32)])
    bases = [min(512 * g, LAST_BASE) for g in range(GROUPS)]
    arrays["x_columns"] = _np.concatenate([inputs["x"][b:b + 512].reshape(F, 4, F).transpose(2, 1, 0).reshape(F, 512) for b in bases])
    io = {name: nc.dram_tensor(f"in_{name}", a.shape, mybir.dt.from_np(a.dtype), kind="ExternalInput").ap() for name, a in arrays.items()}
    for n in ("Z1", "H2", "X2", "X3", "H"):
        io[n] = nc.dram_tensor(n, (N + SLOTS, F), fp32, kind="Internal").ap()
    io["row_of"] = nc.dram_tensor("row_of", (N, 1), i32, kind="Internal").ap()
    io["dst_f"] = nc.dram_tensor("dst_keys", (SLOTS,), fp32, kind="Internal").ap()
    for n in ("link_rows", "back_rows"):
        io[n] = nc.dram_tensor(n, (T, F), fp32, kind="Internal").ap()
    io["x_root"] = nc.dram_tensor("x_root", (F, T, F), fp32, kind="Internal").ap()
    for n in ("max_ends", "max_ends_out"):
        io[n] = nc.dram_tensor(n + "_rows", (T * HEADS * 2,), fp32, kind="Internal").ap()
    io["out"] = nc.dram_tensor("out", (N, F), fp32, kind="ExternalOutput").ap()
    gnn_kernel(nc, io)
    r = _run(nc, [{f"in_{name}": a for name, a in arrays.items()}], core_ids=[0])
    return r.results[0]["out"]
```
